# Optimizing a Trainium2 kernel written in Bass

```python
import numpy as np
import jax
import jax.numpy as jnp

def _softmax(x, axis=-1):
    return jax.nn.softmax(x, axis=axis)

def _gelu(x):
    return jax.nn.gelu(x, approximate=True)

def _silu(x):
    return jax.nn.silu(x)

def _sigmoid(x):
    return jax.nn.sigmoid(x)

def _layernorm(x, axis=-1, eps=1e-05):
    m = jnp.mean(x, axis=axis, keepdims=True)
    v = jnp.var(x, axis=axis, keepdims=True)
    return (x - m) / jnp.sqrt(v + eps)

def _scatter_add(tgt, idx, src, axis=0):
    return tgt.at[idx].add(src)

def _segment_sum(src, seg, n):
    return jax.ops.segment_sum(src, seg, n)
kernel_name = 'mk_gps_d1_gnn_r8_e2f42a'

def setup_inputs(seed: int=0):
    np.random.seed(seed)
    _w = jnp.asarray

    def _rec_inputs():
        import jax
        import jax.numpy as jnp
        _gk = jax.random.key(seed)
        x = -0.0003713 + 1 * jax.random.normal(jax.random.fold_in(_gk, 1), (6250, 256), jnp.float32)
        src = jax.random.randint(jax.random.fold_in(_gk, 2), (200000,), 0, 6250, jnp.int32)
        dst = jnp.minimum((6250 * jax.random.uniform(jax.random.fold_in(_gk, 3), (200000,)) ** 2.0).astype(jnp.int32), 49999)
        _o = jnp.argsort(dst, stable=True)
        src = src[_o]
        dst = dst[_o]
        return (x, src, dst)
    x, src, dst = _rec_inputs()

    def _L0_gnn_setup():
        import jax, jax.numpy as jnp
        import numpy as np
        N = 6250
        E = 200000
        D = 256
        H = 256
        EPS = 1e-05

        def _gnn_layer(x, row, col, W, b, g, beta):
            n = x.shape[0]
            neigh = x[col]
            agg = jax.ops.segment_sum(neigh, row, num_segments=n)
            deg = jax.ops.segment_sum(jnp.ones((row.shape[0],), x.dtype), row, num_segments=n)
            deg = jnp.maximum(deg, 1.0)[:, None]
            h = (x + agg / deg) @ W.T + b
            mu = jnp.mean(h, axis=-1, keepdims=True)
            var = jnp.mean(jnp.square(h - mu), axis=-1, keepdims=True)
            hn = (h - mu) * jax.lax.rsqrt(var + EPS) * g + beta
            return jax.nn.silu(hn)
        key = jax.random.key(seed)
        ks = jax.random.split(key, 12)
        x = jax.random.normal(ks[0], (N, D), dtype=jnp.float32)
        edge_index = jax.random.randint(ks[1], (2, E), 0, N, dtype=jnp.int32)
        s0 = 1.0 / np.sqrt(D)
        s1 = 1.0 / np.sqrt(H)
        W0 = jax.random.uniform(ks[2], (H, D), jnp.float32, -s0, s0)
        b0 = jax.random.uniform(ks[3], (H,), jnp.float32, -s0, s0)
        g0 = jnp.ones((H,), jnp.float32)
        beta0 = jnp.zeros((H,), jnp.float32)
        W1 = jax.random.uniform(ks[4], (H, H), jnp.float32, -s1, s1)
        b1 = jax.random.uniform(ks[5], (H,), jnp.float32, -s1, s1)
        g1 = jnp.ones((H,), jnp.float32)
        beta1 = jnp.zeros((H,), jnp.float32)
        return {'x': x, 'edge_index': edge_index, 'W0': W0, 'b0': b0, 'g0': g0, 'beta0': beta0, 'W1': W1, 'b1': b1, 'g1': g1, 'beta1': beta1}
    _L0_gnn_all = _L0_gnn_setup()
    _L0_gnn_in = {k: v for k, v in _L0_gnn_all.items() if k in ('W0', 'b0', 'g0', 'beta0', 'W1', 'b1', 'g1', 'beta1')}
    del _L0_gnn_all

    def _L0_mix_setup():
        import jax, jax.numpy as jnp
        import numpy as np
        HEADS, DIM_HEAD = (8, 64)
        EPS = 1e-05

        def instance_norm(t):
            mu = jnp.mean(t, axis=-1, keepdims=True)
            var = jnp.mean((t - mu) ** 2, axis=-1, keepdims=True)
            return (t - mu) * jax.lax.rsqrt(var + EPS)
        key = jax.random.key(seed)
        k1, k2, k3, k4 = jax.random.split(key, 4)
        B, N, D = (8, 1024, 256)
        inner = HEADS * DIM_HEAD
        x = jax.random.normal(k1, (B, N, D), jnp.float32)
        w_qkv = jax.random.normal(k2, (3 * inner, D), jnp.float32) / np.sqrt(D).astype(np.float32)
        w_out = jax.random.normal(k3, (D, inner), jnp.float32) / np.sqrt(inner).astype(np.float32)
        b_out = 0.01 * jax.random.normal(k4, (D,), jnp.float32)
        return {'x': x, 'w_qkv': w_qkv, 'w_out': w_out, 'b_out': b_out}
    _L0_mix_all = _L0_mix_setup()
    _L0_mix_in = {k: v for k, v in _L0_mix_all.items() if k in ('w_qkv', 'w_out', 'b_out')}
    del _L0_mix_all

    def _L0_ffn_setup():
        import math
        import jax, jax.numpy as jnp
        import numpy as np
        CAPACITY_FACTOR = 1.25
        TOP_K = 2
        LN_EPS = 1e-05

        def _layer_norm(x, gamma, beta):
            mu = jnp.mean(x, axis=-1, keepdims=True)
            var = jnp.var(x, axis=-1, keepdims=True)
            return (x - mu) * jax.lax.rsqrt(var + LN_EPS) * gamma + beta
        key = jax.random.key(seed)
        ks = jax.random.split(key, 4)
        B, S, D, F, E = (8, 512, 256, 512, 8)
        x = jax.random.normal(ks[0], (B, S, D), dtype=jnp.float32)
        Wr = jax.random.normal(ks[1], (D, E), dtype=jnp.float32) / np.sqrt(D)
        br = jnp.zeros((E,), jnp.float32)
        W1 = jax.random.normal(ks[2], (E, D, F), dtype=jnp.float32) / np.sqrt(D)
        b1 = jnp.zeros((E, F), jnp.float32)
        W2 = jax.random.normal(ks[3], (E, F, D), dtype=jnp.float32) / np.sqrt(F)
        b2 = jnp.zeros((E, D), jnp.float32)
        gamma = jnp.ones((D,), jnp.float32)
        beta = jnp.zeros((D,), jnp.float32)
        return {'x': x, 'Wr': Wr, 'br': br, 'W1': W1, 'b1': b1, 'W2': W2, 'b2': b2, 'gamma': gamma, 'beta': beta}
    _L0_ffn_all = _L0_ffn_setup()
    _L0_ffn_in = {k: v for k, v in _L0_ffn_all.items() if k in ('Wr', 'br', 'W1', 'b1', 'W2', 'b2', 'gamma', 'beta')}
    del _L0_ffn_all
    return {'x': x, 'src': src, 'dst': dst, 'L0_gnn_W0': _L0_gnn_in['W0'], 'L0_gnn_b0': _L0_gnn_in['b0'], 'L0_gnn_g0': _L0_gnn_in['g0'], 'L0_gnn_beta0': _L0_gnn_in['beta0'], 'L0_gnn_W1': _L0_gnn_in['W1'], 'L0_gnn_b1': _L0_gnn_in['b1'], 'L0_gnn_g1': _L0_gnn_in['g1'], 'L0_gnn_beta1': _L0_gnn_in['beta1'], 'L0_mix_w_qkv': _L0_mix_in['w_qkv'], 'L0_mix_w_out': _L0_mix_in['w_out'], 'L0_mix_b_out': _L0_mix_in['b_out'], 'L0_ffn_Wr': _L0_ffn_in['Wr'], 'L0_ffn_br': _L0_ffn_in['br'], 'L0_ffn_W1': _L0_ffn_in['W1'], 'L0_ffn_b1': _L0_ffn_in['b1'], 'L0_ffn_W2': _L0_ffn_in['W2'], 'L0_ffn_b2': _L0_ffn_in['b2'], 'L0_ffn_gamma': _L0_ffn_in['gamma'], 'L0_ffn_beta': _L0_ffn_in['beta']}

def reference(x, src, dst, L0_gnn_W0, L0_gnn_b0, L0_gnn_g0, L0_gnn_beta0, L0_gnn_W1, L0_gnn_b1, L0_gnn_g1, L0_gnn_beta1, L0_mix_w_qkv, L0_mix_w_out, L0_mix_b_out, L0_ffn_Wr, L0_ffn_br, L0_ffn_W1, L0_ffn_b1, L0_ffn_W2, L0_ffn_b2, L0_ffn_gamma, L0_ffn_beta):
    import jax
    import jax.numpy as jnp

    def _L0_gnn_ref(x, edge_index, W0, b0, g0, beta0, W1, b1, g1, beta1):
        import jax, jax.numpy as jnp
        import numpy as np
        N = 6250
        E = 200000
        D = 256
        H = 256
        EPS = 1e-05

        def _gnn_layer(x, row, col, W, b, g, beta):
            n = x.shape[0]
            neigh = x[col]
            agg = jax.ops.segment_sum(neigh, row, num_segments=n)
            deg = jax.ops.segment_sum(jnp.ones((row.shape[0],), x.dtype), row, num_segments=n)
            deg = jnp.maximum(deg, 1.0)[:, None]
            h = (x + agg / deg) @ W.T + b
            mu = jnp.mean(h, axis=-1, keepdims=True)
            var = jnp.mean(jnp.square(h - mu), axis=-1, keepdims=True)
            hn = (h - mu) * jax.lax.rsqrt(var + EPS) * g + beta
            return jax.nn.silu(hn)
        row, col = (edge_index[0], edge_index[1])
        x = _gnn_layer(x, row, col, W0, b0, g0, beta0)
        x = _gnn_layer(x, row, col, W1, b1, g1, beta1)
        return x

    def _L0_mix_ref(x, w_qkv, w_out, b_out):
        import jax, jax.numpy as jnp
        import numpy as np
        HEADS, DIM_HEAD = (8, 64)
        EPS = 1e-05

        def instance_norm(t):
            mu = jnp.mean(t, axis=-1, keepdims=True)
            var = jnp.mean((t - mu) ** 2, axis=-1, keepdims=True)
            return (t - mu) * jax.lax.rsqrt(var + EPS)
        B, N, _ = x.shape
        H, Dh = (HEADS, DIM_HEAD)
        qkv = jnp.einsum('bnd,ed->bne', x, w_qkv)
        q, k, v = jnp.split(qkv, 3, axis=-1)

        def to_heads(t):
            return t.reshape(B, N, H, Dh).transpose(0, 2, 1, 3)
        q, k, v = (to_heads(q), to_heads(k), to_heads(v))
        k = instance_norm(k)
        v = instance_norm(v)
        dots = jnp.einsum('bhnd,bhne->bhde', k, v)
        out = jnp.einsum('bhnd,bhde->bhne', q, dots) / N
        out = out.transpose(0, 2, 1, 3).reshape(B, N, H * Dh)
        return jnp.einsum('bne,de->bnd', out, w_out) + b_out

    def _L0_ffn_ref(x, Wr, br, W1, b1, W2, b2, gamma, beta):
        import math
        import jax, jax.numpy as jnp
        import numpy as np
        CAPACITY_FACTOR = 1.25
        TOP_K = 2
        LN_EPS = 1e-05

        def _layer_norm(x, gamma, beta):
            mu = jnp.mean(x, axis=-1, keepdims=True)
            var = jnp.var(x, axis=-1, keepdims=True)
            return (x - mu) * jax.lax.rsqrt(var + LN_EPS) * gamma + beta
        B, S, D = x.shape
        E = Wr.shape[1]
        N = B * S
        K = TOP_K
        logits = jnp.mean(x, axis=1) @ Wr + br
        routing_weights = jax.nn.softmax(logits, axis=-1)
        capacity = float(math.ceil(N * CAPACITY_FACTOR / E))
        expected_loads = routing_weights.sum(axis=0) * (N / B)
        scale = jnp.where(expected_loads > capacity, capacity / expected_loads, 1.0)
        routing_weights = jax.nn.softmax(routing_weights * scale, axis=-1)
        rw_tok = jnp.broadcast_to(routing_weights[:, None, :], (B, S, E)).reshape(N, E)
        top_w, top_i = jax.lax.top_k(rw_tok, K)
        top_w = jax.nn.softmax(top_w, axis=-1)
        xf = x.reshape(N, D)
        h = jax.nn.gelu(jnp.einsum('nd,edf->enf', xf, W1) + b1[:, None, :], approximate=False)
        y = jnp.einsum('enf,efd->end', h, W2) + b2[:, None, :]
        w_dense = jnp.zeros((N, E), x.dtype).at[jnp.arange(N)[:, None], top_i].add(top_w)
        out = jnp.einsum('ne,end->nd', w_dense, y).reshape(B, S, D)
        out = _layer_norm(out + x, gamma, beta)
        return out
    edge_index = jnp.stack([src, dst])
    xn = _layernorm(x, axis=-1)
    x = x + _L0_gnn_ref(xn, edge_index, L0_gnn_W0, L0_gnn_b0, L0_gnn_g0, L0_gnn_beta0, L0_gnn_W1, L0_gnn_b1, L0_gnn_g1, L0_gnn_beta1) + _L0_mix_ref(xn[None], L0_mix_w_qkv, L0_mix_w_out, L0_mix_b_out)[0]
    x = x + _L0_ffn_ref(_layernorm(x, axis=-1)[None], L0_ffn_Wr, L0_ffn_br, L0_ffn_W1, L0_ffn_b1, L0_ffn_W2, L0_ffn_b2, L0_ffn_gamma, L0_ffn_beta)[0]
    return x

_drawn_inputs = setup_inputs


def setup_inputs(seed=0):
    import zlib

    import numpy as np

    out = dict(_drawn_inputs(seed))
    spreads = {'L0_gnn_g0': (1.0, 0.2),
     'L0_gnn_beta0': (0.0, 0.1),
     'L0_gnn_g1': (1.0, 0.2),
     'L0_gnn_beta1': (0.0, 0.1),
     'L0_ffn_br': (0.0, 0.1),
     'L0_ffn_b1': (0.0, 0.393),
     'L0_ffn_b2': (0.0, 0.271),
     'L0_ffn_gamma': (1.0, 0.2),
     'L0_ffn_beta': (0.0, 0.1)}
    factors = {'L0_mix_b_out': 7.99}
    for name, (base, spread) in spreads.items():
        noise = np.random.default_rng([zlib.crc32(name.encode()), seed]).standard_normal(out[name].shape)
        drawn = base * np.exp(spread * noise) if base else spread * noise
        out[name] = jnp.asarray(drawn.astype(out[name].dtype))
    for name, factor in factors.items():
        out[name] = (out[name] * factor).astype(out[name].dtype)
    return out
```

```python
from contextlib import ExitStack

import concourse.bass as bass
from concourse import mybir

F32 = mybir.dt.float32
F16 = mybir.dt.float16
I32 = mybir.dt.int32
I16 = mybir.dt.int16
U16 = mybir.dt.uint16
ALU = mybir.AluOpType
ACT = mybir.ActivationFunctionType
AX = mybir.AxisListType

P = 128
N = 6250
E = 200000
D = 256
DC = D // P
NT = 50
LAST = N // P
BLK = LAST + 1
NB = BLK + 1
EC = 1568
PAD_NODE = BLK * P
NCH = 1616
TW = 1632
GB = 8
SB = 16
SEG = 7
SC = EC // SEG
AW = D + 1
RW = 2 * D + 2
HEADS, DH = 8, 64
PAIRS = HEADS // 2
INNER = HEADS * DH
NE, F = 8, 512
FJ = 2 * F // P
EPS = 1e-5
X_SCALE = 2048.0
CAP = float(-(-N * 5 // (4 * NE)))

assert (E + (NB - 1) * (P - 1)) // P <= NCH and NCH % (2 * GB) == 0 and EC % (2 * SB) == 0
assert E <= P * EC and (E + (NB - 1) * (P - 1)) // P + -(-(P * EC - E) // P) <= TW
assert SC % (2 * SB) == 0


class Chain:

    def __init__(self, eng, sem):
        self.eng, self.sem, self.n, self.at = eng, sem, 0, 0

    def link(self, ins):
        ins.then_inc(self.sem, 1)
        self.n += 1
        self.eng.wait_ge(self.sem, self.at + self.n)
        if not isinstance(self.at, int):
            self.eng.nop(nofuse=True)

    def loop(self, count, links, body):
        first = self.n
        with self.eng.Fori(0, count) as i:
            self.at = i * links
            body(i)
            assert self.n - first == links, self.n - first
        self.at, self.n = 0, first + count * links


def gps_layer(nc, x, src, dst, w0, b0, g0, be0, w1, b1, g1, be1, wq, wkv, wo, bo,
              wr, br, fw1, fb1, fw2, fb2, ga, be, out):
    ctx = ExitStack()
    with ctx:
        def sb(name, shape, dt=F32):
            return ctx.enter_context(nc.sbuf_tensor(name, shape, dt))

        def sem(name):
            return ctx.enter_context(nc.semaphore(name))

        sorted_edges = nc.dram_tensor("sorted_edges", [P * TW, 1], I32, kind="Internal").ap()
        table = [nc.dram_tensor(f"table{n}", [NT * P, 2 * D], F16, kind="Internal").ap() for n in range(2)]

        xs = sb("xs", [P, NT * D])
        xn = sb("xn", [P, NT * D])
        agg = sb("agg", [P, NT * AW])
        edst = sb("edst", [P, TW], I32)
        esrc = sb("esrc", [P, TW], F16)
        ring = sb("ring", [P, 2, GB, RW], F16)
        sel = sb("sel", [P, 2, GB, P], F16)
        big = sb("big", [P, 4096])
        xT = sb("xT", [P, 2, D])
        stats = sb("stats", [P, NT * 6])
        mv = sb("mv", [P, NT * 2])
        wr_s = sb("wr_s", [P, DC * NE])
        br_s = sb("br_s", [1, NE])
        rstd = sb("rstd", [P, NT])
        nmr = sb("nmr", [P, NT])
        small = sb("small", [P, 320])
        ident = sb("ident", [P, P])
        iota_p = sb("iota_p", [P, P], F16)
        ones = sb("ones", [P, P])
        blk_row = sb("blk_row", [1, TW], I16)
        valid = sb("valid", [P, 1])
        idx_ring = sb("idx_ring", [P, 2, SB], I32)
        val_ring = sb("val_ring", [P, 2, SB], I32)
        eps_c = sb("eps_c", [P, 1])
        scale_c = sb("scale_c", [P, 2])
        unscale_c = sb("unscale_c", [P, 2])

        aggi = agg[:, :].bitcast(I32)
        aggh = agg[:, :].bitcast(F16)
        e_src, e_dst = aggi[:, 0:EC], aggi[:, EC:2 * EC]
        e_pos, e_addr = agg[:, 2 * EC:3 * EC], aggi[:, 2 * EC:3 * EC]
        e_val = e_src
        e_blk = aggh[:, 6 * EC:7 * EC]
        e_mask = aggh[:, 7 * EC:8 * EC]
        e_scan = agg[:, 4 * EC:4 * EC + SC]
        m0 = 4 * EC + SC
        wkv_s = agg[:, m0:m0 + 2048]
        wq_s = agg[:, m0 + 2048:m0 + 3072]
        wo_s = agg[:, m0 + 3072:m0 + 4096]
        kv = agg[:, m0 + 4096:m0 + 5120]
        assert m0 + 5120 <= NT * AW
        ringf = ring[:, :, :, :].rearrange("p a b c -> p (a b c)").bitcast(F32)
        kv_sq = ringf[:, 0:1024]
        m_s = ringf[:, 1024:2048]
        dots_s = ringf[:, 2048:2560]
        zeros = ringf[:, 2560:3072]
        e_zero = ringf[:, 3072:3072 + SC // 2].bitcast(F16)
        tri = ringf[:, 3264:3392]
        g_s = big[:, 0:512]
        gw = [big[:, 512:1024], big[:, 1024:1536]]
        gvec = [(big[:, 1536:1792], big[:, 1792:2048]), (big[:, 2048:2304], big[:, 2304:2560])]
        fw1_s, fw2_s = big[:, 0:2048], big[:, 2048:4096]
        hT = ringf[:, 0:FJ * 512]
        brow = [big[0:1, 2560:2816], big[0:1, 2816:3072]]
        b2two = xT[0:1, :, :].rearrange("p a b -> p (a b)")
        borow, b2row = big[0:1, 3072:3328], b2two[:, 0:D]
        stage = [big[:, 3328:3584], big[:, 3584:3840]]
        sel_f = sel[:, :, :, :].rearrange("p a b c -> p (a b c)").bitcast(F32)
        gab, beb = sel_f[:, 0:D], sel_f[:, D:2 * D]

        cnt = small[:, 0:NB]
        iota_b = small[:, 50:100]
        base = small[:, 100:150]
        cend = small[:, 150:200]
        tmp = small[:, 200:250]
        tmpi = small[:, 250:300].bitcast(I32)
        lastpos = small[:, 300:301]

        mean_all, var_all = mv[:, 0:NT], mv[:, NT:2 * NT]
        aggv = agg[:, :].rearrange("p (t c) -> p t c", c=AW)
        e_cmp = ringf[0:BLK, 0:TW]
        e_tmp = ringf[:, 0:TW].bitcast(I32)
        mean_s = ringf[:, 0:D]

        bank = [ctx.enter_context(nc.psum_tensor(f"bank{n}", [P, 512], F32)) for n in range(8)]

        def tile(buf, t, n=1):
            return buf[:, bass.ds(t * D, n * D)]

        s_edges, s_w, s_wmix, s_tabinit = sem("edges_in"), sem("weights_in"), sem("mix_weights_in"), sem("table_init")
        s_x = [sem(f"x_in{n}") for n in range(5)]
        s_const = sem("constants")
        s_pre = sem("pool_steps")
        s_cnt, s_tot, s_tot2, s_blkc, s_blkp = (sem("counts_ready"), sem("totals_ready"), sem("ends_column"),
                                                sem("chunk_compare"), sem("chunk_blocks"))
        s_endc, s_blkm = sem("block_ends"), sem("chunk_blocks_product")
        s_ci, s_sc = sem("chunk_iota"), sem("table_scales")
        s_rank = sem("segment_ranked")
        s_sidx = sem("scatter_indices")
        s_scat = [sem("scatter_even"), sem("scatter_odd")]
        s_back, s_tab = sem("sorted_back"), [[sem(f"table{l}_{p}_written") for p in ("even", "odd")] for l in range(2)]
        s_dve = sem("dve_chain")
        s_act = sem("act_chain")

        block = ctx.enter_context(nc.Block())

        s_sq1, s_rs1, s_nrm = sem("ln1_var"), sem("ln1_std"), sem("ln1_done")
        s_hi = [sem("table0_high"), sem("table1_high")]
        s_lo = [sem("table0_low"), sem("table1_low")]
        s_wc = sem("kv_weights_centred")
        s_mst, s_mtp, s_mxT, s_kvp, s_kvc, s_kvq, s_kvr, s_kvs, s_kn, s_dots = (
            sem("mix_staged"), sem("mix_transposed"), sem("mix_xT"), sem("kv_product"), sem("kv_copied"), sem("kv_squares"),
            sem("kv_var"), sem("kv_std"), sem("k_scaled"), sem("dots_added"))
        s_dd, s_mp, s_mc, s_gp, s_gc = (sem("dots_diag"), sem("m_product"), sem("m_copied"),
                                        sem("g_product"), sem("g_copied"))
        s_ost = sem("mixout_staged")
        s_otp, s_oxT, s_op, s_oa = sem("mixout_transposed"), sem("mixout_xT"), sem("mixout_product"), sem("mixout_added")
        s_gidx = [sem("gather0_indices"), sem("gather1_indices")]
        s_gath = [[sem(f"gather{l}_even"), sem(f"gather{l}_odd")] for l in range(2)]
        s_sel = [[sem(f"sel{l}_even"), sem(f"sel{l}_odd")] for l in range(2)]
        s_chunk = [sem(f"chunk{l}_product") for l in range(2)]
        s_added = [sem(f"chunk{l}_added") for l in range(2)]
        s_z = [sem(f"z{l}") for l in range(2)]
        s_zt = [sem(f"z{l}_transposed") for l in range(2)]
        s_zc = [sem(f"zT{l}_copied") for l in range(2)]
        s_h = [sem(f"h{l}_product") for l in range(2)]
        s_hc = [sem(f"h{l}_copied") for l in range(2)]
        s_zero = sem("aggregate_cleared")
        s_var = [sem(f"h{l}_var") for l in range(3)]
        s_std = [sem(f"h{l}_std") for l in range(3)]
        s_nr = [sem(f"h{l}_normalised") for l in range(2)]
        s_gb = [sem(f"h{l}_affine") for l in range(2)]
        s_y = [sem(f"y{l}") for l in range(2)]
        s_xc = sem("xf_staged")
        s_xf, s_ft, s_fc, s_mean = sem("xf"), sem("xf_transposed"), sem("xfT_copied"), sem("mean_product")
        s_mb, s_lg, s_ex = sem("mean_spread"), sem("logits"), sem("router_exp")
        s_exin, s_nmr = sem("router_exp_in"), sem("mean_term")
        s_fa = sem("out_affine")
        s_pick, s_fw, s_fw2 = sem("experts_chosen"), sem("expert_weights"), sem("w2_weighted")
        s_up, s_gelu, s_down, s_fo = sem("up_product"), sem("gelu"), sem("down_product"), sem("ffn_added")
        s_fvar, s_fstd, s_fn, s_out, s_fdma = (sem("out_var"), sem("out_std"), sem("out_normalised"),
                                               sem("out_ready"), sem("out_written"))
        FN_GROUPS = 12

        @block.sync
        def _(sp):
            sp.dma_start(e_src, src).then_inc(s_edges, 16)
            sp.dma_start(e_dst, dst).then_inc(s_edges, 16)
            for n in range(5):
                w = NT // 5 * P
                sp.dma_start(xs[:, n * 2560:(n + 1) * 2560].rearrange("p (t d) -> p t d", d=D),
                             x[n * w:(n + 1) * w, :].rearrange("(t p) d -> p t d", p=P)).then_inc(s_x[n], 16)
            sp.dma_start(wkv_s.rearrange("p (c e) -> p c e", c=DC), wkv.rearrange("(c p) e -> p c e", p=P)).then_inc(s_wmix, 16)
            sp.dma_start(wq_s.rearrange("p (c e) -> p c e", c=PAIRS), wq.rearrange("(c p) e -> p c e", p=P)).then_inc(s_wmix, 16)
            sp.dma_start(wo_s.rearrange("p (c e) -> p c e", c=PAIRS), wo.rearrange("(c p) e -> p c e", p=P)).then_inc(s_wmix, 16)
            for l, (w, g, b, r) in enumerate(((w0, g0, be0, b0), (w1, g1, be1, b1))):
                sp.dma_start(gw[l].rearrange("p (c e) -> p c e", c=DC), w.rearrange("(c p) e -> p c e", p=P)).then_inc(s_w, 16)
                sp.dma_start(gvec[l][0], g.to_broadcast([P, D])).then_inc(s_w, 16)
                sp.dma_start(gvec[l][1], b.to_broadcast([P, D])).then_inc(s_w, 16)
                sp.dma_start(brow[l], r).then_inc(s_w, 16)
            sp.dma_start(borow, bo).then_inc(s_w, 16)
            sp.dma_start(wr_s[:, :].rearrange("p (c e) -> p c e", c=DC), wr.rearrange("(c p) e -> p c e", p=P)).then_inc(s_w, 16)
            sp.dma_start(br_s[:, :], br).then_inc(s_w, 16)
            def write_table(l):
                with sp.Fori(0, NT // 2) as i:
                    for b in range(2):
                        sp.wait_ge(s_lo[l], i * 2 + b + 1)
                        sp.dma_start(table[l][bass.ds((i * 2 + b) * P, P), :],
                                     sel[:, b, 0:4, :].rearrange("p k c -> p (k c)")).then_inc(s_tab[l][b], 16)
            write_table(0)
            for b in range(2):
                sp.wait_ge(s_scat[b], EC // 2 * 16)
            sp.dma_start(edst[:, :], sorted_edges.rearrange("(p c) o -> p (c o)", p=P)).then_inc(s_back, 16)
            write_table(1)
            sp.wait_ge(s_pick, 1)
            for k in range(2):
                v = sp.value_load(small[0:1, 64 + k:65 + k].bitcast(I32), min_val=0, max_val=NE - 1)
                sp.dma_start(fw1_s[:, k * 1024:(k + 1) * 1024].rearrange("p (c f) -> p c f", c=DC),
                             fw1[bass.ds(v, 1), :, :].rearrange("o (c p) f -> p (o c) f", p=P)).then_inc(s_fw, 16)
                sp.dma_start(fw2_s[:, k * 1024:(k + 1) * 1024].rearrange("p (c f) -> p c f", c=F // P),
                             fw2[bass.ds(v, 1), :, :].rearrange("o (c p) f -> p (o c) f", p=P)).then_inc(s_fw, 16)
                sp.dma_start(small[:, 80 + 4 * k:84 + 4 * k], fb1[bass.ds(v, 1), :, :].rearrange("o p c -> p (o c)")).then_inc(s_fw, 16)
                sp.dma_start(b2two[:, k * D:(k + 1) * D], fb2[bass.ds(v, 1), :]).then_inc(s_fw, 16)
            sp.dma_start(gab, ga.to_broadcast([P, D])).then_inc(s_fw, 16)
            sp.dma_start(beb, be.to_broadcast([P, D])).then_inc(s_fw, 16)
            with sp.Fori(0, NT // 2) as i:
                sp.wait_ge(s_out, i * 2 + 2)
                sp.dma_start(out[bass.ds(i * 2 * P, 2 * P), :].rearrange("(t p) d -> p t d", p=P),
                             tile(xn, i * 2, 2).rearrange("p (t d) -> p t d", d=D)).then_inc(s_fdma, 16)
            sp.wait_ge(s_fdma, 16 * (NT // 2))

        @block.gpsimd
        def _(pool):
            ch = Chain(pool, s_pre)
            pool.memset(small[:, :], 0.0).then_inc(s_const, 1)
            pool.wait_ge(s_const, 1)
            pool.iota(iota_b, [[1, NB]], base=0, channel_multiplier=0, allow_small_or_imprecise_dtypes=True).then_inc(s_const, 1)
            pool.memset(ones[:, :], 1.0).then_inc(s_const, 1)
            pool.iota(iota_p[:, :], [[1, P]], base=0, channel_multiplier=0, allow_small_or_imprecise_dtypes=True).then_inc(s_const, 1)
            ch.link(pool.memset(tri, 1.0))
            ch.link(pool.memset(ident[:, :], 0.0))
            ch.link(pool.memset(valid[:, :], 1.0))
            pool.affine_select(out=tri, in_=tri, compare_op=ALU.is_gt, fill=0.0, base=0,
                               pattern=[[1, P]], channel_multiplier=-1).then_inc(s_const, 1)
            pool.affine_select(out=ident[:, :], in_=ident[:, :], compare_op=ALU.not_equal, fill=1.0, base=0,
                               pattern=[[-1, P]], channel_multiplier=1).then_inc(s_const, 1)
            pool.affine_select(out=valid[:, :], in_=valid[:, :], compare_op=ALU.is_ge, fill=0.0, base=N - LAST * P - 1,
                               pattern=[[0, 1]], channel_multiplier=-1).then_inc(s_const, 1)
            pool.memset(eps_c[:, :], EPS).then_inc(s_const, 1)
            ch.link(pool.iota(edst[:, :], [[0, TW // 48], [1, 48]], base=0, channel_multiplier=48))
            ch.link(pool.tensor_scalar(edst[:, :], edst[:, :], 256.0, 128.0, op0=ALU.mult, op1=ALU.add))
            pool.dma_start(sorted_edges.rearrange("(p c) o -> p (c o)", p=P), edst[:, :]).then_inc(s_tabinit, 16)
            pool.iota(e_cmp, [[1, TW]], base=0, channel_multiplier=0, allow_small_or_imprecise_dtypes=True).then_inc(s_ci, 1)
            pool.wait_ge(s_tabinit, 16)

            def scatters(i, v):
                for b in range(2):
                    col = (i * 2 + b) * SB
                    if v:
                        pool.wait_ge(s_scat[b], i * (SB * 16))
                        pool.nop(nofuse=True)
                    pool.tensor_copy(idx_ring[:, b, :], e_addr[:, bass.ds(col, SB)]).then_inc(s_sidx, 1)
                    pool.tensor_copy(val_ring[:, b, :], e_val[:, bass.ds(col, SB)]).then_inc(s_sidx, 1)
                    pool.wait_ge(s_sidx, i * 4 + 2 * b + 2)
                    pool.nop(nofuse=True)
                    for k in range(SB):
                        pool.indirect_dma_start(sorted_edges, bass.IndirectOffsetOnAxis(ap=idx_ring[:, b, k:k + 1], axis=0),
                                                val_ring[:, b, k:k + 1], None).then_inc(s_scat[b], 16)
            per = SC // (2 * SB)
            for s in range(SEG):
                pool.wait_ge(s_rank, s + 1)
                if s == 0:
                    scatters(0, False)
                with pool.Fori(max(1, s * per), (s + 1) * per) as i:
                    scatters(i, True)

            for l in range(2):
                for b in range(2):
                    pool.wait_ge(s_tab[l][b], NT // 2 * 16)
                if l == 0:
                    pool.wait_ge(s_blkp, 2)
                with pool.Fori(0, NCH // (2 * GB)) as i:
                    for b in range(2):
                        pool.wait_ge(s_chunk[l], (i * 2 + b + 1) * GB)
                        pool.nop(nofuse=True)
                        pool.tensor_copy(idx_ring[:, b, 0:GB], edst[:, bass.ds((i * 2 + b) * GB, GB)]).then_inc(s_gidx[l], 1)
                        pool.wait_ge(s_gidx[l], i * 2 + b + 1)
                        pool.nop(nofuse=True)
                        for k in range(GB):
                            pool.indirect_dma_start(ring[:, b, k, 0:2 * D], None, table[l],
                                                    bass.IndirectOffsetOnAxis(ap=idx_ring[:, b, k:k + 1], axis=0)).then_inc(s_gath[l][b], 16)
                if l == 0:
                    pool.wait_ge(s_z[0], NT)
                    pool.memset(agg[:, :], 0.0).then_inc(s_zero, 1)
            def xf_stage(i, b, again):
                t = i * 2 + b
                pool.wait_ge(s_xf, t + 1)
                pool.nop(nofuse=True)
                if again:
                    pool.wait_ge(s_ft, t - 1)
                    pool.nop(nofuse=True)
                pool.tensor_copy(stage[b], tile(xn, t)).then_inc(s_xc, 1)
            for b in range(2):
                xf_stage(0, b, False)
            with pool.Fori(1, NT // 2) as i:
                for b in range(2):
                    xf_stage(i, b, True)
            with pool.Fori(0, NT) as t:
                pool.wait_ge(s_fa, t + 1)
                pool.nop(nofuse=True)
                pool.tensor_tensor(tile(xn, t), tile(xn, t), tile(xs, t), op=ALU.add).then_inc(s_out, 1)

        @block.scalar
        def _(act):
            ch = Chain(act, s_act)
            act.wait_ge(s_const, 8)
            act.wait_ge(s_sq1, 1)
            act.activation(rstd[:, :], var_all, ACT.Sqrt, bias=eps_c[:, :]).then_inc(s_rs1, 1)

            def table_high(l, i, b):
                act.activation(sel[:, b, 0:2, :].rearrange("p k c -> p (k c)"), tile(xn, i * 2 + b), ACT.Copy,
                               scale=scale_c[:, l:l + 1]).then_inc(s_hi[l], 1)

            act.wait_ge(s_sc, 1)
            for b in range(2):
                act.wait_ge(s_nrm, b + 1)
                table_high(0, 0, b)
            with act.Fori(1, NT // 2) as i:
                for b in range(2):
                    act.wait_ge(s_nrm, i * 2 + b + 1)
                    act.wait_ge(s_tab[0][b], i * 16)
                    act.nop(nofuse=True)
                    table_high(0, i, b)
            with act.Fori(0, NT) as t:
                act.wait_ge(s_nrm, t + 1)
                act.nop(nofuse=True)
                act.activation(stage[0], tile(xn, t), ACT.Copy).then_inc(s_mst, 1)
                act.wait_ge(s_mtp, t + 1)
                act.nop(nofuse=True)
                act.activation(xT[:, 0, :], bank[4][:, 0:D], ACT.Copy).then_inc(s_mxT, 1)
                act.wait_ge(s_kvp, t + 1)
                act.nop(nofuse=True)
                act.activation(kv[:, 0:512], bank[0][:, :], ACT.Copy)
                act.activation(kv[:, 512:1024], bank[1][:, :], ACT.Copy).then_inc(s_kvc, 1)
                act.wait_ge(s_kvc, t + 1)
                act.nop(nofuse=True)
                act.activation(kv_sq, kv, ACT.Square).then_inc(s_kvq, 1)
                act.wait_ge(s_kvr, t + 1)
                act.nop(nofuse=True)
                act.activation(small[:, 24:32], small[:, 16:24], ACT.Sqrt).then_inc(s_kvs, 1)
            for pr in range(PAIRS):
                act.wait_ge(s_mp, pr + 1)
                act.activation(m_s[:, pr * D:(pr + 1) * D], bank[pr % 2][:, 0:D], ACT.Copy).then_inc(s_mc, 1)
            for c in range(DC):
                act.wait_ge(s_gp, c + 1)
                act.activation(g_s[:, c * D:(c + 1) * D], bank[2 + c][:, 0:D], ACT.Copy, scale=1.0 / N).then_inc(s_gc, 1)
            with act.Fori(0, NT) as t:
                act.activation(stage[0], tile(xn, t), ACT.Copy).then_inc(s_ost, 1)
                act.wait_ge(s_otp, t + 1)
                act.nop(nofuse=True)
                act.activation(xT[:, 0, :], bank[4][:, 0:D], ACT.Copy).then_inc(s_oxT, 1)

            for l in range(2):
                with act.Fori(0, NT // 2) as i:
                    for b in range(2):
                        act.wait_ge(s_zt[l], i * 2 + b + 3)
                        act.nop(nofuse=True)
                        act.activation(xT[:, b, :], bank[4 + b][:, 0:D], ACT.Copy).then_inc(s_zc[l], 1)
                    for b in range(2):
                        act.wait_ge(s_h[l], i * 2 + b + 1)
                        act.nop(nofuse=True)
                        act.activation(tile(xn, i * 2 + b), bank[6 + b][:, 0:D], ACT.Copy).then_inc(s_hc[l], 1)
                act.wait_ge(s_var[l], 1)
                act.activation(rstd[:, :], var_all, ACT.Sqrt, bias=eps_c[:, :]).then_inc(s_std[l], 1)

                def silu(t):
                    act.wait_ge(s_gb[l], t + 1)
                    act.nop(nofuse=True)
                    act.activation(tile(xn, t), tile(xn, t), ACT.Silu).then_inc(s_y[l], 1)

                def normalise(t):
                    act.activation(tile(xn, t), tile(xn, t), ACT.Identity, bias=nmr[:, bass.ds(t, 1)],
                                   scale=rstd[:, bass.ds(t, 1)]).then_inc(s_nr[l], 1)

                act.wait_ge(s_nmr, l + 1)
                act.wait_ge(s_sc, 2)
                normalise(0)
                normalise(1)
                if l == 0:
                    def high(i, b, first=False, more=True):
                        silu(i * 2 + b)
                        act.wait_ge(s_y[0], i * 2 + b + 1)
                        act.nop(nofuse=True)
                        if not first:
                            act.wait_ge(s_tab[1][b], i * 16)
                            act.nop(nofuse=True)
                        table_high(1, i, b)
                        if more:
                            normalise(i * 2 + b + 2)
                    for b in range(2):
                        high(0, b, first=True)
                    with act.Fori(1, NT // 2 - 1) as i:
                        for b in range(2):
                            high(i, b)
                    for b in range(2):
                        high(NT // 2 - 1, b, more=False)
                else:
                    with act.Fori(0, NT - 2) as t:
                        silu(t)
                        normalise(t + 2)
                    for t in range(NT - 2, NT):
                        silu(t)
            act.wait_ge(s_var[2], 1)
            act.activation(rstd[:, :], var_all, ACT.Sqrt, bias=eps_c[:, :]).then_inc(s_std[2], 1)
            with act.Fori(0, NT // 2) as i:
                for b in range(2):
                    act.wait_ge(s_ft, i * 2 + b + 1)
                    act.nop(nofuse=True)
                    act.activation(agg[:, bass.ds((i * 2 + b) * AW, D)], bank[4 + b][:, 0:D], ACT.Copy).then_inc(s_fc, 1)
            for n in range(3):
                act.wait_ge(s_exin, n + 1)
                act.nop(nofuse=True)
                act.activation(small[:, 8:16], small[:, 0:8], ACT.Exp).then_inc(s_ex, 1)
            act.wait_ge(s_fw, 160)

            def gelus(g, w):
                for j in range(FJ):
                    act.wait_ge(s_up, g * FJ + j + 1)
                    act.nop(nofuse=True)
                    act.activation(hT[:, j * 512:j * 512 + w], bank[4 + j % 4][:, 0:w], ACT.Gelu,
                                   bias=small[:, 80 + j:81 + j]).then_inc(s_gelu, 1)
            with act.Fori(0, FN_GROUPS) as g:
                gelus(g, 512)
            gelus(FN_GROUPS, P)
            act.wait_ge(s_fvar, 1)
            act.activation(rstd[:, :], var_all, ACT.Sqrt, bias=eps_c[:, :]).then_inc(s_fstd, 1)
            act.wait_ge(s_nmr, 3)
            with act.Fori(0, NT) as t:
                act.activation(tile(xn, t), tile(xn, t), ACT.Identity, bias=nmr[:, bass.ds(t, 1)],
                               scale=rstd[:, bass.ds(t, 1)]).then_inc(s_fn, 1)

        @block.tensor
        def _(pe):
            mm = pe.matmul
            pe.wait_ge(s_const, 8)
            pe.wait_ge(s_cnt, 1)
            mm(bank[0][:, 0:NB], tri, cnt, start=True, stop=True)
            mm(bank[1][:, 0:NB], ones[:, :], cnt, start=True, stop=True)
            mm(bank[2][0:NB, 0:1], cnt, ones[:, 0:1], start=True, stop=True).then_inc(s_tot, 1)
            pe.wait_ge(s_tot2, 1)
            mm(bank[3][0:BLK, 0:1], tri[0:BLK, 0:BLK], small[0:BLK, 301:302], start=True, stop=False)
            mm(bank[3][0:BLK, 0:1], ident[0:BLK, 0:BLK], small[0:BLK, 301:302], start=False, stop=True).then_inc(s_endc, 1)
            pe.wait_ge(s_blkc, 1)
            for n in range(4):
                w = TW // 4
                m = mm(bank[n][0:1, 0:w], ones[0:BLK, 0:1], e_cmp[:, n * w:(n + 1) * w], start=True, stop=True)
            m.then_inc(s_blkm, 1)

            pe.wait_ge(s_wc, 2)
            pe.wait_ge(s_blkp, 1)
            mm(bank[7][:, :], zeros[:, 0:P], zeros, start=True, stop=False)
            with pe.Fori(0, NT) as t:
                pe.wait_ge(s_mst, t + 1)
                for c in range(DC):
                    m = pe.transpose(bank[4][:, c * P:(c + 1) * P], stage[0][:, c * P:(c + 1) * P], ident[:, :])
                m.then_inc(s_mtp, 1)
                pe.wait_ge(s_mxT, t + 1)
                for h in range(2):
                    for c in range(DC):
                        m = mm(bank[h][:, :], xT[:, 0, c * P:(c + 1) * P],
                               wkv_s[:, c * 1024 + h * 512:c * 1024 + (h + 1) * 512], start=c == 0, stop=c == DC - 1)
                m.then_inc(s_kvp, 1)
                pe.wait_ge(s_kn, t + 1)
                for pr in range(PAIRS):
                    m = mm(bank[7][:, pr * P:(pr + 1) * P], kv[:, 512 + pr * P:512 + (pr + 1) * P],
                           kv[:, pr * P:(pr + 1) * P], start=False, stop=False, skip_group_check=True)
                m.then_inc(s_dots, 1)
            mm(bank[7][:, :], zeros[:, 0:P], zeros, start=False, stop=True).then_inc(s_dots, 1)
            pe.wait_ge(s_dd, 1)
            for pr in range(PAIRS):
                if pr >= 2:
                    pe.wait_ge(s_mc, pr - 1)
                mm(bank[pr % 2][:, 0:D], dots_s[:, pr * P:(pr + 1) * P], wo_s[:, pr * D:(pr + 1) * D],
                   start=True, stop=True).then_inc(s_mp, 1)
            pe.wait_ge(s_mc, PAIRS)
            for c in range(DC):
                for pr in range(PAIRS):
                    m = mm(bank[2 + c][:, 0:D], wq_s[:, pr * D + c * P:pr * D + (c + 1) * P], m_s[:, pr * D:(pr + 1) * D],
                           start=pr == 0, stop=pr == PAIRS - 1)
                m.then_inc(s_gp, 1)
            pe.wait_ge(s_gc, DC)
            pe.wait_ge(s_w, 16 * 11)
            with pe.Fori(0, NT) as t:
                pe.wait_ge(s_ost, t + 1)
                for c in range(DC):
                    m = pe.transpose(bank[4][:, c * P:(c + 1) * P], stage[0][:, c * P:(c + 1) * P], ident[:, :])
                m.then_inc(s_otp, 1)
                pe.wait_ge(s_oxT, t + 1)
                pe.wait_ge(s_oa, t + 1)
                for c in range(DC):
                    mm(bank[0][:, 0:D], xT[:, 0, c * P:(c + 1) * P], g_s[:, c * D:(c + 1) * D], start=c == 0, stop=False)
                mm(bank[0][:, 0:D], ones[0:1, :], borow, start=False, stop=True).then_inc(s_op, 1)

            for l in range(2):
                pe.sem_inc(s_chunk[l], 2 * GB)
                if l == 0:
                    pe.wait_ge(s_oa, NT + 1)
                with pe.Fori(0, NCH // (2 * GB)) as i:
                    for b in range(2):
                        pe.wait_ge(s_gath[l][b], i * (GB * 16) + GB * 16)
                        pe.wait_ge(s_sel[l][b], i + 1)
                        for k in range(GB):
                            n = (i * 2 + b) * GB + k
                            pe.wait_ge(s_added[l], n + 1)
                            mm(bank[k % 4][:, 0:AW], sel[:, b, k, :], ring[:, b, k, D:2 * D + 1], start=True, stop=False)
                            m = mm(bank[k % 4][:, 0:D], sel[:, b, k, :], ring[:, b, k, 0:D], start=False, stop=True)
                            m.then_inc(s_chunk[l], 1)
                def transposes(i, b):
                    pe.wait_ge(s_z[l], i * 2 + b + 1)
                    for c in range(DC):
                        m = pe.transpose(bank[4 + b][:, c * P:(c + 1) * P], stage[b][:, c * P:(c + 1) * P], ident[:, :])
                    m.then_inc(s_zt[l], 1)

                def product(i, b, again):
                    pe.wait_ge(s_zc[l], i * 2 + b + 1)
                    if again:
                        pe.wait_ge(s_hc[l], i * 2 + b - 1)
                    for c in range(DC):
                        mm(bank[6 + b][:, 0:D], xT[:, b, c * P:(c + 1) * P], gw[l][:, c * D:(c + 1) * D], start=c == 0, stop=False)
                    mm(bank[6 + b][:, 0:D], ones[0:1, :], brow[l], start=False, stop=True).then_inc(s_h[l], 1)

                pe.sem_inc(s_zt[l], 2)
                for b in range(2):
                    transposes(0, b)
                for b in range(2):
                    product(0, b, False)
                with pe.Fori(1, NT // 2) as i:
                    for b in range(2):
                        transposes(i, b)
                    for b in range(2):
                        product(i, b, True)
            def xf_tile(i, b, again, mask, first, last):
                pe.wait_ge(s_xc, i * 2 + b + 1)
                if mask is not None:
                    for c in range(DC):
                        m = mm(bank[c][:, 0:1], stage[b][:, c * P:(c + 1) * P], mask,
                               start=first, stop=last, skip_group_check=True)
                    if last:
                        m.then_inc(s_mean, 1)
                if again:
                    pe.wait_ge(s_fc, i * 2 + b - 1)
                for c in range(DC):
                    m = pe.transpose(bank[4 + b][:, c * P:(c + 1) * P], stage[b][:, c * P:(c + 1) * P], ident[:, :])
                m.then_inc(s_ft, 1)
            for b in range(2):
                xf_tile(0, b, False, ones[:, 0:1], b == 0, False)
            with pe.Fori(1, LAST // 2) as i:
                for b in range(2):
                    xf_tile(i, b, True, ones[:, 0:1], False, False)
            xf_tile(LAST // 2, 0, True, valid[:, :], False, True)
            xf_tile(LAST // 2, 1, True, None, False, False)
            pe.wait_ge(s_mb, 1)
            for c in range(DC):
                mm(bank[2][:, 0:NE], mean_s[:, c * P:(c + 1) * P], wr_s[:, c * NE:(c + 1) * NE], start=c == 0, stop=False)
            mm(bank[2][:, 0:NE], ones[0:1, :], br_s[:, :], start=False, stop=True).then_inc(s_lg, 1)
            pe.wait_ge(s_fw2, 1)
            pe.wait_ge(s_fc, NT)

            def ups(g, j, nt):
                k, jj = j // 4, j % 4
                if j >= 4:
                    pe.wait_ge(s_gelu, g * FJ + j - 3)
                elif not isinstance(g, int) or g > 0:
                    pe.wait_ge(s_gelu, g * FJ + j - 3)
                for c in range(DC):
                    rhs = aggv[:, bass.ds(g * 4, nt), c * P:(c + 1) * P]
                    m = mm(bank[4 + j % 4][:, 0:nt * P], fw1_s[:, k * 1024 + c * 512 + jj * P:k * 1024 + c * 512 + (jj + 1) * P],
                           rhs, start=c == 0, stop=c == DC - 1)
                m.then_inc(s_up, 1)

            def downs(g, j, nt):
                pe.wait_ge(s_gelu, g * FJ + j + 1)
                if j == 0 and (not isinstance(g, int) or g > 0):
                    pe.wait_ge(s_fo, g * 4)
                for q in range(nt):
                    if j == 0:
                        mm(bank[q][:, 0:D], ones[0:1, :], b2row, start=True, stop=False)
                    m = mm(bank[q][:, 0:D], hT[:, j * 512 + q * P:j * 512 + (q + 1) * P], fw2_s[:, j * D:(j + 1) * D],
                           start=False, stop=j == FJ - 1)
                    if j == FJ - 1:
                        m.then_inc(s_down, 1)

            def experts(g, nt):
                ups(g, 0, nt)
                ups(g, 1, nt)
                for j in range(FJ):
                    if j + 2 < FJ:
                        ups(g, j + 2, nt)
                    downs(g, j, nt)
            experts(0, 4)
            with pe.Fori(1, FN_GROUPS) as g:
                experts(g, 4)
            experts(FN_GROUPS, 1)

        @block.vector
        def _(dve):
            ch = Chain(dve, s_dve)
            link = ch.link
            dve.wait_ge(s_const, 8)
            dve.wait_ge(s_edges, 32)
            link(dve.tensor_scalar(e_addr, e_src, 7, None, op0=ALU.arith_shift_right))
            link(dve.tensor_copy(e_blk, e_addr))
            link(dve.tensor_scalar(e_src, e_src, P - 1, None, op0=ALU.bitwise_and))
            link(dve.scalar_tensor_tensor(e_val, e_dst, 256.0, e_src, op0=ALU.mult, op1=ALU.add))
            link(dve.memset(e_zero, 0.0))

            def count(i):
                for k in range(5):
                    b = i * 5 + k
                    ins = dve.tensor_scalar(e_mask, e_blk, iota_b[:, bass.ds(b, 1)], 0.0, op0=ALU.is_equal, op1=ALU.add,
                                            accum_out=cnt[:, bass.ds(b, 1)])
                    link(ins)
            ch.loop(NB // 5, 5, count)
            dve.sem_inc(s_cnt, 1)
            dve.wait_ge(s_tot, 1)
            link(dve.tensor_scalar(tmpi, bank[1][:, 0:NB], float(P - 1), None, op0=ALU.add))
            link(dve.tensor_scalar(tmpi, tmpi, 7, None, op0=ALU.arith_shift_right))
            link(dve.tensor_copy(tmp, tmpi))
            link(dve.tensor_tensor_scan(cend, tmp, e_zero[:, 0:NB], 0.0, op0=ALU.add, op1=ALU.add))
            link(dve.tensor_sub(tmp, cend, tmp))
            link(dve.scalar_tensor_tensor(base, tmp, float(P), bank[0][:, 0:NB], op0=ALU.mult, op1=ALU.add))
            link(dve.tensor_scalar(base, base, -1.0, None, op0=ALU.add))
            link(dve.tensor_scalar(tmpi[0:NB, 0:1], bank[2][0:NB, 0:1], float(P - 1), None, op0=ALU.add))
            link(dve.tensor_scalar(tmpi[0:NB, 0:1], tmpi[0:NB, 0:1], 7, None, op0=ALU.arith_shift_right))
            dve.tensor_copy(small[0:NB, 301:302], tmpi[0:NB, 0:1]).then_inc(s_tot2, 1)

            for s in range(SEG):
                cols = slice(s * SC, (s + 1) * SC)

                def rank(i):
                    for k in range(5):
                        b = i * 5 + k
                        link(dve.tensor_scalar(e_mask[:, 0:SC], e_blk[:, cols], iota_b[:, bass.ds(b, 1)], None, op0=ALU.is_equal))
                        link(dve.tensor_tensor_scan(e_scan, e_mask[:, 0:SC], e_zero, base[:, bass.ds(b, 1)], op0=ALU.add, op1=ALU.add))
                        dve.tensor_copy(base[:, bass.ds(b, 1)], e_scan[:, SC - 1:SC])
                        link(dve.copy_predicated(e_pos[:, cols], e_mask[:, 0:SC].bitcast(U16), e_scan))
                ch.loop(NB // 5, 15, rank)
                ip = e_addr[:, cols]
                link(dve.tensor_copy(ip, e_pos[:, cols]))
                link(dve.tensor_scalar(e_scan.bitcast(I32), ip, 7, None, op0=ALU.arith_shift_right))
                link(dve.tensor_scalar(ip, ip, P - 1, None, op0=ALU.bitwise_and))
                dve.scalar_tensor_tensor(ip, ip, float(TW), e_scan.bitcast(I32), op0=ALU.mult, op1=ALU.add).then_inc(s_rank, 1)

            dve.wait_ge(s_endc, 1)
            link(dve.tensor_copy(small[0:BLK, 302:303], bank[3][0:BLK, 0:1]))
            dve.wait_ge(s_ci, 1)
            dve.tensor_scalar(e_cmp, e_cmp, small[0:BLK, 302:303], None, op0=ALU.is_ge).then_inc(s_blkc, 1)
            dve.wait_ge(s_blkm, 1)
            for n in range(4):
                w = TW // 4
                ins = dve.tensor_copy(blk_row[0:1, n * w:(n + 1) * w], bank[n][0:1, 0:w])
            ins.then_inc(s_blkp, 1)

            def stat_tile(buf, t):
                return dve.bn_stats(stats[:, bass.ds(t * 6, 6)], tile(buf, t))

            def variances(ready):
                sv = stats[:, :].rearrange("p (t c) -> p t c", c=6)
                link(dve.tensor_tensor(mean_all, sv[:, :, 1], sv[:, :, 4], op=ALU.add))
                link(dve.tensor_scalar(mean_all, mean_all, 0.5, None, op0=ALU.mult))
                link(dve.tensor_tensor(nmr[:, :], sv[:, :, 1], sv[:, :, 4], op=ALU.subtract))
                link(dve.tensor_tensor(nmr[:, :], nmr[:, :], nmr[:, :], op=ALU.mult))
                link(dve.tensor_tensor(var_all, sv[:, :, 2], sv[:, :, 5], op=ALU.add))
                link(dve.tensor_scalar(nmr[:, :], nmr[:, :], 0.25, None, op0=ALU.mult))
                dve.scalar_tensor_tensor(var_all, var_all, 1.0 / D, nmr[:, :], op0=ALU.mult, op1=ALU.add).then_inc(ready, 1)

            def finish_stats(std, value, signal=True):
                dve.wait_ge(std, value)
                link(dve.reciprocal(rstd[:, :], rstd[:, :]))
                ins = dve.scalar_tensor_tensor(nmr[:, :], mean_all, -1.0, rstd[:, :], op0=ALU.mult, op1=ALU.mult)
                if signal:
                    ins.then_inc(s_nmr, 1)
                else:
                    link(ins)

            for n in range(5):
                dve.wait_ge(s_x[n], 16)
            ch.loop(NT, 1, lambda t: link(stat_tile(xs, t)))
            variances(s_sq1)
            finish_stats(s_rs1, 1, False)
            link(dve.memset(scale_c[:, 0:1], X_SCALE))
            link(dve.memset(unscale_c[:, 0:1], 1.0 / X_SCALE))
            dve.sem_inc(s_sc, 1)

            def table_low(l, t, b):
                dve.wait_ge(s_hi[l], t + 1)
                dve.nop(nofuse=True)
                dve.scalar_tensor_tensor(sel[:, b, 2:4, :].rearrange("p k c -> p (k c)"), tile(xn, t), scale_c[:, l:l + 1],
                                         sel[:, b, 0:2, :].rearrange("p k c -> p (k c)"),
                                         op0=ALU.mult, op1=ALU.subtract).then_inc(s_lo[l], 1)

            with dve.Fori(0, NT // 2) as i:
                for b in range(2):
                    t = i * 2 + b
                    dve.tensor_scalar(tile(xn, t), tile(xs, t), rstd[:, bass.ds(t, 1)], nmr[:, bass.ds(t, 1)],
                                      op0=ALU.mult, op1=ALU.add).then_inc(s_nrm, 1)
                for b in range(2):
                    table_low(0, i * 2 + b, b)

            dve.wait_ge(s_wmix, 48)
            wg = wkv_s.rearrange("p (g e) -> p g e", e=DH)
            link(dve.tensor_reduce(small[:, 0:32], wg, axis=AX.X, op=ALU.add))
            link(dve.tensor_scalar(small[:, 0:32], small[:, 0:32], -1.0 / DH, None, op0=ALU.mult))
            dve.tensor_tensor(wg, wg, small[:, 0:32].unsqueeze(2).to_broadcast([P, 32, DH]), op=ALU.add).then_inc(s_wc, 1)
            dve.memset(zeros, 0.0).then_inc(s_wc, 1)
            link(dve.memset(dots_s, 0.0))

            def kv_tile(t):
                dve.wait_ge(s_kvq, t + 1)
                dve.nop(nofuse=True)
                link(dve.tensor_reduce(small[:, 0:16], kv_sq.rearrange("p (g e) -> p g e", e=DH), axis=AX.X, op=ALU.add))
                link(dve.tensor_scalar(small[:, 0:16], small[:, 0:16], 1.0 / DH, EPS, op0=ALU.mult, op1=ALU.add))
                dve.tensor_tensor(small[:, 16:24], small[:, 0:8], small[:, 8:16], op=ALU.mult).then_inc(s_kvr, 1)
                dve.wait_ge(s_kvs, t + 1)
                dve.nop(nofuse=True)
                link(dve.reciprocal(small[:, 32:40], small[:, 24:32]))
                kg = kv[:, 0:512].rearrange("p (g e) -> p g e", e=DH)
                dve.tensor_tensor(kg, kg, small[:, 32:40].unsqueeze(2).to_broadcast([P, 8, DH]), op=ALU.mult).then_inc(s_kn, 1)
            ch.loop(NT, 3, kv_tile)
            dve.wait_ge(s_dots, NT + 1)
            for h in range(2):
                src_d = bank[7][h * DH:(h + 1) * DH, :].rearrange("p (q d) -> p q d", d=P)[:, :, h * DH:(h + 1) * DH]
                dst_d = dots_s[h * DH:(h + 1) * DH, :].rearrange("p (q d) -> p q d", d=P)[:, :, h * DH:(h + 1) * DH]
                ins = dve.tensor_copy(dst_d, src_d)
                if h == 0:
                    link(ins)
            ins.then_inc(s_dd, 1)
            dve.sem_inc(s_oa, 1)
            with dve.Fori(0, NT) as t:
                dve.wait_ge(s_op, t + 1)
                dve.nop(nofuse=True)
                dve.tensor_tensor(tile(xs, t), tile(xs, t), bank[0][:, 0:D], op=ALU.add).then_inc(s_oa, 1)
            dve.wait_ge(s_w, 16 * 11)
            link(dve.tensor_reduce(small[:, 40:41], gvec[0][0], axis=AX.X, op=ALU.max, apply_absolute_value=True))
            link(dve.tensor_reduce(small[:, 41:42], gvec[0][1], axis=AX.X, op=ALU.max, apply_absolute_value=True))
            link(dve.scalar_tensor_tensor(small[:, 40:41], small[:, 40:41], 16.0, small[:, 41:42], op0=ALU.mult, op1=ALU.add))
            link(dve.tensor_scalar(small[:, 40:41], small[:, 40:41], 2.0 ** -60, 2.0 ** 60, op0=ALU.max, op1=ALU.min))
            bits = small[:, 42:43].bitcast(I32)
            link(dve.tensor_scalar(bits, small[:, 40:41].bitcast(I32), 0x7F800000, None, op0=ALU.bitwise_and))
            link(dve.tensor_scalar(scale_c[:, 1:2].bitcast(I32), bits, -1.0, float(268 << 23), op0=ALU.mult, op1=ALU.add))
            link(dve.tensor_scalar(unscale_c[:, 1:2].bitcast(I32), bits, -float(14 << 23), None, op0=ALU.add))
            dve.sem_inc(s_sc, 1)
            dve.wait_ge(s_back, 16)
            link(dve.tensor_scalar(e_tmp, edst[:, :], 255, None, op0=ALU.bitwise_and))
            link(dve.tensor_copy(esrc[:, :], e_tmp))
            link(dve.tensor_scalar(edst[:, :], edst[:, :], 8, None, op0=ALU.arith_shift_right))
            link(dve.memset(ring[:, :, :, 2 * D:2 * D + 1], 1.0))
            dve.memset(agg[:, :], 0.0).then_inc(s_blkp, 1)
            dve.wait_ge(s_blkp, 2)

            for l in range(2):
                def selectors(i, b):
                    dve.wait_ge(s_chunk[l], (i * 2 + b + 1) * GB)
                    dve.nop(nofuse=True)
                    dve.tensor_tensor(sel[:, b, :, :], iota_p[:, :].unsqueeze(1).to_broadcast([P, GB, P]),
                                      esrc[:, bass.ds((i * 2 + b) * GB, GB)].unsqueeze(2).to_broadcast([P, GB, P]),
                                      op=ALU.is_equal).then_inc(s_sel[l][b], 1)
                for b in range(2):
                    dve.wait_ge(s_tab[l][b], NT // 2 * 16)
                dve.sem_inc(s_added[l], 4)
                if l == 1:
                    dve.wait_ge(s_zero, 1)
                for b in range(2):
                    selectors(0, b)
                with dve.Fori(0, NCH // (2 * GB)) as i:
                    for b in range(2):
                        _, where = nc.values_load_multi_w_load_instructions(
                            blk_row[0:1, bass.ds((i * 2 + b) * GB, GB)], engines=(mybir.EngineType.DVE,), min_val=0, max_val=NT - 1)
                        for k in range(GB):
                            n = (i * 2 + b) * GB + k
                            dve.wait_ge(s_chunk[l], n + 2 * GB + 1)
                            dve.wait_ge(s_added[l], n + 4)
                            dve.nop(nofuse=True)
                            part = agg[:, bass.ds(where[k] * AW, AW)]
                            dve.tensor_tensor(part, part, bank[k % 4][:, 0:AW], op=ALU.add).then_inc(s_added[l], 1)
                        selectors(i + 1, b)
                dve.wait_ge(s_added[l], NCH + 4)
                u = small[:, 0:NT]
                link(dve.tensor_scalar(u, aggv[:, :, D], 1.0, None, op0=ALU.max))
                link(dve.reciprocal(u, u))
                link(dve.tensor_scalar(u, u, unscale_c[:, l:l + 1], None, op0=ALU.mult))
                with dve.Fori(0, NT // 2) as i:
                    for b in range(2):
                        t = i * 2 + b
                        dve.wait_ge(s_zt[l], t + 1)
                        dve.nop(nofuse=True)
                        dve.scalar_tensor_tensor(stage[b], agg[:, bass.ds(t * AW, D)], small[:, bass.ds(t, 1)], tile(xn, t),
                                                 op0=ALU.mult, op1=ALU.add).then_inc(s_z[l], 1)

                def h_stats(t):
                    dve.wait_ge(s_hc[l], t + 1)
                    dve.nop(nofuse=True)
                    link(stat_tile(xn, t))
                ch.loop(NT, 1, h_stats)
                variances(s_var[l])
                finish_stats(s_std[l], 1)

                def affine(t):
                    dve.wait_ge(s_nr[l], t + 1)
                    dve.nop(nofuse=True)
                    link(dve.tensor_tensor(tile(xn, t), tile(xn, t), gvec[l][0], op=ALU.mult))
                    dve.tensor_tensor(tile(xn, t), tile(xn, t), gvec[l][1], op=ALU.add).then_inc(s_gb[l], 1)
                if l == 0:
                    affine(0)
                    affine(1)

                    def lows(i):
                        for b in range(2):
                            table_low(1, i * 2 + b, b)
                            affine(i * 2 + b + 2)
                    ch.loop(NT // 2 - 1, 2, lows)
                    for b in range(2):
                        table_low(1, NT - 2 + b, b)
                else:
                    ch.loop(NT, 1, affine)

                    def residual(t):
                        dve.wait_ge(s_y[1], t + 1)
                        dve.nop(nofuse=True)
                        link(dve.tensor_tensor(tile(xs, t), tile(xs, t), tile(xn, t), op=ALU.add))
                        link(stat_tile(xs, t))
                    ch.loop(NT, 2, residual)
            variances(s_var[2])
            finish_stats(s_std[2], 1, False)
            with dve.Fori(0, NT) as t:
                dve.tensor_scalar(tile(xn, t), tile(xs, t), rstd[:, bass.ds(t, 1)], nmr[:, bass.ds(t, 1)],
                                  op0=ALU.mult, op1=ALU.add).then_inc(s_xf, 1)

            dve.wait_ge(s_mean, 1)
            for c in range(DC):
                ins = dve.tensor_scalar(mean_s[:, c * P:(c + 1) * P], ones[:, :], bank[c][:, 0:1], 1.0 / N, op0=ALU.mult, op1=ALU.mult)
            ins.then_inc(s_mb, 1)
            w8, e8, c8, o8, p8 = (small[:, 8 * n:8 * n + 8] for n in (0, 1, 2, 3, 4))
            one = small[:, 60:61]

            def softmax(src_ap, dst_ap, n):
                link(dve.tensor_reduce(one, src_ap, axis=AX.X, op=ALU.max))
                dve.tensor_scalar(w8, src_ap, one, None, op0=ALU.subtract).then_inc(s_exin, 1)
                dve.wait_ge(s_ex, n)
                dve.nop(nofuse=True)
                link(dve.tensor_reduce(one, e8, axis=AX.X, op=ALU.add))
                link(dve.reciprocal(one, one))
                link(dve.tensor_scalar(dst_ap, e8, one, None, op0=ALU.mult))
            dve.wait_ge(s_lg, 1)
            softmax(bank[2][:, 0:NE], c8, 1)
            link(dve.tensor_scalar(o8, c8, float(N), 1e-30, op0=ALU.mult, op1=ALU.max))
            link(dve.reciprocal(o8, o8))
            link(dve.tensor_scalar(o8, o8, CAP, 1.0, op0=ALU.mult, op1=ALU.min))
            link(dve.tensor_tensor(c8, c8, o8, op=ALU.mult))
            softmax(c8, c8, 2)
            for k in range(2):
                top = small[:, 62 + k:63 + k]
                link(dve.tensor_reduce(top, c8, axis=AX.X, op=ALU.max))
                link(dve.tensor_scalar(o8, c8, top, -100.0, op0=ALU.is_equal, op1=ALU.mult))
                link(dve.tensor_tensor(o8, o8, iota_b[:, 0:NE], op=ALU.add))
                link(dve.tensor_reduce(small[:, 66 + k:67 + k], o8, axis=AX.X, op=ALU.min))
                link(dve.tensor_scalar(small[:, 66 + k:67 + k], small[:, 66 + k:67 + k], 100.0, None, op0=ALU.add))
                link(dve.tensor_copy(small[:, 64 + k:65 + k].bitcast(I32), small[:, 66 + k:67 + k]))
                if k == 0:
                    link(dve.tensor_scalar(p8, iota_b[:, 0:NE], small[:, 66:67], 4.0, op0=ALU.is_equal, op1=ALU.mult))
                    link(dve.tensor_tensor(c8, c8, p8, op=ALU.subtract))
            dve.sem_inc(s_pick, 1)
            dve.tensor_scalar(w8, ones[:, 0:NE], small[:, 63:64], small[:, 62:63], op0=ALU.mult, op1=ALU.subtract).then_inc(s_exin, 1)
            dve.wait_ge(s_ex, 3)
            tw = [small[:, 70:71], small[:, 71:72]]
            link(dve.tensor_scalar(tw[0], e8[:, 0:1], 1.0, None, op0=ALU.add))
            link(dve.reciprocal(tw[0], tw[0]))
            link(dve.tensor_tensor(tw[1], e8[:, 0:1], tw[0], op=ALU.mult))
            dve.wait_ge(s_fw, 160)
            for k in range(2):
                link(dve.tensor_scalar(fw2_s[:, k * 1024:(k + 1) * 1024], fw2_s[:, k * 1024:(k + 1) * 1024], tw[k], None, op0=ALU.mult))
                link(dve.tensor_scalar(b2two[:, k * D:(k + 1) * D], b2two[:, k * D:(k + 1) * D], tw[k][0:1, :], None, op0=ALU.mult))
            dve.tensor_tensor(b2row, b2row, b2two[:, D:2 * D], op=ALU.add).then_inc(s_fw2, 1)

            def outputs(g, nt):
                for q in range(nt):
                    t = g * 4 + q
                    dve.wait_ge(s_down, t + 1)
                    dve.nop(nofuse=True)
                    dve.tensor_tensor(tile(xn, t), tile(xn, t), bank[q][:, 0:D], op=ALU.add).then_inc(s_fo, 1)
                    dve.wait_ge(s_fo, t + 1)
                    dve.nop(nofuse=True)
                    link(stat_tile(xn, t))
            ch.loop(FN_GROUPS, 4, lambda g: outputs(g, 4))
            outputs(FN_GROUPS, 1)
            variances(s_fvar)
            finish_stats(s_fstd, 1)

            def out_affine(t):
                dve.wait_ge(s_fn, t + 1)
                dve.nop(nofuse=True)
                link(dve.tensor_tensor(tile(xn, t), tile(xn, t), gab, op=ALU.mult))
                dve.tensor_tensor(tile(xn, t), tile(xn, t), beb, op=ALU.add).then_inc(s_fa, 1)
            ch.loop(NT, 1, out_affine)


def kernel(**inputs):
    import numpy as np
    import concourse.bacc as bacc
    from concourse.bass_utils import run_bass_kernel_spmd

    a = {k: np.ascontiguousarray(v) for k, v in inputs.items()}
    edges = {}
    for name, fill in (("src", PAD_NODE), ("dst", 0)):
        flat = np.full(P * EC, fill, a[name].dtype)
        flat[:E] = a[name]
        edges[name] = flat.reshape(P, EC)
    rows = np.zeros((NT * P, D), a["x"].dtype)
    rows[:N] = a["x"]
    wqkv = a["L0_mix_w_qkv"]

    def row(name):
        return a[name].reshape(1, -1)
    arrays = {
        "x": rows, "src": edges["src"], "dst": edges["dst"],
        "w0": np.ascontiguousarray(a["L0_gnn_W0"].T), "b0": row("L0_gnn_b0"), "g0": row("L0_gnn_g0"), "be0": row("L0_gnn_beta0"),
        "w1": np.ascontiguousarray(a["L0_gnn_W1"].T), "b1": row("L0_gnn_b1"), "g1": row("L0_gnn_g1"), "be1": row("L0_gnn_beta1"),
        "wq": np.ascontiguousarray(wqkv[:INNER]), "wkv": np.ascontiguousarray(wqkv[INNER:].T),
        "wo": np.ascontiguousarray(a["L0_mix_w_out"].T), "bo": row("L0_mix_b_out"),
        "wr": a["L0_ffn_Wr"], "br": row("L0_ffn_br"), "fw1": a["L0_ffn_W1"],
        "fb1": np.ascontiguousarray(a["L0_ffn_b1"].reshape(NE, F // P, P).transpose(0, 2, 1)),
        "fw2": a["L0_ffn_W2"], "fb2": a["L0_ffn_b2"], "ga": row("L0_ffn_gamma"), "be": row("L0_ffn_beta"),
    }
    nc = bacc.Bacc("TRN2", target_bir_lowering=False, num_devices=1)
    args = {n: nc.dram_tensor(f"in_{n}", v.shape, mybir.dt.from_np(v.dtype), kind="ExternalInput").ap() for n, v in arrays.items()}
    out = nc.dram_tensor("out", (NT * P, D), F32, kind="ExternalOutput").ap()
    gps_layer(nc, **args, out=out)
    r = run_bass_kernel_spmd(nc, [{f"in_{n}": v for n, v in arrays.items()}], core_ids=[0])
    return r.results[0]["out"][:N]
```

```python
from contextlib import ExitStack

import concourse.bass as bass
from concourse import mybir

F32 = mybir.dt.float32
F16 = mybir.dt.float16
I32 = mybir.dt.int32
I16 = mybir.dt.int16
U16 = mybir.dt.uint16
ALU = mybir.AluOpType
ACT = mybir.ActivationFunctionType
AX = mybir.AxisListType

P = 128
N = 6250
E = 200000
D = 256
DC = D // P
NT = 50
LAST = N // P
BLK = LAST + 1
NB = BLK + 1
EC = 1568
PAD_NODE = BLK * P
NCH = 1616
TW = 1632
GB = 8
SB = 16
SEGS = (64, 160, 576, 768)
SC = max(SEGS)
HB = NB // 2
NP = NT // 2
AW = D + 1
RW = 2 * D + 2
HEADS, DH = 8, 64
PAIRS = HEADS // 2
INNER = HEADS * DH
NE, F = 8, 512
FJ = 2 * F // P
EPS = 1e-5
X_SCALE = 2048.0
CAP = float(-(-N * 5 // (4 * NE)))

assert (E + (NB - 1) * (P - 1)) // P <= NCH and NCH % (2 * GB) == 0 and EC % (2 * SB) == 0
assert E <= P * EC and (E + (NB - 1) * (P - 1)) // P + -(-(P * EC - E) // P) <= TW
assert sum(SEGS) == EC and all(c % (2 * SB) == 0 for c in SEGS)


class Chain:

    def __init__(self, eng, sem):
        self.eng, self.sem, self.n, self.at = eng, sem, 0, 0

    def link(self, ins):
        ins.then_inc(self.sem, 1)
        self.n += 1
        self.eng.wait_ge(self.sem, self.at + self.n)
        if not isinstance(self.at, int):
            self.eng.nop(nofuse=True)

    def loop(self, count, links, body):
        first = self.n
        with self.eng.Fori(0, count) as i:
            self.at = i * links
            body(i)
            assert self.n - first == links, self.n - first
        self.at, self.n = 0, first + count * links


def pairs(eng, body):
    for p in range(2):
        body(p, p)
    with eng.Fori(1, (NP - 3) // 2) as i:
        for b in range(2):
            body(i * 2 + b, b)
    for p in range(NP - 3, NP):
        body(p, p % 2)


def gps_layer(nc, x, src, dst, w0, b0, g0, be0, w1, b1, g1, be1, wq, wkv, wo, bo,
              wr, br, fw1, fb1, fw2, fb2, ga, be, out):
    ctx = ExitStack()
    with ctx:
        def sb(name, shape, dt=F32):
            return ctx.enter_context(nc.sbuf_tensor(name, shape, dt))

        def sem(name):
            return ctx.enter_context(nc.semaphore(name))

        sorted_edges = nc.dram_tensor("sorted_edges", [P * TW, 1], I32, kind="Internal").ap()
        table = [nc.dram_tensor(f"table{n}", [NT * P, 2 * D], F16, kind="Internal").ap() for n in range(2)]

        xs = sb("xs", [P, NT * D])
        xn = sb("xn", [P, NT * D])
        agg = sb("agg", [P, NT * AW])
        edst = sb("edst", [P, TW], I32)
        esrc = sb("esrc", [P, TW], F16)
        ring = sb("ring", [P, 2, GB, RW], F16)
        sel = sb("sel", [P, 2, GB, P], F16)
        big = sb("big", [P, 4096])
        xT = sb("xT", [P, 2, D])
        stats = sb("stats", [P, NT * 6])
        mv = sb("mv", [P, NT * 2])
        wr_s = sb("wr_s", [P, DC * NE])
        br_s = sb("br_s", [1, NE])
        rstd = sb("rstd", [P, NT])
        nmr = sb("nmr", [P, NT])
        small = sb("small", [P, 320])
        ident = sb("ident", [P, P])
        iota_p = sb("iota_p", [P, P], F16)
        ones = sb("ones", [P, P])
        blk_row = sb("blk_row", [1, TW], I16)
        valid = sb("valid", [P, 1])
        idx_ring = sb("idx_ring", [P, 2, SB], I32)
        val_ring = sb("val_ring", [P, 2, SB], I32)
        eps_c = sb("eps_c", [P, 1])
        scale_c = sb("scale_c", [P, 2])
        unscale_c = sb("unscale_c", [P, 2])

        aggi = agg[:, :].bitcast(I32)
        aggh = agg[:, :].bitcast(F16)
        e_src, e_dst = aggi[:, 0:EC], aggi[:, EC:2 * EC]
        e_pos, e_addr = agg[:, 2 * EC:3 * EC], aggi[:, 2 * EC:3 * EC]
        e_val = e_src
        e_blk = aggh[:, 6 * EC:7 * EC]
        e_mask = aggh[:, 7 * EC:8 * EC]
        e_scan = agg[:, 4 * EC:4 * EC + SC]
        m0 = 4 * EC + SC
        wkv_s = agg[:, m0:m0 + 2048]
        wq_s = agg[:, m0 + 2048:m0 + 3072]
        wo_s = agg[:, m0 + 3072:m0 + 4096]
        kv = agg[:, m0 + 4096:m0 + 5120]
        assert m0 + 5120 <= NT * AW
        ringf = ring[:, :, :, :].rearrange("p a b c -> p (a b c)").bitcast(F32)
        kv_sq = ringf[:, 0:1024]
        m_s = ringf[:, 1024:2048]
        dots_s = ringf[:, 2048:2560]
        zeros = ringf[:, 2560:3072]
        e_zero = ringf[:, 3072:3072 + SC // 2].bitcast(F16)
        e_sign = kv.bitcast(F16)[:, 0:EC]
        tri = ringf[:, 3456:3584]
        g_s = big[:, 0:512]
        gw = [big[:, 512:1024], big[:, 1024:1536]]
        gvec = [(big[:, 1536:1792], big[:, 1792:2048]), (big[:, 2048:2304], big[:, 2304:2560])]
        fw1_s, fw2_s = big[:, 0:2048], big[:, 2048:4096]
        hT = ringf[:, 0:FJ * 512]
        brow = [big[:, 2560:2816], big[:, 2816:3072]]
        b2two = xT[0:1, :, :].rearrange("p a b -> p (a b)")
        borow, b2row = big[0:1, 3072:3328], b2two[:, 0:D]
        stage = [big[:, 3328:3840], big[:, 0:512]]
        xTp = [xT[:, :, :].rearrange("p a b -> p (a b)"), ringf[:, 0:2 * D]]
        sel_f = sel[:, :, :, :].rearrange("p a b c -> p (a b c)").bitcast(F32)
        gab, beb = sel_f[:, 0:D], sel_f[:, D:2 * D]

        cnt = small[:, 0:NB]
        iota_b = small[:, 50:100]
        base = small[:, 100:150]
        nhalf = small[:, 150:200]
        cend = small[:, 150:200]
        tmp = small[:, 200:250]
        tmpi = small[:, 250:300].bitcast(I32)
        lastpos = small[:, 300:301]

        mean_all, var_all = mv[:, 0:NT], mv[:, NT:2 * NT]
        aggv = agg[:, :].rearrange("p (t c) -> p t c", c=AW)
        e_cmp = ringf[0:BLK, 0:TW]
        e_tmp = ringf[:, 0:TW].bitcast(I32)
        mean_s = ringf[:, 0:D]

        bank = [ctx.enter_context(nc.psum_tensor(f"bank{n}", [P, 512], F32)) for n in range(8)]

        def split(b):
            return sel[:, b, :, :].rearrange("p k c -> p (k c)").rearrange("p (t h d) -> p t h d", t=2, h=2)

        def two(ap):
            return ap.rearrange("p (t d) -> p t d", t=2)

        def both(ap):
            return ap.unsqueeze(1).to_broadcast([P, 2, D])

        def tile(buf, t, n=1):
            return buf[:, bass.ds(t * D, n * D)]

        s_edges, s_w, s_wmix, s_tabinit = sem("edges_in"), sem("weights_in"), sem("mix_weights_in"), sem("table_init")
        s_x = [sem(f"x_in{n}") for n in range(5)]
        s_const = sem("constants")
        s_pre = sem("pool_steps")
        s_cnt, s_tot, s_tot2, s_blkc, s_blkp = (sem("counts_ready"), sem("totals_ready"), sem("ends_column"),
                                                sem("chunk_compare"), sem("chunk_blocks"))
        s_endc, s_blkm = sem("block_ends"), sem("chunk_blocks_product")
        s_ci, s_sc = sem("chunk_iota"), sem("table_scales")
        s_rank = sem("segment_ranked")
        s_cin, s_sgn = sem("count_inputs"), sem("sign_sums")
        s_sidx = sem("scatter_indices")
        s_scat = [sem("scatter_even"), sem("scatter_odd")]
        s_back, s_tab = sem("sorted_back"), [[sem(f"table{l}_{p}_written") for p in ("even", "odd")] for l in range(2)]
        s_dve = sem("dve_chain")
        s_act = sem("act_chain")

        block = ctx.enter_context(nc.Block())

        s_sq1, s_rs1, s_nrm = sem("ln1_var"), sem("ln1_std"), sem("ln1_done")
        s_hi = [sem("table0_high"), sem("table1_high")]
        s_lo = [sem("table0_low"), sem("table1_low")]
        s_wc = sem("kv_weights_centred")
        s_mst, s_mtp, s_mxT, s_kvp, s_kvc, s_kvq, s_kvr, s_kvs, s_kn, s_dots = (
            sem("mix_staged"), sem("mix_transposed"), sem("mix_xT"), sem("kv_product"), sem("kv_copied"), sem("kv_squares"),
            sem("kv_var"), sem("kv_std"), sem("k_scaled"), sem("dots_added"))
        s_dd, s_mp, s_mc, s_gp, s_gc = (sem("dots_diag"), sem("m_product"), sem("m_copied"),
                                        sem("g_product"), sem("g_copied"))
        s_ost = sem("mixout_staged")
        s_otp, s_oxT, s_op, s_oa = sem("mixout_transposed"), sem("mixout_xT"), sem("mixout_product"), sem("mixout_added")
        s_gidx = [sem("gather0_indices"), sem("gather1_indices")]
        s_gath = [[sem(f"gather{l}_even"), sem(f"gather{l}_odd")] for l in range(2)]
        s_sel = [[sem(f"sel{l}_even"), sem(f"sel{l}_odd")] for l in range(2)]
        s_chunk = [sem(f"chunk{l}_product") for l in range(2)]
        s_added = [sem(f"chunk{l}_added") for l in range(2)]
        s_z = [sem(f"z{l}") for l in range(2)]
        s_zt = [sem(f"z{l}_transposed") for l in range(2)]
        s_zc = [sem(f"zT{l}_copied") for l in range(2)]
        s_st = [sem(f"stats{l}_done") for l in range(3)]
        s_res = sem("residual_added")
        s_h = [sem(f"h{l}_product") for l in range(2)]
        s_hc = [sem(f"h{l}_copied") for l in range(2)]
        s_zero = sem("aggregate_cleared")
        s_var = [sem(f"h{l}_var") for l in range(3)]
        s_std = [sem(f"h{l}_std") for l in range(3)]
        s_nr = [sem(f"h{l}_normalised") for l in range(2)]
        s_gb = [sem(f"h{l}_affine") for l in range(2)]
        s_y = [sem(f"y{l}") for l in range(2)]
        s_xc = sem("xf_staged")
        s_xf, s_ft, s_fc, s_mean = sem("xf"), sem("xf_transposed"), sem("xfT_copied"), sem("mean_product")
        s_mb, s_lg, s_ex = sem("mean_spread"), sem("logits"), sem("router_exp")
        s_exin, s_nmr = sem("router_exp_in"), sem("mean_term")
        s_fa = sem("out_affine")
        s_pick, s_fw, s_fw2 = sem("experts_chosen"), sem("expert_weights"), sem("w2_weighted")
        s_up, s_gelu, s_down, s_fo = sem("up_product"), sem("gelu"), sem("down_product"), sem("ffn_added")
        s_fvar, s_fstd, s_fn, s_out, s_fdma = (sem("out_var"), sem("out_std"), sem("out_normalised"),
                                               sem("out_ready"), sem("out_written"))
        FN_GROUPS = 12

        @block.sync
        def _(sp):
            sp.dma_start(e_src, src).then_inc(s_edges, 16)
            sp.dma_start(e_dst, dst).then_inc(s_edges, 16)
            for n in range(5):
                w = NT // 5 * P
                sp.dma_start(xs[:, n * 2560:(n + 1) * 2560].rearrange("p (t d) -> p t d", d=D),
                             x[n * w:(n + 1) * w, :].rearrange("(t p) d -> p t d", p=P)).then_inc(s_x[n], 16)
            sp.dma_start(wkv_s.rearrange("p (c e) -> p c e", c=DC), wkv.rearrange("(c p) e -> p c e", p=P)).then_inc(s_wmix, 16)
            sp.dma_start(wq_s.rearrange("p (c e) -> p c e", c=PAIRS), wq.rearrange("(c p) e -> p c e", p=P)).then_inc(s_wmix, 16)
            sp.dma_start(wo_s.rearrange("p (c e) -> p c e", c=PAIRS), wo.rearrange("(c p) e -> p c e", p=P)).then_inc(s_wmix, 16)
            for l, (w, g, b, r) in enumerate(((w0, g0, be0, b0), (w1, g1, be1, b1))):
                sp.dma_start(gw[l].rearrange("p (c e) -> p c e", c=DC), w.rearrange("(c p) e -> p c e", p=P)).then_inc(s_w, 16)
                sp.dma_start(gvec[l][0], g.to_broadcast([P, D])).then_inc(s_w, 16)
                sp.dma_start(gvec[l][1], b.to_broadcast([P, D])).then_inc(s_w, 16)
                sp.dma_start(brow[l], r.to_broadcast([P, D])).then_inc(s_w, 16)
            sp.dma_start(borow, bo).then_inc(s_w, 16)
            sp.dma_start(wr_s[:, :].rearrange("p (c e) -> p c e", c=DC), wr.rearrange("(c p) e -> p c e", p=P)).then_inc(s_w, 16)
            sp.dma_start(br_s[:, :], br).then_inc(s_w, 16)
            def write_pair(l, p, b):
                sp.wait_ge(s_lo[l], p + 1)
                sp.dma_start(table[l][bass.ds(p * 2 * P, 2 * P), :].rearrange("(t p) c -> p t c", p=P),
                             sel[:, b, :, :].rearrange("p k c -> p (k c)").rearrange("p (t c) -> p t c", t=2)).then_inc(s_tab[l][b], 16)

            def write_table(l):
                with sp.Fori(0, NP // 2) as i:
                    for b in range(2):
                        write_pair(l, i * 2 + b, b)
                write_pair(l, NP - 1, 0)
            write_table(0)
            for b in range(2):
                sp.wait_ge(s_scat[b], EC // 2 * 16)
            sp.dma_start(edst[:, :], sorted_edges.rearrange("(p c) o -> p (c o)", p=P)).then_inc(s_back, 16)
            write_table(1)
            sp.wait_ge(s_pick, 1)
            for k in range(2):
                v = sp.value_load(small[0:1, 64 + k:65 + k].bitcast(I32), min_val=0, max_val=NE - 1)
                sp.dma_start(fw1_s[:, k * 1024:(k + 1) * 1024].rearrange("p (c f) -> p c f", c=DC),
                             fw1[bass.ds(v, 1), :, :].rearrange("o (c p) f -> p (o c) f", p=P)).then_inc(s_fw, 16)
                sp.dma_start(fw2_s[:, k * 1024:(k + 1) * 1024].rearrange("p (c f) -> p c f", c=F // P),
                             fw2[bass.ds(v, 1), :, :].rearrange("o (c p) f -> p (o c) f", p=P)).then_inc(s_fw, 16)
                sp.dma_start(small[:, 80 + 4 * k:84 + 4 * k], fb1[bass.ds(v, 1), :, :].rearrange("o p c -> p (o c)")).then_inc(s_fw, 16)
                sp.dma_start(b2two[:, k * D:(k + 1) * D], fb2[bass.ds(v, 1), :]).then_inc(s_fw, 16)
            sp.dma_start(gab, ga.to_broadcast([P, D])).then_inc(s_fw, 16)
            sp.dma_start(beb, be.to_broadcast([P, D])).then_inc(s_fw, 16)
            with sp.Fori(0, NT // 2) as i:
                sp.wait_ge(s_out, i + 1)
                sp.dma_start(out[bass.ds(i * 2 * P, 2 * P), :].rearrange("(t p) d -> p t d", p=P),
                             tile(xn, i * 2, 2).rearrange("p (t d) -> p t d", d=D)).then_inc(s_fdma, 16)
            sp.wait_ge(s_fdma, 16 * (NT // 2))

        @block.gpsimd
        def _(pool):
            ch = Chain(pool, s_pre)
            pool.memset(small[:, :], 0.0).then_inc(s_const, 1)
            pool.wait_ge(s_const, 1)
            pool.iota(iota_b, [[1, NB]], base=0, channel_multiplier=0, allow_small_or_imprecise_dtypes=True).then_inc(s_const, 1)
            pool.memset(ones[:, :], 1.0).then_inc(s_const, 1)
            pool.iota(iota_p[:, :], [[1, P]], base=0, channel_multiplier=0, allow_small_or_imprecise_dtypes=True).then_inc(s_const, 1)
            ch.link(pool.memset(tri, 1.0))
            ch.link(pool.memset(ident[:, :], 0.0))
            ch.link(pool.memset(valid[:, :], 1.0))
            pool.affine_select(out=tri, in_=tri, compare_op=ALU.is_gt, fill=0.0, base=0,
                               pattern=[[1, P]], channel_multiplier=-1).then_inc(s_const, 1)
            pool.affine_select(out=ident[:, :], in_=ident[:, :], compare_op=ALU.not_equal, fill=1.0, base=0,
                               pattern=[[-1, P]], channel_multiplier=1).then_inc(s_const, 1)
            pool.affine_select(out=valid[:, :], in_=valid[:, :], compare_op=ALU.is_ge, fill=0.0, base=N - LAST * P - 1,
                               pattern=[[0, 1]], channel_multiplier=-1).then_inc(s_const, 1)
            pool.memset(eps_c[:, :], EPS).then_inc(s_const, 1)
            ch.link(pool.iota(edst[:, :], [[0, TW // 48], [1, 48]], base=0, channel_multiplier=48))
            ch.link(pool.tensor_scalar(edst[:, :], edst[:, :], 256.0, 128.0, op0=ALU.mult, op1=ALU.add))
            pool.dma_start(sorted_edges.rearrange("(p c) o -> p (c o)", p=P), edst[:, :]).then_inc(s_tabinit, 16)
            pool.iota(e_cmp, [[1, TW]], base=0, channel_multiplier=0, allow_small_or_imprecise_dtypes=True).then_inc(s_ci, 1)
            pool.wait_ge(s_tabinit, 16)

            def scatters(i, v):
                for b in range(2):
                    col = (i * 2 + b) * SB
                    if v:
                        pool.wait_ge(s_scat[b], i * (SB * 16))
                        pool.nop(nofuse=True)
                    pool.tensor_copy(idx_ring[:, b, :], e_addr[:, bass.ds(col, SB)]).then_inc(s_sidx, 1)
                    pool.tensor_copy(val_ring[:, b, :], e_val[:, bass.ds(col, SB)]).then_inc(s_sidx, 1)
                    pool.wait_ge(s_sidx, i * 4 + 2 * b + 2)
                    pool.nop(nofuse=True)
                    for k in range(SB):
                        pool.indirect_dma_start(sorted_edges, bass.IndirectOffsetOnAxis(ap=idx_ring[:, b, k:k + 1], axis=0),
                                                val_ring[:, b, k:k + 1], None).then_inc(s_scat[b], 16)
            done = 0
            for n, cols in enumerate(SEGS):
                pool.wait_ge(s_rank, n + 1)
                if n == 0:
                    scatters(0, False)
                more = done + cols // (2 * SB)
                if more > max(1, done):
                    with pool.Fori(max(1, done), more) as i:
                        scatters(i, True)
                done = more

            for l in range(2):
                for b in range(2):
                    pool.wait_ge(s_tab[l][b], (NP + 1 - b) // 2 * 16)
                with pool.Fori(0, NCH // (2 * GB)) as i:
                    for b in range(2):
                        pool.wait_ge(s_gidx[l], i * 2 + b + 1)
                        pool.nop(nofuse=True)
                        for k in range(GB):
                            pool.indirect_dma_start(ring[:, b, k, 0:2 * D], None, table[l],
                                                    bass.IndirectOffsetOnAxis(ap=idx_ring[:, b, k:k + 1], axis=0)).then_inc(s_gath[l][b], 16)
                if l == 0:
                    pool.wait_ge(s_z[0], NP)
                    pool.memset(agg[:, :], 0.0).then_inc(s_zero, 1)
                with pool.Fori(0, NP) as p:
                    pool.wait_ge(s_nr[l], p + 1)
                    pool.nop(nofuse=True)
                    pool.tensor_tensor(two(tile(xn, p * 2, 2)), two(tile(xn, p * 2, 2)), both(gvec[l][1]),
                                       op=ALU.add).then_inc(s_gb[l], 1)
            def xf_stage(p, b):
                pool.wait_ge(s_xf, p + 1)
                if not isinstance(p, int) or p >= 2:
                    pool.wait_ge(s_ft, p - 1)
                pool.nop(nofuse=True)
                pool.tensor_copy(stage[b], tile(xn, p * 2, 2)).then_inc(s_xc, 1)
            pairs(pool, xf_stage)
            with pool.Fori(0, NP) as p:
                pool.wait_ge(s_fa, p + 1)
                pool.nop(nofuse=True)
                pool.tensor_tensor(tile(xn, p * 2, 2), tile(xn, p * 2, 2), tile(xs, p * 2, 2), op=ALU.add).then_inc(s_out, 1)

        @block.scalar
        def _(act):
            ch = Chain(act, s_act)
            act.wait_ge(s_const, 8)
            act.wait_ge(s_cin, 1)
            with act.Fori(0, (NB - HB) // 5) as i:
                for k in range(5):
                    b = i * 5 + k + HB
                    act.activation(e_sign, e_blk, ACT.Sign, bias=nhalf[:, bass.ds(b, 1)],
                                   accum_out=small[:, bass.ds(b + 200, 1)]).then_inc(s_act, 1)
                    act.wait_ge(s_act, i * 5 + k + 1)
                    act.nop(nofuse=True)
            act.sem_inc(s_sgn, 1)
            act.wait_ge(s_sq1, 1)
            act.activation(rstd[:, :], var_all, ACT.Sqrt, bias=eps_c[:, :]).then_inc(s_rs1, 1)

            def table_high(l, p, b):
                if not isinstance(p, int) or p >= 2:
                    act.wait_ge(s_tab[l][b], (p - b) * 8)
                    act.nop(nofuse=True)
                act.activation(split(b)[:, :, 0, :], two(tile(xn, p * 2, 2)), ACT.Copy,
                               scale=scale_c[:, l:l + 1]).then_inc(s_hi[l], 1)

            def first_high(p, b):
                act.wait_ge(s_nrm, p + 1)
                act.nop(nofuse=True)
                table_high(0, p, b)
            act.wait_ge(s_sc, 1)
            pairs(act, first_high)
            with act.Fori(0, NT) as t:
                act.activation(stage[0][:, 0:D], tile(xn, t), ACT.Copy).then_inc(s_mst, 1)
                act.wait_ge(s_mtp, t + 1)
                act.nop(nofuse=True)
                act.activation(xT[:, 0, :], bank[4][:, 0:D], ACT.Copy).then_inc(s_mxT, 1)
                act.wait_ge(s_kvp, t + 1)
                act.nop(nofuse=True)
                act.activation(kv[:, 0:512], bank[0][:, :], ACT.Copy)
                act.activation(kv[:, 512:1024], bank[1][:, :], ACT.Copy).then_inc(s_kvc, 1)
                act.wait_ge(s_kvc, t + 1)
                act.nop(nofuse=True)
                act.activation(kv_sq, kv, ACT.Square).then_inc(s_kvq, 1)
                act.wait_ge(s_kvr, t + 1)
                act.nop(nofuse=True)
                act.activation(small[:, 24:32], small[:, 16:24], ACT.Sqrt).then_inc(s_kvs, 1)
            for pr in range(PAIRS):
                act.wait_ge(s_mp, pr + 1)
                act.activation(m_s[:, pr * D:(pr + 1) * D], bank[pr % 2][:, 0:D], ACT.Copy).then_inc(s_mc, 1)
            for c in range(DC):
                act.wait_ge(s_gp, c + 1)
                act.activation(g_s[:, c * D:(c + 1) * D], bank[2 + c][:, 0:D], ACT.Copy, scale=1.0 / N).then_inc(s_gc, 1)
            def mixout(p, b):
                act.activation(stage[0], tile(xn, p * 2, 2), ACT.Copy).then_inc(s_ost, 1)
                act.wait_ge(s_otp, p + 1)
                act.nop(nofuse=True)
                act.activation(xTp[b], bank[4 + b][:, :], ACT.Copy).then_inc(s_oxT, 1)
            pairs(act, mixout)

            for l in range(2):
                with act.Fori(0, NCH // (2 * GB)) as i:
                    for b in range(2):
                        act.wait_ge(s_chunk[l], (i * 2 + b + 1) * GB)
                        act.nop(nofuse=True)
                        act.activation(idx_ring[:, b, 0:GB], edst[:, bass.ds((i * 2 + b) * GB, GB)], ACT.Copy).then_inc(s_gidx[l], 1)

                def zT(p, b):
                    act.wait_ge(s_zt[l], p + 1)
                    if not isinstance(p, int) or p >= 2:
                        act.wait_ge(s_h[l], p - 1)
                    act.nop(nofuse=True)
                    act.activation(xTp[b], bank[4 + b][:, :], ACT.Copy).then_inc(s_zc[l], 1)
                pairs(act, zT)
                act.wait_ge(s_var[l], 1)
                act.activation(rstd[:, :], var_all, ACT.Sqrt, bias=eps_c[:, :]).then_inc(s_std[l], 1)

                def silu(p, b):
                    act.wait_ge(s_gb[l], p + 1)
                    act.nop(nofuse=True)
                    act.activation(tile(xn, p * 2, 2), tile(xn, p * 2, 2), ACT.Silu).then_inc(s_y[l], 1)
                    if l == 0:
                        act.wait_ge(s_y[0], p + 1)
                        act.nop(nofuse=True)
                        table_high(1, p, b)
                act.wait_ge(s_sc, 2)
                pairs(act, silu)
            act.wait_ge(s_var[2], 1)
            act.activation(rstd[:, :], var_all, ACT.Sqrt, bias=eps_c[:, :]).then_inc(s_std[2], 1)

            def xfT(p, b):
                act.wait_ge(s_ft, p + 1)
                act.nop(nofuse=True)
                act.activation(aggv[:, bass.ds(p * 2, 2), 0:D], two(bank[4 + b][:, :]), ACT.Copy).then_inc(s_fc, 1)
            pairs(act, xfT)
            for n in range(3):
                act.wait_ge(s_exin, n + 1)
                act.nop(nofuse=True)
                act.activation(small[:, 8:16], small[:, 0:8], ACT.Exp).then_inc(s_ex, 1)
            act.wait_ge(s_fw, 160)

            def gelus(g, w):
                for j in range(FJ):
                    act.wait_ge(s_up, g * FJ + j + 1)
                    act.nop(nofuse=True)
                    act.activation(hT[:, j * 512:j * 512 + w], bank[4 + j % 4][:, 0:w], ACT.Gelu,
                                   bias=small[:, 80 + j:81 + j]).then_inc(s_gelu, 1)
            with act.Fori(0, FN_GROUPS) as g:
                gelus(g, 512)
            gelus(FN_GROUPS, P)
            act.wait_ge(s_fvar, 1)
            act.activation(rstd[:, :], var_all, ACT.Sqrt, bias=eps_c[:, :]).then_inc(s_fstd, 1)
            act.wait_ge(s_nmr, 1)
            with act.Fori(0, NT) as t:
                act.activation(tile(xn, t), tile(xn, t), ACT.Identity, bias=nmr[:, bass.ds(t, 1)],
                               scale=rstd[:, bass.ds(t, 1)]).then_inc(s_fn, 1)

        @block.tensor
        def _(pe):
            mm = pe.matmul
            pe.wait_ge(s_const, 8)
            pe.wait_ge(s_cnt, 1)
            mm(bank[0][:, 0:NB], tri, cnt, start=True, stop=True)
            mm(bank[1][:, 0:NB], ones[:, :], cnt, start=True, stop=True)
            mm(bank[2][0:NB, 0:1], cnt, ones[:, 0:1], start=True, stop=True).then_inc(s_tot, 1)
            pe.wait_ge(s_tot2, 1)
            mm(bank[3][0:BLK, 0:1], tri[0:BLK, 0:BLK], small[0:BLK, 301:302], start=True, stop=False)
            mm(bank[3][0:BLK, 0:1], ident[0:BLK, 0:BLK], small[0:BLK, 301:302], start=False, stop=True).then_inc(s_endc, 1)
            pe.wait_ge(s_blkc, 1)
            for n in range(4):
                w = TW // 4
                m = mm(bank[n][0:1, 0:w], ones[0:BLK, 0:1], e_cmp[:, n * w:(n + 1) * w], start=True, stop=True)
            m.then_inc(s_blkm, 1)

            pe.wait_ge(s_wc, 2)
            pe.wait_ge(s_blkp, 1)
            mm(bank[7][:, :], zeros[:, 0:P], zeros, start=True, stop=False)
            with pe.Fori(0, NT) as t:
                pe.wait_ge(s_mst, t + 1)
                for c in range(DC):
                    m = pe.transpose(bank[4][:, c * P:(c + 1) * P], stage[0][:, c * P:(c + 1) * P], ident[:, :])
                m.then_inc(s_mtp, 1)
                pe.wait_ge(s_mxT, t + 1)
                for h in range(2):
                    for c in range(DC):
                        m = mm(bank[h][:, :], xT[:, 0, c * P:(c + 1) * P],
                               wkv_s[:, c * 1024 + h * 512:c * 1024 + (h + 1) * 512], start=c == 0, stop=c == DC - 1)
                m.then_inc(s_kvp, 1)
                pe.wait_ge(s_kn, t + 1)
                for pr in range(PAIRS):
                    m = mm(bank[7][:, pr * P:(pr + 1) * P], kv[:, 512 + pr * P:512 + (pr + 1) * P],
                           kv[:, pr * P:(pr + 1) * P], start=False, stop=False, skip_group_check=True)
                m.then_inc(s_dots, 1)
            mm(bank[7][:, :], zeros[:, 0:P], zeros, start=False, stop=True).then_inc(s_dots, 1)
            pe.wait_ge(s_dd, 1)
            for pr in range(PAIRS):
                if pr >= 2:
                    pe.wait_ge(s_mc, pr - 1)
                mm(bank[pr % 2][:, 0:D], dots_s[:, pr * P:(pr + 1) * P], wo_s[:, pr * D:(pr + 1) * D],
                   start=True, stop=True).then_inc(s_mp, 1)
            pe.wait_ge(s_mc, PAIRS)
            for c in range(DC):
                for pr in range(PAIRS):
                    m = mm(bank[2 + c][:, 0:D], wq_s[:, pr * D + c * P:pr * D + (c + 1) * P], m_s[:, pr * D:(pr + 1) * D],
                           start=pr == 0, stop=pr == PAIRS - 1)
                m.then_inc(s_gp, 1)
            pe.wait_ge(s_gc, DC)
            pe.wait_ge(s_w, 16 * 11)
            def transposes(stage_b, out_bank):
                for q in range(2 * DC):
                    m = pe.transpose(out_bank[:, q * P:(q + 1) * P], stage_b[:, q * P:(q + 1) * P], ident[:, :])
                return m

            def mixout(p, b):
                pe.wait_ge(s_ost, p + 1)
                transposes(stage[0], bank[4 + b]).then_inc(s_otp, 1)
                pe.wait_ge(s_oxT, p + 1)
                if not isinstance(p, int) or p >= 2:
                    pe.wait_ge(s_oa, p - 1)
                for q in range(2):
                    for c in range(DC):
                        mm(bank[b][:, q * D:(q + 1) * D], xTp[b][:, (q * DC + c) * P:(q * DC + c + 1) * P],
                           g_s[:, c * D:(c + 1) * D], start=c == 0, stop=False)
                    m = mm(bank[b][:, q * D:(q + 1) * D], ones[0:1, :], borow, start=False, stop=True)
                m.then_inc(s_op, 1)
            pairs(pe, mixout)

            for l in range(2):
                if l == 0:
                    pe.wait_ge(s_blkp, 2)
                pe.sem_inc(s_chunk[l], 2 * GB)
                if l == 0:
                    pe.wait_ge(s_oa, NP)
                with pe.Fori(0, NCH // (2 * GB)) as i:
                    for b in range(2):
                        pe.wait_ge(s_gath[l][b], i * (GB * 16) + GB * 16)
                        pe.wait_ge(s_sel[l][b], i + 1)
                        for k in range(GB):
                            n = (i * 2 + b) * GB + k
                            pe.wait_ge(s_added[l], n + 1)
                            mm(bank[k % 4][:, 0:AW], sel[:, b, k, :], ring[:, b, k, D:2 * D + 1], start=True, stop=False)
                            m = mm(bank[k % 4][:, 0:D], sel[:, b, k, :], ring[:, b, k, 0:D], start=False, stop=True)
                            m.then_inc(s_chunk[l], 1)
                def z_transposes(p, b):
                    pe.wait_ge(s_z[l], p + 1)
                    transposes(stage[b], bank[4 + b]).then_inc(s_zt[l], 1)

                def product(p, b):
                    if not isinstance(p, int) or p + 1 < NP:
                        z_transposes(p + 1, 1 - b)
                    pe.wait_ge(s_zc[l], p + 1)
                    if not isinstance(p, int) or p >= 2:
                        pe.wait_ge(s_hc[l], p - 1)
                    for q in range(2):
                        for c in range(DC):
                            m = mm(bank[6 + b][:, q * D:(q + 1) * D], xTp[b][:, (q * DC + c) * P:(q * DC + c + 1) * P],
                                   gw[l][:, c * D:(c + 1) * D], start=c == 0, stop=c == DC - 1)
                    m.then_inc(s_h[l], 1)
                z_transposes(0, 0)
                pairs(pe, product)

            def xf_pair(p, b):
                pe.wait_ge(s_xc, p + 1)
                last = isinstance(p, int) and p == NP - 1
                for q in range(1 if last else 2):
                    for c in range(DC):
                        m = mm(bank[c][:, 0:1], stage[b][:, (q * DC + c) * P:(q * DC + c + 1) * P],
                               valid[:, :] if last else ones[:, 0:1],
                               start=isinstance(p, int) and p == 0 and q == 0, stop=last, skip_group_check=True)
                if last:
                    m.then_inc(s_mean, 1)
                if not isinstance(p, int) or p >= 2:
                    pe.wait_ge(s_fc, p - 1)
                transposes(stage[b], bank[4 + b]).then_inc(s_ft, 1)
            pairs(pe, xf_pair)
            pe.wait_ge(s_mb, 1)
            for c in range(DC):
                mm(bank[2][:, 0:NE], mean_s[:, c * P:(c + 1) * P], wr_s[:, c * NE:(c + 1) * NE], start=c == 0, stop=False)
            mm(bank[2][:, 0:NE], ones[0:1, :], br_s[:, :], start=False, stop=True).then_inc(s_lg, 1)
            pe.wait_ge(s_fw2, 1)
            pe.wait_ge(s_fc, NP)

            def ups(g, j, nt):
                k, jj = j // 4, j % 4
                if j >= 4:
                    pe.wait_ge(s_gelu, g * FJ + j - 3)
                elif not isinstance(g, int) or g > 0:
                    pe.wait_ge(s_gelu, g * FJ + j - 3)
                for c in range(DC):
                    rhs = aggv[:, bass.ds(g * 4, nt), c * P:(c + 1) * P]
                    m = mm(bank[4 + j % 4][:, 0:nt * P], fw1_s[:, k * 1024 + c * 512 + jj * P:k * 1024 + c * 512 + (jj + 1) * P],
                           rhs, start=c == 0, stop=c == DC - 1)
                m.then_inc(s_up, 1)

            def downs(g, j, nt):
                pe.wait_ge(s_gelu, g * FJ + j + 1)
                if j == 0 and (not isinstance(g, int) or g > 0):
                    pe.wait_ge(s_fo, g * 4)
                for q in range(nt):
                    if j == 0:
                        mm(bank[q][:, 0:D], ones[0:1, :], b2row, start=True, stop=False)
                    m = mm(bank[q][:, 0:D], hT[:, j * 512 + q * P:j * 512 + (q + 1) * P], fw2_s[:, j * D:(j + 1) * D],
                           start=False, stop=j == FJ - 1)
                    if j == FJ - 1:
                        m.then_inc(s_down, 1)

            def experts(g, nt):
                ups(g, 0, nt)
                ups(g, 1, nt)
                for j in range(FJ):
                    if j + 2 < FJ:
                        ups(g, j + 2, nt)
                    downs(g, j, nt)
            experts(0, 4)
            with pe.Fori(1, FN_GROUPS) as g:
                experts(g, 4)
            experts(FN_GROUPS, 1)

        @block.vector
        def _(dve):
            ch = Chain(dve, s_dve)
            link = ch.link
            dve.wait_ge(s_const, 8)
            dve.wait_ge(s_edges, 32)
            link(dve.tensor_scalar(e_addr, e_src, 7, None, op0=ALU.arith_shift_right))
            link(dve.tensor_copy(e_blk, e_addr))
            link(dve.tensor_scalar(e_src, e_src, P - 1, None, op0=ALU.bitwise_and))
            link(dve.scalar_tensor_tensor(e_val, e_dst, 256.0, e_src, op0=ALU.mult, op1=ALU.add))
            link(dve.memset(e_zero, 0.0))

            link(dve.tensor_scalar(nhalf, iota_b, -1.0, 0.5, op0=ALU.mult, op1=ALU.add))
            dve.sem_inc(s_cin, 1)

            def count(i):
                for k in range(5):
                    b = i * 5 + k
                    link(dve.tensor_scalar(e_mask, e_blk, iota_b[:, bass.ds(b, 1)], 0.0, op0=ALU.is_equal, op1=ALU.add,
                                           accum_out=cnt[:, bass.ds(b, 1)]))
            ch.loop(HB // 5, 5, count)
            link(dve.memset(small[:, NB + 200:NB + 201], -float(EC)))
            dve.wait_ge(s_sgn, 1)
            link(dve.tensor_tensor(cnt[:, HB:NB], small[:, HB + 200:NB + 200], small[:, HB + 201:NB + 201], op=ALU.subtract))
            dve.tensor_scalar(cnt[:, HB:NB], cnt[:, HB:NB], 0.5, None, op0=ALU.mult).then_inc(s_cnt, 1)
            dve.wait_ge(s_tot, 1)
            link(dve.tensor_scalar(tmpi, bank[1][:, 0:NB], float(P - 1), None, op0=ALU.add))
            link(dve.tensor_scalar(tmpi, tmpi, 7, None, op0=ALU.arith_shift_right))
            link(dve.tensor_copy(tmp, tmpi))
            link(dve.tensor_tensor_scan(cend, tmp, e_zero[:, 0:NB], 0.0, op0=ALU.add, op1=ALU.add))
            link(dve.tensor_sub(tmp, cend, tmp))
            link(dve.scalar_tensor_tensor(base, tmp, float(P), bank[0][:, 0:NB], op0=ALU.mult, op1=ALU.add))
            link(dve.tensor_scalar(base, base, -1.0, None, op0=ALU.add))
            link(dve.tensor_scalar(tmpi[0:NB, 0:1], bank[2][0:NB, 0:1], float(P - 1), None, op0=ALU.add))
            link(dve.tensor_scalar(tmpi[0:NB, 0:1], tmpi[0:NB, 0:1], 7, None, op0=ALU.arith_shift_right))
            dve.tensor_copy(small[0:NB, 301:302], tmpi[0:NB, 0:1]).then_inc(s_tot2, 1)

            for n, width in enumerate(SEGS):
                cols = slice(sum(SEGS[:n]), sum(SEGS[:n + 1]))
                scan = e_scan[:, 0:width]
                mask = e_mask[:, 0:width]

                def rank(i):
                    for k in range(5):
                        b = i * 5 + k
                        link(dve.tensor_scalar(mask, e_blk[:, cols], iota_b[:, bass.ds(b, 1)], None, op0=ALU.is_equal))
                        link(dve.tensor_tensor_scan(scan, mask, e_zero[:, 0:width], base[:, bass.ds(b, 1)], op0=ALU.add, op1=ALU.add))
                        dve.tensor_copy(base[:, bass.ds(b, 1)], scan[:, width - 1:width])
                        link(dve.copy_predicated(e_pos[:, cols], mask.bitcast(U16), scan))
                ch.loop(NB // 5, 15, rank)
                ip = e_addr[:, cols]
                link(dve.tensor_copy(ip, e_pos[:, cols]))
                link(dve.tensor_scalar(scan.bitcast(I32), ip, 7, None, op0=ALU.arith_shift_right))
                link(dve.tensor_scalar(ip, ip, P - 1, None, op0=ALU.bitwise_and))
                dve.scalar_tensor_tensor(ip, ip, float(TW), scan.bitcast(I32), op0=ALU.mult, op1=ALU.add).then_inc(s_rank, 1)
                dve.wait_ge(s_rank, n + 1)

            dve.wait_ge(s_endc, 1)
            link(dve.tensor_copy(small[0:BLK, 302:303], bank[3][0:BLK, 0:1]))
            dve.wait_ge(s_ci, 1)
            dve.tensor_scalar(e_cmp, e_cmp, small[0:BLK, 302:303], None, op0=ALU.is_ge).then_inc(s_blkc, 1)
            dve.wait_ge(s_blkm, 1)
            for n in range(4):
                w = TW // 4
                ins = dve.tensor_copy(blk_row[0:1, n * w:(n + 1) * w], bank[n][0:1, 0:w])
            ins.then_inc(s_blkp, 1)

            def stat_tile(buf, t):
                return dve.bn_stats(stats[:, bass.ds(t * 6, 6)], tile(buf, t))

            def variances(ready):
                sv = stats[:, :].rearrange("p (t c) -> p t c", c=6)
                link(dve.tensor_tensor(mean_all, sv[:, :, 1], sv[:, :, 4], op=ALU.add))
                link(dve.tensor_scalar(mean_all, mean_all, 0.5, None, op0=ALU.mult))
                link(dve.tensor_tensor(nmr[:, :], sv[:, :, 1], sv[:, :, 4], op=ALU.subtract))
                link(dve.tensor_tensor(nmr[:, :], nmr[:, :], nmr[:, :], op=ALU.mult))
                link(dve.tensor_tensor(var_all, sv[:, :, 2], sv[:, :, 5], op=ALU.add))
                link(dve.tensor_scalar(nmr[:, :], nmr[:, :], 0.25, None, op0=ALU.mult))
                dve.scalar_tensor_tensor(var_all, var_all, 1.0 / D, nmr[:, :], op0=ALU.mult, op1=ALU.add).then_inc(ready, 1)

            def finish_stats(std, value, signal=True):
                dve.wait_ge(std, value)
                link(dve.reciprocal(rstd[:, :], rstd[:, :]))
                ins = dve.scalar_tensor_tensor(nmr[:, :], mean_all, -1.0, rstd[:, :], op0=ALU.mult, op1=ALU.mult)
                if signal:
                    ins.then_inc(s_nmr, 1)
                else:
                    link(ins)

            for n in range(5):
                dve.wait_ge(s_x[n], 16)
            ch.loop(NT, 1, lambda t: link(stat_tile(xs, t)))
            variances(s_sq1)
            finish_stats(s_rs1, 1, False)
            link(dve.memset(scale_c[:, 0:1], X_SCALE))
            link(dve.memset(unscale_c[:, 0:1], 1.0 / X_SCALE))
            dve.sem_inc(s_sc, 1)

            def table_low(l, p, b):
                dve.wait_ge(s_hi[l], p + 1)
                dve.nop(nofuse=True)
                dve.scalar_tensor_tensor(split(b)[:, :, 1, :], two(tile(xn, p * 2, 2)), scale_c[:, l:l + 1],
                                         split(b)[:, :, 0, :], op0=ALU.mult, op1=ALU.subtract).then_inc(s_lo[l], 1)

            def norm_pair(p):
                for q in range(2):
                    t = p * 2 + q
                    ins = dve.tensor_scalar(tile(xn, t), tile(xs, t), rstd[:, bass.ds(t, 1)], nmr[:, bass.ds(t, 1)],
                                            op0=ALU.mult, op1=ALU.add)
                return ins

            def first(p, b):
                if isinstance(p, int) and p == 0:
                    norm_pair(0).then_inc(s_nrm, 1)
                if not isinstance(p, int) or p + 1 < NP:
                    norm_pair(p + 1).then_inc(s_nrm, 1)
                table_low(0, p, b)
            pairs(dve, first)

            dve.wait_ge(s_wmix, 48)
            wg = wkv_s.rearrange("p (g e) -> p g e", e=DH)
            link(dve.tensor_reduce(small[:, 0:32], wg, axis=AX.X, op=ALU.add))
            link(dve.tensor_scalar(small[:, 0:32], small[:, 0:32], -1.0 / DH, None, op0=ALU.mult))
            dve.tensor_tensor(wg, wg, small[:, 0:32].unsqueeze(2).to_broadcast([P, 32, DH]), op=ALU.add).then_inc(s_wc, 1)
            dve.memset(zeros, 0.0).then_inc(s_wc, 1)
            link(dve.memset(dots_s, 0.0))

            def kv_tile(t):
                dve.wait_ge(s_kvq, t + 1)
                dve.nop(nofuse=True)
                link(dve.tensor_reduce(small[:, 0:16], kv_sq.rearrange("p (g e) -> p g e", e=DH), axis=AX.X, op=ALU.add))
                link(dve.tensor_scalar(small[:, 0:16], small[:, 0:16], 1.0 / DH, EPS, op0=ALU.mult, op1=ALU.add))
                dve.tensor_tensor(small[:, 16:24], small[:, 0:8], small[:, 8:16], op=ALU.mult).then_inc(s_kvr, 1)
                dve.wait_ge(s_kvs, t + 1)
                dve.nop(nofuse=True)
                link(dve.reciprocal(small[:, 32:40], small[:, 24:32]))
                kg = kv[:, 0:512].rearrange("p (g e) -> p g e", e=DH)
                dve.tensor_tensor(kg, kg, small[:, 32:40].unsqueeze(2).to_broadcast([P, 8, DH]), op=ALU.mult).then_inc(s_kn, 1)
            ch.loop(NT, 3, kv_tile)
            dve.wait_ge(s_dots, NT + 1)
            for h in range(2):
                src_d = bank[7][h * DH:(h + 1) * DH, :].rearrange("p (q d) -> p q d", d=P)[:, :, h * DH:(h + 1) * DH]
                dst_d = dots_s[h * DH:(h + 1) * DH, :].rearrange("p (q d) -> p q d", d=P)[:, :, h * DH:(h + 1) * DH]
                ins = dve.tensor_copy(dst_d, src_d)
                if h == 0:
                    link(ins)
            ins.then_inc(s_dd, 1)
            with dve.Fori(0, NP // 2) as i:
                for b in range(2):
                    p = i * 2 + b
                    dve.wait_ge(s_op, p + 1)
                    dve.nop(nofuse=True)
                    dve.tensor_tensor(tile(xs, p * 2, 2), tile(xs, p * 2, 2), bank[b][:, :], op=ALU.add).then_inc(s_oa, 1)
            dve.wait_ge(s_op, NP)
            dve.tensor_tensor(tile(xs, NT - 2, 2), tile(xs, NT - 2, 2), bank[0][:, :], op=ALU.add).then_inc(s_oa, 1)
            dve.wait_ge(s_w, 16 * 11)
            for l in range(2):
                gwv = gw[l].rearrange("p (c e) -> p c e", c=DC)
                link(dve.tensor_reduce(small[:, 0:DC], gwv, axis=AX.X, op=ALU.add))
                link(dve.tensor_reduce(small[:, DC:DC + 1], brow[l], axis=AX.X, op=ALU.add))
                link(dve.tensor_scalar(small[:, 0:DC + 1], small[:, 0:DC + 1], -1.0 / D, None, op0=ALU.mult))
                link(dve.tensor_tensor(gwv, gwv, small[:, 0:DC].unsqueeze(2).to_broadcast([P, DC, D]), op=ALU.add))
                link(dve.tensor_scalar(brow[l], brow[l], small[:, DC:DC + 1], None, op0=ALU.add))
            link(dve.tensor_reduce(small[:, 40:41], gvec[0][0], axis=AX.X, op=ALU.max, apply_absolute_value=True))
            link(dve.tensor_reduce(small[:, 41:42], gvec[0][1], axis=AX.X, op=ALU.max, apply_absolute_value=True))
            link(dve.scalar_tensor_tensor(small[:, 40:41], small[:, 40:41], 16.0, small[:, 41:42], op0=ALU.mult, op1=ALU.add))
            link(dve.tensor_scalar(small[:, 40:41], small[:, 40:41], 2.0 ** -60, 2.0 ** 60, op0=ALU.max, op1=ALU.min))
            bits = small[:, 42:43].bitcast(I32)
            link(dve.tensor_scalar(bits, small[:, 40:41].bitcast(I32), 0x7F800000, None, op0=ALU.bitwise_and))
            link(dve.tensor_scalar(scale_c[:, 1:2].bitcast(I32), bits, -1.0, float(268 << 23), op0=ALU.mult, op1=ALU.add))
            link(dve.tensor_scalar(unscale_c[:, 1:2].bitcast(I32), bits, -float(14 << 23), None, op0=ALU.add))
            dve.sem_inc(s_sc, 1)
            dve.wait_ge(s_back, 16)
            link(dve.tensor_scalar(e_tmp, edst[:, :], 255, None, op0=ALU.bitwise_and))
            link(dve.tensor_scalar(edst[:, :], edst[:, :], 8, None, op0=ALU.arith_shift_right))
            link(dve.tensor_copy(esrc[:, :], e_tmp))
            link(dve.memset(ring[:, :, :, 2 * D:2 * D + 1], 1.0))
            dve.sem_inc(s_blkp, 1)

            for l in range(2):
                def selectors(i, b):
                    dve.wait_ge(s_chunk[l], (i * 2 + b + 1) * GB)
                    dve.nop(nofuse=True)
                    dve.tensor_tensor(sel[:, b, :, :], iota_p[:, :].unsqueeze(1).to_broadcast([P, GB, P]),
                                      esrc[:, bass.ds((i * 2 + b) * GB, GB)].unsqueeze(2).to_broadcast([P, GB, P]),
                                      op=ALU.is_equal).then_inc(s_sel[l][b], 1)
                for b in range(2):
                    dve.wait_ge(s_tab[l][b], (NP + 1 - b) // 2 * 16)
                for b in range(2):
                    selectors(0, b)
                if l == 0:
                    link(dve.memset(agg[:, :], 0.0))
                else:
                    dve.wait_ge(s_zero, 1)
                dve.sem_inc(s_added[l], 4)
                with dve.Fori(0, NCH // (2 * GB)) as i:
                    for b in range(2):
                        _, where = nc.values_load_multi_w_load_instructions(
                            blk_row[0:1, bass.ds((i * 2 + b) * GB, GB)], engines=(mybir.EngineType.DVE,), min_val=0, max_val=NT - 1)
                        for k in range(GB):
                            n = (i * 2 + b) * GB + k
                            dve.wait_ge(s_chunk[l], n + 2 * GB + 1)
                            dve.wait_ge(s_added[l], n + 4)
                            dve.nop(nofuse=True)
                            part = agg[:, bass.ds(where[k] * AW, AW)]
                            dve.tensor_tensor(part, part, bank[k % 4][:, 0:AW], op=ALU.add).then_inc(s_added[l], 1)
                        selectors(i + 1, b)
                dve.wait_ge(s_added[l], NCH + 4)
                u = small[:, 0:NT]
                link(dve.tensor_scalar(u, aggv[:, :, D], 1.0, None, op0=ALU.max))
                link(dve.reciprocal(u, u))
                link(dve.tensor_scalar(u, u, unscale_c[:, l:l + 1], None, op0=ALU.mult))

                def z_pair(p, b):
                    if not isinstance(p, int) or p >= 2:
                        dve.wait_ge(s_zt[l], p - 1)
                        dve.nop(nofuse=True)
                    for q in range(2):
                        t = p * 2 + q
                        ins = dve.scalar_tensor_tensor(stage[b][:, q * D:(q + 1) * D], agg[:, bass.ds(t * AW, D)],
                                                       small[:, bass.ds(t, 1)], tile(xn, t), op0=ALU.mult, op1=ALU.add)
                    ins.then_inc(s_z[l], 1)

                def h_pair(p, b):
                    dve.wait_ge(s_h[l], p + 1)
                    dve.nop(nofuse=True)
                    dve.tensor_tensor(two(tile(xn, p * 2, 2)), two(bank[6 + b][:, :]), both(brow[l]), op=ALU.add).then_inc(s_hc[l], 1)
                    if not isinstance(p, int) or p + 2 < NP:
                        z_pair(p + 2, b)
                    dve.wait_ge(s_hc[l], p + 1)
                    dve.nop(nofuse=True)
                    for q in range(2):
                        stat_tile(xn, p * 2 + q).then_inc(s_st[l], 1)
                z_pair(0, 0)
                z_pair(1, 1)
                pairs(dve, h_pair)
                dve.wait_ge(s_st[l], NT)
                variances(s_var[l])
                finish_stats(s_std[l], 1, False)
                if l == 0:
                    link(dve.memset(ring[:, :, :, 2 * D:2 * D + 1], 1.0))

                def scaled(p):
                    for q in range(2):
                        t = p * 2 + q
                        ins = dve.scalar_tensor_tensor(tile(xn, t), tile(xn, t), rstd[:, bass.ds(t, 1)], gvec[l][0],
                                                       op0=ALU.mult, op1=ALU.mult)
                    ins.then_inc(s_nr[l], 1)

                def emit(p, b):
                    if not isinstance(p, int) or p + 2 < NP:
                        scaled(p + 2)
                    if l == 0:
                        table_low(1, p, b)
                    else:
                        dve.wait_ge(s_y[1], p + 1)
                        dve.nop(nofuse=True)
                        dve.tensor_tensor(tile(xs, p * 2, 2), tile(xs, p * 2, 2), tile(xn, p * 2, 2), op=ALU.add).then_inc(s_res, 1)
                        dve.wait_ge(s_res, p + 1)
                        dve.nop(nofuse=True)
                        for q in range(2):
                            stat_tile(xs, p * 2 + q).then_inc(s_st[2], 1)
                scaled(0)
                scaled(1)
                pairs(dve, emit)
            dve.wait_ge(s_st[2], NT)
            variances(s_var[2])
            finish_stats(s_std[2], 1, False)
            with dve.Fori(0, NP) as p:
                norm_pair(p).then_inc(s_xf, 1)

            dve.wait_ge(s_mean, 1)
            for c in range(DC):
                ins = dve.tensor_scalar(mean_s[:, c * P:(c + 1) * P], ones[:, :], bank[c][:, 0:1], 1.0 / N, op0=ALU.mult, op1=ALU.mult)
            ins.then_inc(s_mb, 1)
            w8, e8, c8, o8, p8 = (small[:, 8 * n:8 * n + 8] for n in (0, 1, 2, 3, 4))
            one = small[:, 60:61]

            def softmax(src_ap, dst_ap, n):
                link(dve.tensor_reduce(one, src_ap, axis=AX.X, op=ALU.max))
                dve.tensor_scalar(w8, src_ap, one, None, op0=ALU.subtract).then_inc(s_exin, 1)
                dve.wait_ge(s_ex, n)
                dve.nop(nofuse=True)
                link(dve.tensor_reduce(one, e8, axis=AX.X, op=ALU.add))
                link(dve.reciprocal(one, one))
                link(dve.tensor_scalar(dst_ap, e8, one, None, op0=ALU.mult))
            dve.wait_ge(s_lg, 1)
            softmax(bank[2][:, 0:NE], c8, 1)
            link(dve.tensor_scalar(o8, c8, float(N), 1e-30, op0=ALU.mult, op1=ALU.max))
            link(dve.reciprocal(o8, o8))
            link(dve.tensor_scalar(o8, o8, CAP, 1.0, op0=ALU.mult, op1=ALU.min))
            link(dve.tensor_tensor(c8, c8, o8, op=ALU.mult))
            softmax(c8, c8, 2)
            for k in range(2):
                top = small[:, 62 + k:63 + k]
                link(dve.tensor_reduce(top, c8, axis=AX.X, op=ALU.max))
                link(dve.tensor_scalar(o8, c8, top, -100.0, op0=ALU.is_equal, op1=ALU.mult))
                link(dve.tensor_tensor(o8, o8, iota_b[:, 0:NE], op=ALU.add))
                link(dve.tensor_reduce(small[:, 66 + k:67 + k], o8, axis=AX.X, op=ALU.min))
                link(dve.tensor_scalar(small[:, 66 + k:67 + k], small[:, 66 + k:67 + k], 100.0, None, op0=ALU.add))
                link(dve.tensor_copy(small[:, 64 + k:65 + k].bitcast(I32), small[:, 66 + k:67 + k]))
                if k == 0:
                    link(dve.tensor_scalar(p8, iota_b[:, 0:NE], small[:, 66:67], 4.0, op0=ALU.is_equal, op1=ALU.mult))
                    link(dve.tensor_tensor(c8, c8, p8, op=ALU.subtract))
            dve.sem_inc(s_pick, 1)
            dve.tensor_scalar(w8, ones[:, 0:NE], small[:, 63:64], small[:, 62:63], op0=ALU.mult, op1=ALU.subtract).then_inc(s_exin, 1)
            dve.wait_ge(s_ex, 3)
            tw = [small[:, 70:71], small[:, 71:72]]
            link(dve.tensor_scalar(tw[0], e8[:, 0:1], 1.0, None, op0=ALU.add))
            link(dve.reciprocal(tw[0], tw[0]))
            link(dve.tensor_tensor(tw[1], e8[:, 0:1], tw[0], op=ALU.mult))
            dve.wait_ge(s_fw, 160)
            for k in range(2):
                link(dve.tensor_scalar(fw2_s[:, k * 1024:(k + 1) * 1024], fw2_s[:, k * 1024:(k + 1) * 1024], tw[k], None, op0=ALU.mult))
                link(dve.tensor_scalar(b2two[:, k * D:(k + 1) * D], b2two[:, k * D:(k + 1) * D], tw[k][0:1, :], None, op0=ALU.mult))
            dve.tensor_tensor(b2row, b2row, b2two[:, D:2 * D], op=ALU.add).then_inc(s_fw2, 1)

            def outputs(g, nt):
                for q in range(nt):
                    t = g * 4 + q
                    dve.wait_ge(s_down, t + 1)
                    dve.nop(nofuse=True)
                    dve.tensor_tensor(tile(xn, t), tile(xn, t), bank[q][:, 0:D], op=ALU.add).then_inc(s_fo, 1)
                    dve.wait_ge(s_fo, t + 1)
                    dve.nop(nofuse=True)
                    link(stat_tile(xn, t))
            ch.loop(FN_GROUPS, 4, lambda g: outputs(g, 4))
            outputs(FN_GROUPS, 1)
            variances(s_fvar)
            finish_stats(s_fstd, 1)

            def out_affine(p):
                dve.wait_ge(s_fn, p * 2 + 2)
                dve.nop(nofuse=True)
                pair = two(tile(xn, p * 2, 2))
                link(dve.tensor_tensor(pair, pair, both(gab), op=ALU.mult))
                dve.tensor_tensor(pair, pair, both(beb), op=ALU.add).then_inc(s_fa, 1)
            ch.loop(NP, 1, out_affine)


def kernel(**inputs):
    import numpy as np
    import concourse.bacc as bacc
    from concourse.bass_utils import run_bass_kernel_spmd

    a = {k: np.ascontiguousarray(v) for k, v in inputs.items()}
    edges = {}
    for name, fill in (("src", PAD_NODE), ("dst", 0)):
        flat = np.full(P * EC, fill, a[name].dtype)
        flat[:E] = a[name]
        edges[name] = flat.reshape(P, EC)
    rows = np.zeros((NT * P, D), a["x"].dtype)
    rows[:N] = a["x"]
    wqkv = a["L0_mix_w_qkv"]

    def row(name):
        return a[name].reshape(1, -1)
    arrays = {
        "x": rows, "src": edges["src"], "dst": edges["dst"],
        "w0": np.ascontiguousarray(a["L0_gnn_W0"].T), "b0": row("L0_gnn_b0"), "g0": row("L0_gnn_g0"), "be0": row("L0_gnn_beta0"),
        "w1": np.ascontiguousarray(a["L0_gnn_W1"].T), "b1": row("L0_gnn_b1"), "g1": row("L0_gnn_g1"), "be1": row("L0_gnn_beta1"),
        "wq": np.ascontiguousarray(wqkv[:INNER]), "wkv": np.ascontiguousarray(wqkv[INNER:].T),
        "wo": np.ascontiguousarray(a["L0_mix_w_out"].T), "bo": row("L0_mix_b_out"),
        "wr": a["L0_ffn_Wr"], "br": row("L0_ffn_br"), "fw1": a["L0_ffn_W1"],
        "fb1": np.ascontiguousarray(a["L0_ffn_b1"].reshape(NE, F // P, P).transpose(0, 2, 1)),
        "fw2": a["L0_ffn_W2"], "fb2": a["L0_ffn_b2"], "ga": row("L0_ffn_gamma"), "be": row("L0_ffn_beta"),
    }
    nc = bacc.Bacc("TRN2", target_bir_lowering=False, num_devices=1)
    args = {n: nc.dram_tensor(f"in_{n}", v.shape, mybir.dt.from_np(v.dtype), kind="ExternalInput").ap() for n, v in arrays.items()}
    out = nc.dram_tensor("out", (NT * P, D), F32, kind="ExternalOutput").ap()
    gps_layer(nc, **args, out=out)
    r = run_bass_kernel_spmd(nc, [{f"in_{n}": v for n, v in arrays.items()}], core_ids=[0])
    return r.results[0]["out"][:N]
```

```python
from contextlib import ExitStack

import concourse.bass as bass
from concourse import mybir

F32 = mybir.dt.float32
F16 = mybir.dt.float16
BF16 = mybir.dt.bfloat16
I32 = mybir.dt.int32
I16 = mybir.dt.int16
U16 = mybir.dt.uint16
ALU = mybir.AluOpType
ACT = mybir.ActivationFunctionType
AX = mybir.AxisListType

P = 128
N = 6250
E = 200000
D = 256
DC = D // P
NT = 50
LAST = N // P
BLK = LAST + 1
NB = BLK + 1
EC = 1564
PAD_NODE = BLK * P
NCH = 1616
TW = 1632
USED = (E + (BLK - 1) * (P - 1)) // P
GB = 8
SB = 34
ES, EW = 3, 68
SEGS = (EW,) * ES + (612, 748)
SC = max(SEGS)
HB = 30
NP = NT // 2
AW = D + 1
RW = 2 * D + 2
HEADS, DH = 8, 64
PAIRS = HEADS // 2
INNER = HEADS * DH
NE, F = 8, 512
FJ = 2 * F // P
EPS = 1e-5
X_SCALE = 2048.0
CAP = float(-(-N * 5 // (4 * NE)))

assert 0 < NCH - USED < GB
assert (E + (NB - 1) * (P - 1)) // P <= NCH and NCH % (2 * GB) == 0 and EC % (2 * SB) == 0
assert E <= P * EC and (E + (NB - 1) * (P - 1)) // P + -(-(P * EC - E) // P) <= TW
assert NP % 4 == 1 and NP > 9
assert sum(SEGS) == EC and all(c % (2 * SB) == 0 for c in SEGS)


class Chain:

    def __init__(self, eng, sem):
        self.eng, self.sem, self.n, self.at = eng, sem, 0, 0

    def link(self, ins):
        ins.then_inc(self.sem, 1)
        self.n += 1
        self.eng.wait_ge(self.sem, self.at + self.n)
        if not isinstance(self.at, int):
            self.eng.nop(nofuse=True)

    def loop(self, count, links, body):
        first = self.n
        with self.eng.Fori(0, count) as i:
            self.at = i * links
            body(i)
            assert self.n - first == links, self.n - first
        self.at, self.n = 0, first + count * links


def pairs(eng, body):
    for p in range(2):
        body(p, p)
    with eng.Fori(1, (NP - 3) // 2) as i:
        for b in range(2):
            body(i * 2 + b, b)
    for p in range(NP - 3, NP):
        body(p, p % 2)


def quads(eng, body):
    for p in range(4):
        body(p, p)
    with eng.Fori(1, (NP - 5) // 4) as i:
        for b in range(4):
            body(i * 4 + b, b)
    for p in range(NP - 5, NP):
        body(p, p % 4)


def gps_layer(nc, x, src, dst, w0, b0, g0, be0, w1, b1, g1, be1, wq, wkv, wo, bo,
              wr, br, fw1, fb1, fw2, fb2, ga, be, out):
    ctx = ExitStack()
    with ctx:
        def sb(name, shape, dt=F32):
            return ctx.enter_context(nc.sbuf_tensor(name, shape, dt))

        def sem(name):
            return ctx.enter_context(nc.semaphore(name))

        sorted_edges = nc.dram_tensor("sorted_edges", [P * TW, 1], I32, kind="Internal").ap()
        table = [nc.dram_tensor(f"table{n}", [NT * P, 2 * D], F16, kind="Internal").ap() for n in range(2)]

        xs = sb("xs", [P, NT * D])
        xn = sb("xn", [P, NT * D])
        agg = sb("agg", [P, NT * AW])
        edst = sb("edst", [P, TW], I32)
        esrc = sb("esrc", [P, TW], F16)
        ring = sb("ring", [P, 2, GB, RW], F16)
        sel = sb("sel", [P, 2, GB, P], F16)
        big = sb("big", [P, 4096])
        xT = sb("xT", [P, 2, D])
        stats = sb("stats", [P, NT * 6])
        mv = sb("mv", [P, NT * 2])
        wr_s = sb("wr_s", [P, DC * NE])
        br_s = sb("br_s", [1, NE])
        rstd = sb("rstd", [P, NT])
        nmr = sb("nmr", [P, NT])
        small = sb("small", [P, 320])
        ident = sb("ident", [P, P])
        iota_p = sb("iota_p", [P, P], F16)
        ones = sb("ones", [P, P])
        ones_b = sb("ones_b", [P, P], BF16)
        blk_row = sb("blk_row", [1, TW], I16)
        valid = sb("valid", [P, 1])
        edge_ring = sb("edge_ring", [P, 2, 2, SB], I32)
        val_ring, idx_ring = edge_ring[:, :, 0, :], edge_ring[:, :, 1, :]
        eps_c = sb("eps_c", [P, 1])
        scale_c = sb("scale_c", [P, 2])
        unscale_c = sb("unscale_c", [P, 2])
        fsc = sb("product_scales", [P, 16])
        zsc = sb("z_scales", [P, 2])

        aggi = agg[:, :].bitcast(I32)
        aggh = agg[:, :].bitcast(F16)
        e_src, e_dst = aggi[:, 0:EC], aggi[:, EC:2 * EC]
        e_pos, e_addr = agg[:, 2 * EC:3 * EC], aggi[:, 2 * EC:3 * EC]
        e_val = e_src
        e_out = aggi[:, 0:4 * EC].rearrange("p (a c) -> p a c", a=4)[:, 0:4:2, :]
        e_blk = aggh[:, 6 * EC:7 * EC]
        e_mask = aggh[:, 7 * EC:8 * EC]
        e_scan = agg[:, 4 * EC:4 * EC + SC]
        m0 = 4 * EC + SC
        wkv_s = agg[:, m0:m0 + 2048]
        wq_s = agg[:, m0 + 2048:m0 + 3072]
        wo_s = agg[:, m0 + 3072:m0 + 4096]
        kv = agg[:, m0 + 4096:m0 + 5120]
        assert m0 + 5120 <= NT * AW
        ringf = ring[:, :, :, :].rearrange("p a b c -> p (a b c)").bitcast(F32)
        kv_sq = ringf[:, 0:1024]
        r_mask = xn[:, 0:NB * (EW + 1)].rearrange("p (b w) -> p b w", b=NB)
        r_scan = xn[:, NB * (EW + 1):2 * NB * (EW + 1)].rearrange("p (b w) -> p b w", b=NB)
        r_pos = xn[:, 2 * NB * (EW + 1):2 * NB * (EW + 1) + NB * EW].rearrange("p (b w) -> p b w", b=NB)
        r0 = 2 * NB * (EW + 1) + NB * EW
        r_keep = xn[:, r0:r0 + NB * (EW + 1) // 2].bitcast(F16)
        m_s = ringf[:, 1024:2048]
        dots_s = ringf[:, 2048:2560]
        zeros = ringf[:, 2560:3072]
        e_zero = ringf[:, 3072:3072 + SC // 2].bitcast(F16)
        c_mask = [xn[:, k * EC // 2:(k + 1) * EC // 2].bitcast(F16) for k in range(5)]
        c_sign = [xn[:, (k + 5) * EC // 2:(k + 6) * EC // 2].bitcast(F16) for k in range(5)]
        tri = ringf[:, 3456:3584]
        g_s = big[:, 0:512]
        gw = [big[:, 512:1024], big[:, 1024:1536]]
        gvec = [(big[:, 1536:1792], big[:, 1792:2048]), (big[:, 2048:2304], big[:, 2304:2560])]
        fw1_in, fw2_in = ringf[:, 0:2048], ringf[:, 2048:4096]
        w1p = big[:, 0:2048].bitcast(F16).rearrange("p (h c) -> p h c", h=2)
        w2p = big[:, 2048:4096].bitcast(F16).rearrange("p (h c) -> p h c", h=2)
        xfp = aggh.rearrange("p (t c) -> p t c", c=2 * AW)
        hid = [edst[:, n * 512:(n + 1) * 512].bitcast(F32) for n in range(2)]
        hp = ringf[:, 0:2048].bitcast(F16).rearrange("p (s h c) -> p s h c", s=4, h=2)
        fw_all = agg[:, 4 * EC + SC:4 * EC + SC + 4096]
        brow = [big[:, 2560:2816], big[:, 2816:3072]]
        b2two = xT[:, :, :].rearrange("p a b -> p (a b)")
        gwp = [w.bitcast(F16).rearrange("p (h c) -> p h c", h=2) for w in gw]
        bparts = [brow[l].bitcast(BF16) for l in range(2)]
        borow, b2row = big[0:1, 3072:3328], b2two[:, 0:D]
        stage = [big[:, 3328:3840], big[:, 0:512]]
        xf_stages = stage + [big[:, 512:1024], big[:, 1024:1536]]
        xTp = [xT[:, :, :].rearrange("p a b -> p (a b)"), ringf[:, 0:2 * D]]
        xTs = [x.bitcast(F16).rearrange("p (h c) -> p h c", h=2) for x in xTp]
        sel_f = sel[:, :, :, :].rearrange("p a b c -> p (a b c)").bitcast(F32)
        gab, beb = sel_f[:, 0:D], sel_f[:, D:2 * D]

        cnt = small[:, 0:NB]
        iota_b = small[:, 50:100]
        base = small[:, 100:150]
        nhalf = small[:, 150:200]
        cend = small[:, 150:200]
        tmp = small[:, 200:250]
        tmpi = small[:, 250:300].bitcast(I32)

        mean_all, var_all = mv[:, 0:NT], mv[:, NT:2 * NT]
        aggv = agg[:, :].rearrange("p (t c) -> p t c", c=AW)
        e_cmp = ringf[0:BLK, 0:TW]
        e_tmp = ringf[:, 0:TW].bitcast(I32)
        mean_s, mean_row = ringf[:, 0:D], ringf[0:1, D:2 * D]

        bank = [ctx.enter_context(nc.psum_tensor(f"bank{n}", [P, 512], F32)) for n in range(8)]

        rows_buf = [sel[:, b, :, :].rearrange("p k c -> p (k c)") for b in range(2)] + [xTp[0].bitcast(F16), stage[0].bitcast(F16)]
        BUFS = (2, 4)

        def split(b):
            return rows_buf[b].rearrange("p (t h d) -> p t h d", t=2, h=2)

        def tab_written(eng, l):
            for b in range(BUFS[l]):
                eng.wait_ge(s_tab[l][b], ((NP - 1 - b) // BUFS[l] + 1) * 16)

        def two(ap):
            return ap.rearrange("p (t d) -> p t d", t=2)

        def both(ap):
            return ap.unsqueeze(1).to_broadcast([P, 2, D])

        def tile(buf, t, n=1):
            return buf[:, bass.ds(t * D, n * D)]

        s_edges, s_w, s_wmix, s_tabinit = sem("edges_in"), sem("weights_in"), sem("mix_weights_in"), sem("table_init")
        s_x = [sem(f"x_in{n}") for n in range(5)]
        s_const = sem("constants")
        s_pre = sem("pool_steps")
        s_cnt, s_tot, s_tot2, s_blkc, s_blkp = (sem("counts_ready"), sem("totals_ready"), sem("ends_column"),
                                                sem("chunk_compare"), sem("chunk_blocks"))
        s_endc, s_blkm = sem("block_ends"), sem("chunk_blocks_product")
        s_ci, s_sc = sem("chunk_iota"), sem("table_scales")
        s_rank, s_keep = sem("segment_ranked"), sem("block_starts")
        s_cin, s_sgn = sem("count_inputs"), sem("sign_sums")
        s_sidx = sem("scatter_indices")
        s_scat = [sem("scatter_even"), sem("scatter_odd")]
        s_back, s_tab = sem("sorted_back"), [[sem(f"table{l}_buffer{b}_written") for b in range(BUFS[l])] for l in range(2)]
        s_dve = sem("dve_chain")
        s_act = sem("act_chain")

        block = ctx.enter_context(nc.Block())

        s_sq1, s_rs1, s_nrm = sem("ln1_var"), sem("ln1_std"), sem("ln1_done")
        s_hi = [sem("table0_high"), sem("table1_high")]
        s_lo = [sem("table0_low"), sem("table1_low")]
        s_wc = sem("kv_weights_centred")
        s_mst, s_mtp, s_mxT, s_kvp, s_kvc, s_kvq, s_kvr, s_kvs, s_kn, s_dots = (
            sem("mix_staged"), sem("mix_transposed"), sem("mix_xT"), sem("kv_product"), sem("kv_copied"), sem("kv_squares"),
            sem("kv_var"), sem("kv_std"), sem("k_scaled"), sem("dots_added"))
        s_dd, s_mp, s_mc, s_gp, s_gc = (sem("dots_diag"), sem("m_product"), sem("m_copied"),
                                        sem("g_product"), sem("g_copied"))
        s_ost = sem("mixout_staged")
        s_otp, s_oxT, s_op, s_oa = sem("mixout_transposed"), sem("mixout_xT"), sem("mixout_product"), sem("mixout_added")
        s_gidx = [sem("gather0_indices"), sem("gather1_indices")]
        s_gath = [[sem(f"gather{l}_even"), sem(f"gather{l}_odd")] for l in range(2)]
        s_sel = [[sem(f"sel{l}_even"), sem(f"sel{l}_odd")] for l in range(2)]
        s_chunk = [sem(f"chunk{l}_product") for l in range(2)]
        s_added = [sem(f"chunk{l}_added") for l in range(2)]
        s_z = [sem(f"z{l}") for l in range(2)]
        s_zt = [sem(f"z{l}_transposed") for l in range(2)]
        s_zl = [sem(f"zT{l}_low") for l in range(2)]
        s_zc = [sem(f"zT{l}_copied") for l in range(2)]
        s_st = [sem(f"stats{l}_done") for l in range(3)]
        s_res = sem("residual_added")
        s_h = [sem(f"h{l}_product") for l in range(2)]
        s_hc = [sem(f"h{l}_copied") for l in range(2)]
        s_zero = sem("aggregate_cleared")
        s_var = [sem(f"h{l}_var") for l in range(3)]
        s_std = [sem(f"h{l}_std") for l in range(3)]
        s_nr = [sem(f"h{l}_normalised") for l in range(2)]
        s_gb = [sem(f"h{l}_affine") for l in range(2)]
        s_y = [sem(f"y{l}") for l in range(2)]
        s_xc = [sem("xf_staged_even"), sem("xf_staged_odd")]
        s_xf, s_ft, s_fc, s_mean = sem("xf"), sem("xf_transposed"), sem("xfT_copied"), sem("mean_product")
        s_mb, s_lg, s_ex = sem("mean_spread"), sem("logits"), sem("router_exp")
        s_exin, s_nmr = sem("router_exp_in"), sem("mean_term")
        s_pick, s_fw1, s_fw2, s_fvec = sem("experts_chosen"), sem("w1_in"), sem("w2_in"), sem("out_vectors_in")
        s_wmax, s_wred, s_rowmax, s_scrow, s_scall = (sem("all_weights_in"), sem("weights_reduced"), sem("maxima_in_rows"),
                                                      sem("scales_in_row"), sem("scales_everywhere"))
        s_w1h, s_w1l, s_w2t, s_w2h, s_w2l = (sem("w1_high"), sem("w1_low"), sem("w2_weighted"), sem("w2_high"), sem("w2_low"))
        s_fl, s_b2, s_xfb = sem("xfT_low"), sem("b2_row"), sem("b2_on_input")
        s_mrow, s_mcol = sem("mean_row"), sem("mean_column")
        s_resb = sem("beta_on_residual")
        s_up, s_gelu, s_hhi, s_hlo = sem("up_product"), sem("gelu"), sem("hidden_high"), sem("hidden_low")
        s_down, s_outp, s_fo = sem("down_product"), sem("ffn_product"), sem("ffn_added")
        s_fvar, s_fstd, s_out, s_fdma = sem("out_var"), sem("out_std"), sem("out_ready"), sem("out_written")
        FN_GROUPS = LAST // 4
        assert LAST % 4 == 0

        @block.sync
        def _(sp):
            sp.dma_start(e_src, src).then_inc(s_edges, 16)
            sp.dma_start(e_dst, dst).then_inc(s_edges, 16)
            for n in range(5):
                w = NT // 5 * P
                sp.dma_start(xs[:, n * 2560:(n + 1) * 2560].rearrange("p (t d) -> p t d", d=D),
                             x[n * w:(n + 1) * w, :].rearrange("(t p) d -> p t d", p=P)).then_inc(s_x[n], 16)
            sp.dma_start(wkv_s.rearrange("p (c e) -> p c e", c=DC), wkv.rearrange("(c p) e -> p c e", p=P)).then_inc(s_wmix, 16)
            sp.dma_start(wq_s.rearrange("p (c e) -> p c e", c=PAIRS), wq.rearrange("(c p) e -> p c e", p=P)).then_inc(s_wmix, 16)
            sp.dma_start(wo_s.rearrange("p (c e) -> p c e", c=PAIRS), wo.rearrange("(c p) e -> p c e", p=P)).then_inc(s_wmix, 16)
            for l, (w, g, b, r) in enumerate(((w0, g0, be0, b0), (w1, g1, be1, b1))):
                sp.dma_start(gw[l].rearrange("p (c e) -> p c e", c=DC), w.rearrange("(c p) e -> p c e", p=P)).then_inc(s_w, 16)
                sp.dma_start(gvec[l][0], g.to_broadcast([P, D])).then_inc(s_w, 16)
                sp.dma_start(gvec[l][1], b.to_broadcast([P, D])).then_inc(s_w, 16)
                sp.dma_start(brow[l], r.to_broadcast([P, D])).then_inc(s_w, 16)
            sp.dma_start(borow, bo).then_inc(s_w, 16)
            sp.dma_start(wr_s[:, :].rearrange("p (c e) -> p c e", c=DC), wr.rearrange("(c p) e -> p c e", p=P)).then_inc(s_w, 16)
            sp.dma_start(br_s[:, :], br).then_inc(s_w, 16)
            def write_pair(l, p, b):
                sp.wait_ge(s_lo[l], p + 1)
                sp.dma_start(table[l][bass.ds(p * 2 * P, 2 * P), :].rearrange("(t p) c -> p t c", p=P),
                             rows_buf[b].rearrange("p (t c) -> p t c", t=2)).then_inc(s_tab[l][b], 16)

            def write_table(l):
                with sp.Fori(0, NP // BUFS[l]) as i:
                    for b in range(BUFS[l]):
                        write_pair(l, i * BUFS[l] + b, b)
                write_pair(l, NP - 1, 0)
            write_table(0)
            for n in range(4):
                if n == 0:
                    sp.wait_ge(s_oa, NP)
                else:
                    sp.wait_ge(s_wred, n)
                h = slice(n % 2 * (NE // 2), (n % 2 + 1) * (NE // 2))
                if n < 2:
                    sp.dma_start(fw_all.rearrange("p (c f) -> p c f", f=F),
                                 fw1[h, :, :].rearrange("e (c p) f -> p (e c) f", p=P)).then_inc(s_wmax, 16)
                else:
                    sp.dma_start(fw_all.rearrange("p (c f) -> p c f", f=D),
                                 fw2[h, :, :].rearrange("e (c p) f -> p (e c) f", p=P)).then_inc(s_wmax, 16)
            sp.wait_ge(s_wred, 4)
            sp.dma_start(fw_all[:, 0:NE * F // P].rearrange("p (e c) -> p e c", e=NE),
                         fb1.rearrange("e p c -> p e c")).then_inc(s_wmax, 16)
            for b in range(2):
                sp.wait_ge(s_scat[b], EC // 2 * 16)
            sp.dma_start(edst[:, :], sorted_edges.rearrange("(p c) o -> p (c o)", p=P)).then_inc(s_back, 16)
            write_table(1)
            sp.wait_ge(s_added[1], USED + 4)
            sp.dma_start(gab, ga.to_broadcast([P, D])).then_inc(s_fvec, 16)
            sp.dma_start(beb, be.to_broadcast([P, D])).then_inc(s_fvec, 16)
            sp.wait_ge(s_pick, 1)
            _, chosen = nc.values_load_multi_w_load_instructions(small[0:1, 64:66].bitcast(I32), engines=(mybir.EngineType.SP,),
                                                                 min_val=0, max_val=NE - 1)
            for k, v in enumerate(chosen):
                sp.dma_start(fw1_in[:, k * 1024:(k + 1) * 1024].rearrange("p (c f) -> p c f", c=DC),
                             fw1[bass.ds(v, 1), :, :].rearrange("o (c p) f -> p (o c) f", p=P)).then_inc(s_fw1, 16)
                sp.dma_start(small[:, 80 + 4 * k:84 + 4 * k], fb1[bass.ds(v, 1), :, :].rearrange("o p c -> p (o c)")).then_inc(s_fw1, 16)
            for k, v in enumerate(chosen):
                sp.dma_start(fw2_in[:, k * 1024:(k + 1) * 1024].rearrange("p (c f) -> p c f", c=F // P),
                             fw2[bass.ds(v, 1), :, :].rearrange("o (c p) f -> p (o c) f", p=P)).then_inc(s_fw2, 16)
                sp.dma_start(b2two[:, k * D:(k + 1) * D], fb2[bass.ds(v, 1), :].to_broadcast([P, D])).then_inc(s_fw2, 16)
            with sp.Fori(0, FN_GROUPS) as g:
                sp.wait_ge(s_out, g + 1)
                sp.dma_start(out[bass.ds(g * 4 * P, 4 * P), :].rearrange("(t p) d -> p t d", p=P),
                             tile(xn, g * 4, 4).rearrange("p (t d) -> p t d", d=D)).then_inc(s_fdma, 16)
            sp.wait_ge(s_out, FN_GROUPS + 1)
            sp.dma_start(out[LAST * P:LAST * P + P, :], xn[:, LAST * D:LAST * D + D]).then_inc(s_fdma, 16)
            sp.wait_ge(s_fdma, 16 * (FN_GROUPS + 1))

        @block.gpsimd
        def _(pool):
            ch = Chain(pool, s_pre)
            pool.memset(small[:, :], 0.0).then_inc(s_const, 1)
            pool.wait_ge(s_const, 1)
            pool.iota(iota_b, [[1, NB]], base=0, channel_multiplier=0, allow_small_or_imprecise_dtypes=True).then_inc(s_const, 1)
            pool.memset(ones[:, :], 1.0).then_inc(s_const, 1)
            pool.memset(ones_b[:, :], 1.0).then_inc(s_const, 1)
            pool.iota(iota_p[:, :], [[1, P]], base=0, channel_multiplier=0, allow_small_or_imprecise_dtypes=True).then_inc(s_const, 1)
            ch.link(pool.memset(tri, 1.0))
            ch.link(pool.memset(ident[:, :], 0.0))
            ch.link(pool.memset(valid[:, :], 1.0))
            ch.link(pool.memset(r_keep, 1.0))
            pool.memset(r_keep.rearrange("p (b w) -> p b w", b=NB)[:, :, 0], 0.0).then_inc(s_keep, 1)
            pool.affine_select(out=tri, in_=tri, compare_op=ALU.is_gt, fill=0.0, base=0,
                               pattern=[[1, P]], channel_multiplier=-1).then_inc(s_const, 1)
            pool.affine_select(out=ident[:, :], in_=ident[:, :], compare_op=ALU.not_equal, fill=1.0, base=0,
                               pattern=[[-1, P]], channel_multiplier=1).then_inc(s_const, 1)
            pool.affine_select(out=valid[:, :], in_=valid[:, :], compare_op=ALU.is_ge, fill=0.0, base=N - LAST * P - 1,
                               pattern=[[0, 1]], channel_multiplier=-1).then_inc(s_const, 1)
            pool.memset(eps_c[:, :], EPS).then_inc(s_const, 1)
            ch.link(pool.iota(edst[:, :], [[0, TW // 48], [1, 48]], base=0, channel_multiplier=48))
            ch.link(pool.tensor_scalar(edst[:, :], edst[:, :], 256.0, 128.0, op0=ALU.mult, op1=ALU.add))
            pool.dma_start(sorted_edges.rearrange("(p c) o -> p (c o)", p=P), edst[:, :]).then_inc(s_tabinit, 16)
            pool.iota(e_cmp, [[1, TW]], base=0, channel_multiplier=0, allow_small_or_imprecise_dtypes=True).then_inc(s_ci, 1)
            pool.wait_ge(s_tabinit, 16)

            def scatters(i, v):
                for b in range(2):
                    col = (i * 2 + b) * SB
                    if v:
                        pool.wait_ge(s_scat[b], i * (SB * 16))
                        pool.nop(nofuse=True)
                    pool.tensor_copy(edge_ring[:, b, :, :], e_out[:, :, bass.ds(col, SB)]).then_inc(s_sidx, 1)
                    pool.wait_ge(s_sidx, i * 2 + b + 1)
                    pool.nop(nofuse=True)
                    for k in range(SB):
                        pool.indirect_dma_start(sorted_edges, bass.IndirectOffsetOnAxis(ap=idx_ring[:, b, k:k + 1], axis=0),
                                                val_ring[:, b, k:k + 1], None).then_inc(s_scat[b], 16)
            done = 0
            for n, cols in enumerate(SEGS):
                pool.wait_ge(s_rank, n + 1)
                if n == 0:
                    scatters(0, False)
                more = done + cols // (2 * SB)
                if more > max(1, done):
                    with pool.Fori(max(1, done), more) as i:
                        scatters(i, True)
                done = more

            for l in range(2):
                tab_written(pool, l)

                def gathers(i, b, count):
                    pool.wait_ge(s_gidx[l], i * 2 + b + 1)
                    pool.nop(nofuse=True)
                    for k in range(count):
                        pool.indirect_dma_start(ring[:, b, k, 0:2 * D], None, table[l],
                                                bass.IndirectOffsetOnAxis(ap=idx_ring[:, b, k:k + 1], axis=0)).then_inc(s_gath[l][b], 16)
                rounds = NCH // (2 * GB)
                with pool.Fori(0, rounds - 1) as i:
                    for b in range(2):
                        gathers(i, b, GB)
                gathers(rounds - 1, 0, GB)
                gathers(rounds - 1, 1, GB - (NCH - USED))
                if l == 0:
                    first = NP // 2
                    pool.wait_ge(s_z[0], first)
                    pool.memset(agg[:, 0:2 * first * AW], 0.0).then_inc(s_zero, 1)
                    pool.wait_ge(s_z[0], NP)
                    pool.memset(agg[:, 2 * first * AW:], 0.0).then_inc(s_zero, 1)
                with pool.Fori(0, NP) as p:
                    pool.wait_ge(s_nr[l], p + 1)
                    pool.nop(nofuse=True)
                    pool.tensor_tensor(two(tile(xn, p * 2, 2)), two(tile(xn, p * 2, 2)), both(gvec[l][1]),
                                       op=ALU.add).then_inc(s_gb[l], 1)
            def xf_stage(p, b):
                if b % 2 == 1:
                    pool.wait_ge(s_xf, p + 1)
                    if not isinstance(p, int) or p >= 4:
                        pool.wait_ge(s_ft, p - 3)
                    pool.nop(nofuse=True)
                    pool.tensor_copy(xf_stages[b], tile(xn, p * 2, 2)).then_inc(s_xc[1], 2)
            quads(pool, xf_stage)
            pool.wait_ge(s_fvec, 32)
            pool.wait_ge(s_xf, NP)
            pool.wait_ge(s_xc[0], NP + 1)
            with pool.Fori(0, NP) as p:
                pool.tensor_tensor(two(tile(xs, p * 2, 2)), two(tile(xs, p * 2, 2)), both(beb), op=ALU.add).then_inc(s_resb, 1)
            pool.wait_ge(s_b2, 1)
            with pool.Fori(0, NP) as p:
                pool.tensor_tensor(two(tile(xn, p * 2, 2)), two(tile(xn, p * 2, 2)), both(b2row), op=ALU.add).then_inc(s_xfb, 1)

        @block.scalar
        def _(act):
            ch = Chain(act, s_act)
            act.wait_ge(s_const, 9)
            act.wait_ge(s_cin, 1)
            def signs(i):
                for k in range(5):
                    b = i * 5 + k + HB
                    act.activation(c_sign[k], e_blk, ACT.Sign, bias=nhalf[:, bass.ds(b, 1)],
                                   accum_out=small[:, bass.ds(b + 200, 1)]).then_inc(s_sgn, 1)
            signs(0)
            with act.Fori(1, (NB - HB) // 5) as i:
                act.wait_ge(s_sgn, i * 5)
                act.nop(nofuse=True)
                signs(i)
            act.wait_ge(s_sq1, 1)
            act.activation(rstd[:, :], var_all, ACT.Sqrt, bias=eps_c[:, :]).then_inc(s_rs1, 1)

            def table_high(l, p, b):
                if not isinstance(p, int) or p >= BUFS[l]:
                    act.wait_ge(s_tab[l][b], (p - b) * (16 // BUFS[l]))
                    act.nop(nofuse=True)
                act.activation(split(b)[:, :, 0, :], two(tile(xn, p * 2, 2)), ACT.Copy,
                               scale=scale_c[:, l:l + 1]).then_inc(s_hi[l], 1)

            def first_high(p, b):
                act.wait_ge(s_nrm, p + 1)
                act.nop(nofuse=True)
                table_high(0, p, b)
            act.wait_ge(s_sc, 1)
            pairs(act, first_high)
            with act.Fori(0, NT) as t:
                act.activation(stage[0][:, 0:D], tile(xn, t), ACT.Copy).then_inc(s_mst, 1)
                act.wait_ge(s_mtp, t + 1)
                act.nop(nofuse=True)
                act.activation(xT[:, 0, :], bank[4][:, 0:D], ACT.Copy).then_inc(s_mxT, 1)
                act.wait_ge(s_kvp, t + 1)
                act.nop(nofuse=True)
                act.activation(kv[:, 0:512], bank[0][:, :], ACT.Copy)
                act.activation(kv[:, 512:1024], bank[1][:, :], ACT.Copy).then_inc(s_kvc, 1)
                act.wait_ge(s_kvc, t + 1)
                act.nop(nofuse=True)
                act.activation(kv_sq, kv, ACT.Square).then_inc(s_kvq, 1)
                act.wait_ge(s_kvr, t + 1)
                act.nop(nofuse=True)
                act.activation(small[:, 24:32], small[:, 16:24], ACT.Sqrt).then_inc(s_kvs, 1)
            for pr in range(PAIRS):
                act.wait_ge(s_mp, pr + 1)
                act.activation(m_s[:, pr * D:(pr + 1) * D], bank[pr % 2][:, 0:D], ACT.Copy).then_inc(s_mc, 1)
            for c in range(DC):
                act.wait_ge(s_gp, c + 1)
                act.activation(g_s[:, c * D:(c + 1) * D], bank[2 + c][:, 0:D], ACT.Copy, scale=1.0 / N).then_inc(s_gc, 1)
            def mixout(p, b):
                act.activation(stage[0], tile(xn, p * 2, 2), ACT.Copy).then_inc(s_ost, 1)
                act.wait_ge(s_otp, p + 1)
                act.nop(nofuse=True)
                act.activation(xTp[b], bank[4 + b][:, :], ACT.Copy).then_inc(s_oxT, 1)
            pairs(act, mixout)

            for l in range(2):
                with act.Fori(0, NCH // (2 * GB)) as i:
                    for b in range(2):
                        act.wait_ge(s_chunk[l], (i * 2 + b + 1) * GB)
                        act.nop(nofuse=True)
                        act.activation(idx_ring[:, b, 0:GB], edst[:, bass.ds((i * 2 + b) * GB, GB)], ACT.Copy).then_inc(s_gidx[l], 1)

                def zT(p, b):
                    act.wait_ge(s_zt[l], p + 1)
                    if not isinstance(p, int) or p >= 2:
                        act.wait_ge(s_h[l], p - 1)
                    act.nop(nofuse=True)
                    act.activation(xTs[b][:, 0, :], bank[4 + b][:, :], ACT.Copy, scale=zsc[:, l:l + 1]).then_inc(s_zc[l], 1)
                    if not isinstance(p, int) or p >= 1:
                        h_rows(p - 1, 1 - b)

                def h_rows(p, b):
                    act.wait_ge(s_h[l], p + 1)
                    act.nop(nofuse=True)
                    act.activation(tile(xn, p * 2, 2), bank[6 + b][:, :], ACT.Copy, scale=fsc[:, 12 + l:13 + l]).then_inc(s_hc[l], 1)
                pairs(act, zT)
                h_rows(NP - 1, (NP - 1) % 2)
                act.wait_ge(s_var[l], 1)
                act.activation(rstd[:, :], var_all, ACT.Sqrt, bias=eps_c[:, :]).then_inc(s_std[l], 1)
                act.activation(small[:, 316:317], small[:, 317:318], ACT.Silu)

                def silu(p, b):
                    act.wait_ge(s_gb[l], p + 1)
                    act.nop(nofuse=True)
                    act.activation(tile(xn, p * 2, 2), tile(xn, p * 2, 2), ACT.Silu).then_inc(s_y[l], 1)
                    if l == 0:
                        act.wait_ge(s_y[0], p + 1)
                        act.nop(nofuse=True)
                        table_high(1, p, b)
                act.wait_ge(s_sc, 2)
                (quads if l == 0 else pairs)(act, silu)
            act.wait_ge(s_var[2], 1)
            act.activation(rstd[:, :], var_all, ACT.Sqrt, bias=eps_c[:, :]).then_inc(s_std[2], 1)

            def xf_stage(p, b):
                if not isinstance(p, int) or p >= 4:
                    act.wait_ge(s_ft, p - 3)
                    act.nop(nofuse=True)
                for q in range(2):
                    t = p * 2 + q
                    ins = act.activation(xf_stages[b][:, q * D:(q + 1) * D], tile(xs, t), ACT.Identity,
                                         bias=nmr[:, bass.ds(t, 1)], scale=rstd[:, bass.ds(t, 1)])
                ins.then_inc(s_xc[0], 2)

            def xfT(p, b):
                act.wait_ge(s_ft, p + 1)
                act.nop(nofuse=True)
                act.activation(xfp[:, bass.ds(p * 2, 2), 0:D], two(bank[4 + b][:, :]), ACT.Copy, scale=X_SCALE).then_inc(s_fc, 1)
                if b % 2 == 0 and (not isinstance(p, int) or p + 4 < NP):
                    xf_stage(p + 4, b)
            act.wait_ge(s_nmr, 1)
            xf_stage(0, 0)
            xf_stage(2, 2)
            quads(act, xfT)
            act.activation(small[:, 316:317], small[:, 317:318], ACT.Exp)
            for n in range(3):
                act.wait_ge(s_exin, n + 1)
                act.nop(nofuse=True)
                act.activation(small[:, 8:16], small[:, 0:8], ACT.Exp).then_inc(s_ex, 1)
            act.wait_ge(s_fw1, 64)
            for k in range(2):
                act.activation(w1p[:, 0, k * 1024:(k + 1) * 1024], fw1_in[:, k * 1024:(k + 1) * 1024], ACT.Copy,
                               scale=fsc[:, 0:1]).then_inc(s_w1h, 1)
            for k in range(2):
                act.wait_ge(s_w2t, k + 1)
                act.activation(w2p[:, 0, k * 1024:(k + 1) * 1024], fw2_in[:, k * 1024:(k + 1) * 1024], ACT.Copy).then_inc(s_w2h, 1)

            act.activation(small[:, 316:317], small[:, 317:318], ACT.Gelu)

            def gelus(g, nt, before):
                w = nt * P
                for j in range(FJ):
                    n = g * FJ + j
                    act.wait_ge(s_up, n + 1)
                    if not isinstance(g, int) or n >= 2:
                        act.wait_ge(s_hlo, n - 1)
                    act.nop(nofuse=True)
                    act.activation(hid[j % 2][:, 0:w], bank[4 + j % 4][:, 0:w], ACT.Gelu,
                                   bias=small[:, 80 + j:81 + j], scale=fsc[:, 10:11]).then_inc(s_gelu, 1)
                    act.wait_ge(s_gelu, n + 1)
                    if j == 3 and (not isinstance(g, int) or g > 0):
                        act.wait_ge(s_outp, g * 4)
                    elif not isinstance(g, int) or n >= 4:
                        act.wait_ge(s_down, g * (FJ - 1) + (j - 3 if j > 3 else j - 2))
                    act.nop(nofuse=True)
                    act.activation(hp[:, j % 4, 0, 0:w], hid[j % 2][:, 0:w], ACT.Copy, scale=fsc[:, 2:3]).then_inc(s_hhi, 1)
                    if j == 4 and before:
                        std(g - 1)

            def std(g):
                act.wait_ge(s_fvar, g + 1)
                act.nop(nofuse=True)
                act.activation(small[:, 24:28], small[:, 20:24], ACT.Sqrt, bias=eps_c[:, :]).then_inc(s_fstd, 1)
            gelus(0, 4, False)
            with act.Fori(1, FN_GROUPS) as g:
                gelus(g, 4, True)
            gelus(FN_GROUPS, 1, True)
            std(FN_GROUPS)

        @block.tensor
        def _(pe):
            mm = pe.matmul
            PARTS = ((0, 0), (0, 1), (1, 0))
            pe.wait_ge(s_const, 9)
            pe.wait_ge(s_cnt, 1)
            mm(bank[0][:, 0:NB], tri, cnt, start=True, stop=True)
            mm(bank[1][:, 0:NB], ones[:, :], cnt, start=True, stop=True)
            mm(bank[2][0:NB, 0:1], cnt, ones[:, 0:1], start=True, stop=True).then_inc(s_tot, 1)
            pe.wait_ge(s_tot2, 1)
            mm(bank[3][0:BLK, 0:1], tri[0:BLK, 0:BLK], small[0:BLK, 301:302], start=True, stop=False)
            mm(bank[3][0:BLK, 0:1], ident[0:BLK, 0:BLK], small[0:BLK, 301:302], start=False, stop=True).then_inc(s_endc, 1)
            pe.wait_ge(s_blkc, 1)
            for n in range(4):
                w = TW // 4
                m = mm(bank[n][0:1, 0:w], ones[0:BLK, 0:1], e_cmp[:, n * w:(n + 1) * w], start=True, stop=True)
            m.then_inc(s_blkm, 1)

            pe.wait_ge(s_wc, 2)
            pe.wait_ge(s_blkp, 1)
            mm(bank[7][:, :], zeros[:, 0:P], zeros, start=True, stop=False)
            with pe.Fori(0, NT) as t:
                pe.wait_ge(s_mst, t + 1)
                for c in range(DC):
                    m = pe.transpose(bank[4][:, c * P:(c + 1) * P], stage[0][:, c * P:(c + 1) * P], ident[:, :])
                m.then_inc(s_mtp, 1)
                pe.wait_ge(s_mxT, t + 1)
                for h in range(2):
                    for c in range(DC):
                        m = mm(bank[h][:, :], xT[:, 0, c * P:(c + 1) * P],
                               wkv_s[:, c * 1024 + h * 512:c * 1024 + (h + 1) * 512], start=c == 0, stop=c == DC - 1)
                m.then_inc(s_kvp, 1)
                pe.wait_ge(s_kn, t + 1)
                for pr in range(PAIRS):
                    m = mm(bank[7][:, pr * P:(pr + 1) * P], kv[:, 512 + pr * P:512 + (pr + 1) * P],
                           kv[:, pr * P:(pr + 1) * P], start=False, stop=False, skip_group_check=True)
                m.then_inc(s_dots, 1)
            mm(bank[7][:, :], zeros[:, 0:P], zeros, start=False, stop=True).then_inc(s_dots, 1)
            pe.wait_ge(s_dd, 1)
            for pr in range(PAIRS):
                if pr >= 2:
                    pe.wait_ge(s_mc, pr - 1)
                mm(bank[pr % 2][:, 0:D], dots_s[:, pr * P:(pr + 1) * P], wo_s[:, pr * D:(pr + 1) * D],
                   start=True, stop=True).then_inc(s_mp, 1)
            pe.wait_ge(s_mc, PAIRS)
            for c in range(DC):
                for pr in range(PAIRS):
                    m = mm(bank[2 + c][:, 0:D], wq_s[:, pr * D + c * P:pr * D + (c + 1) * P], m_s[:, pr * D:(pr + 1) * D],
                           start=pr == 0, stop=pr == PAIRS - 1)
                m.then_inc(s_gp, 1)
            pe.wait_ge(s_gc, DC)
            pe.wait_ge(s_w, 16 * 11)
            def transposes(stage_b, out_bank):
                for q in range(2 * DC):
                    m = pe.transpose(out_bank[:, q * P:(q + 1) * P], stage_b[:, q * P:(q + 1) * P], ident[:, :])
                return m

            def mixout(p, b):
                pe.wait_ge(s_ost, p + 1)
                transposes(stage[0], bank[4 + b]).then_inc(s_otp, 1)
                pe.wait_ge(s_oxT, p + 1)
                if not isinstance(p, int) or p >= 2:
                    pe.wait_ge(s_oa, p - 1)
                for q in range(2):
                    for c in range(DC):
                        mm(bank[b][:, q * D:(q + 1) * D], xTp[b][:, (q * DC + c) * P:(q * DC + c + 1) * P],
                           g_s[:, c * D:(c + 1) * D], start=c == 0, stop=False)
                    m = mm(bank[b][:, q * D:(q + 1) * D], ones[0:1, :], borow, start=False, stop=True)
                m.then_inc(s_op, 1)
            pairs(pe, mixout)

            pe.wait_ge(s_wred, 5)
            pe.wait_ge(s_oa, NP)
            for n in range(5):
                m = mm(bank[6 + n // 3][0:1, n % 3 * P:(n % 3 + 1) * P], small[:, 44 + n:45 + n], ident[:, :], start=True, stop=True)
            m.then_inc(s_rowmax, 1)
            pe.wait_ge(s_scrow, 1)
            mm(bank[5][:, 0:10], ones[0:1, :], fsc[0:1, 0:10], start=True, stop=True).then_inc(s_scall, 1)

            for l in range(2):
                if l == 0:
                    pe.wait_ge(s_blkp, 2)
                pe.sem_inc(s_chunk[l], 2 * GB)
                if l == 0:
                    pe.wait_ge(s_oa, NP)

                def chunks(i, skip):
                    for b in range(2):
                        pe.wait_ge(s_gath[l][b], i * (GB * 16) + (GB - skip * b) * 16)
                        pe.wait_ge(s_sel[l][b], i + 1)
                        for k in range(GB - skip * b):
                            n = (i * 2 + b) * GB + k
                            pe.wait_ge(s_added[l], n + 1)
                            mm(bank[k % 4][:, 0:AW], sel[:, b, k, :], ring[:, b, k, D:2 * D + 1], start=True, stop=False)
                            m = mm(bank[k % 4][:, 0:D], sel[:, b, k, :], ring[:, b, k, 0:D], start=False, stop=True)
                            m.then_inc(s_chunk[l], 1)
                with pe.Fori(0, NCH // (2 * GB) - 1) as i:
                    chunks(i, 0)
                chunks(NCH // (2 * GB) - 1, NCH - USED)
                def z_transposes(p, b):
                    pe.wait_ge(s_z[l], p + 1)
                    if not isinstance(p, int) or p >= 2:
                        pe.wait_ge(s_zl[l], p - 1)
                    transposes(stage[b], bank[4 + b]).then_inc(s_zt[l], 1)

                def product(p, b):
                    if not isinstance(p, int) or p + 1 < NP:
                        z_transposes(p + 1, 1 - b)
                    pe.wait_ge(s_zl[l], p + 1)
                    if not isinstance(p, int) or p >= 2:
                        pe.wait_ge(s_hc[l], p - 1)
                    mm(bank[6 + b][:, :], ones_b[0:3, :], bparts[l][0:3, :], start=True, stop=False)
                    for q in range(2):
                        for c in range(DC):
                            for x, w in PARTS:
                                m = mm(bank[6 + b][:, q * D:(q + 1) * D], xTs[b][:, x, (q * DC + c) * P:(q * DC + c + 1) * P],
                                       gwp[l][:, w, c * D:(c + 1) * D], start=False, stop=q == 1 and c == DC - 1 and x == 1)
                    m.then_inc(s_h[l], 1)
                z_transposes(0, 0)
                pairs(pe, product)

            def xf_pair(p, b):
                pe.wait_ge(s_xc[b % 2], p - b % 2 + 2)
                last = isinstance(p, int) and p == NP - 1
                for q in range(1 if last else 2):
                    m = mm(bank[0][0:1, 0:D], valid[:, :] if last else ones[:, 0:1], xf_stages[b][:, q * D:(q + 1) * D],
                           start=isinstance(p, int) and p == 0 and q == 0, stop=last, skip_group_check=True)
                if last:
                    m.then_inc(s_mean, 1)
                if not isinstance(p, int) or p >= 4:
                    pe.wait_ge(s_fl, p - 3)
                transposes(xf_stages[b], bank[4 + b]).then_inc(s_ft, 1)
            quads(pe, xf_pair)
            pe.wait_ge(s_mrow, 1)
            for c in range(DC):
                m = mm(bank[1 + 2 * c][:, 0:1], mean_row[:, c * P:(c + 1) * P], ones[0:1, 0:1], start=True, stop=True)
            m.then_inc(s_mcol, 1)
            pe.wait_ge(s_mb, 1)
            for c in range(DC):
                mm(bank[2][:, 0:NE], mean_s[:, c * P:(c + 1) * P], wr_s[:, c * NE:(c + 1) * NE], start=c == 0, stop=False)
            mm(bank[2][:, 0:NE], ones[0:1, :], br_s[:, :], start=False, stop=True).then_inc(s_lg, 1)
            pe.wait_ge(s_w1l, 2)
            pe.wait_ge(s_fl, NP)

            def ups(g, j, nt):
                k, jj = j // 4, j % 4
                n = g * FJ + j
                if not isinstance(g, int) or n >= 4:
                    pe.wait_ge(s_gelu, n - 3)
                for c in range(DC):
                    w = k * 1024 + c * 512 + jj * P
                    for a, b in PARTS:
                        m = mm(bank[4 + j % 4][:, 0:nt * P], w1p[:, a, w:w + P],
                               xfp[:, bass.ds(g * 4, nt), b * D + c * P:b * D + (c + 1) * P],
                               start=c == a == b == 0, stop=c == DC - 1 and a == 1)
                m.then_inc(s_up, 1)

            def downs(g, j, nt):
                pe.wait_ge(s_hlo, g * FJ + j + 1)
                if isinstance(g, int) and g == 0 and j % 4 == 0:
                    pe.wait_ge(s_w2l, j // 4 + 1)
                for q in range(nt):
                    if j == 0 and (not isinstance(g, int) or g > 0):
                        pe.wait_ge(s_fo, g * 4 + q - 3)
                    for a, b in PARTS:
                        m = mm(bank[q][:, 0:D], hp[:, j % 4, a, q * P:(q + 1) * P], w2p[:, b, j * D:(j + 1) * D],
                               start=j == a == b == 0, stop=j == FJ - 1 and a == 1)
                    if j == FJ - 1:
                        m.then_inc(s_outp, 1)
                if j < FJ - 1:
                    m.then_inc(s_down, 1)

            def experts(g, nt, after):
                for j in range(FJ):
                    if j + 2 < FJ:
                        ups(g, j + 2, nt)
                    elif after:
                        ups(g + 1, j + 2 - FJ, after)
                    downs(g, j, nt)
            ups(0, 0, 4)
            ups(0, 1, 4)
            experts(0, 4, 4)
            with pe.Fori(1, FN_GROUPS - 1) as g:
                experts(g, 4, 4)
            experts(FN_GROUPS - 1, 4, 1)
            experts(FN_GROUPS, 1, 0)

        @block.vector
        def _(dve):
            ch = Chain(dve, s_dve)
            link = ch.link
            dve.wait_ge(s_const, 9)
            dve.wait_ge(s_edges, 32)
            link(dve.tensor_scalar(e_addr, e_src, 7, None, op0=ALU.arith_shift_right))
            link(dve.tensor_copy(e_blk, e_addr))
            link(dve.tensor_scalar(nhalf, iota_b, -1.0, 0.5, op0=ALU.mult, op1=ALU.add))
            dve.sem_inc(s_cin, 1)

            def count(i):
                for k in range(5):
                    b = i * 5 + k
                    ins = dve.tensor_scalar(c_mask[k], e_blk, iota_b[:, bass.ds(b, 1)], 0.0, op0=ALU.is_equal, op1=ALU.add,
                                            accum_out=cnt[:, bass.ds(b, 1)])
                link(ins)
            ch.loop(HB // 5, 1, count)
            link(dve.memset(small[:, NB + 200:NB + 201], -float(EC)))
            dve.wait_ge(s_sgn, NB - HB)
            link(dve.tensor_tensor(cnt[:, HB:NB], small[:, HB + 200:NB + 200], small[:, HB + 201:NB + 201], op=ALU.subtract))
            dve.tensor_scalar(cnt[:, HB:NB], cnt[:, HB:NB], 0.5, None, op0=ALU.mult).then_inc(s_cnt, 1)
            link(dve.tensor_scalar(e_src, e_src, P - 1, None, op0=ALU.bitwise_and))
            link(dve.scalar_tensor_tensor(e_val, e_dst, 256.0, e_src, op0=ALU.mult, op1=ALU.add))
            link(dve.memset(e_zero, 0.0))
            dve.wait_ge(s_tot, 1)
            link(dve.tensor_scalar(tmpi, bank[1][:, 0:NB], float(P - 1), None, op0=ALU.add))
            link(dve.tensor_scalar(tmpi, tmpi, 7, None, op0=ALU.arith_shift_right))
            link(dve.tensor_copy(tmp, tmpi))
            link(dve.tensor_tensor_scan(cend, tmp, e_zero[:, 0:NB], 0.0, op0=ALU.add, op1=ALU.add))
            link(dve.tensor_sub(tmp, cend, tmp))
            link(dve.scalar_tensor_tensor(base, tmp, float(P), bank[0][:, 0:NB], op0=ALU.mult, op1=ALU.add))
            link(dve.tensor_scalar(r_mask[:, :, 0], base, -1.0, None, op0=ALU.add))
            link(dve.tensor_scalar(tmpi[0:NB, 0:1], bank[2][0:NB, 0:1], float(P - 1), None, op0=ALU.add))
            link(dve.tensor_scalar(tmpi[0:NB, 0:1], tmpi[0:NB, 0:1], 7, None, op0=ALU.arith_shift_right))
            dve.tensor_copy(small[0:NB, 301:302], tmpi[0:NB, 0:1]).then_inc(s_tot2, 1)

            def addresses(ip, scan):
                link(dve.tensor_scalar(scan.bitcast(I32), ip, 7, None, op0=ALU.arith_shift_right))
                link(dve.tensor_scalar(ip, ip, P - 1, None, op0=ALU.bitwise_and))
                return dve.scalar_tensor_tensor(ip, ip, float(TW), scan.bitcast(I32), op0=ALU.mult, op1=ALU.add)

            dve.wait_ge(s_keep, 1)

            def rank_all(n):
                link(dve.tensor_tensor(r_mask[:, :, 1:], e_blk[:, bass.ds(n * EW, EW)].unsqueeze(1).to_broadcast([P, NB, EW]),
                                       iota_b.unsqueeze(2).to_broadcast([P, NB, EW]), op=ALU.is_equal))
                link(dve.tensor_tensor_scan(r_scan.rearrange("p b w -> p (b w)"), r_keep, r_mask.rearrange("p b w -> p (b w)"),
                                            0.0, op0=ALU.mult, op1=ALU.add))
                dve.tensor_copy(r_mask[:, :, 0], r_scan[:, :, EW])
                link(dve.tensor_tensor(r_pos, r_scan[:, :, 1:], r_mask[:, :, 1:], op=ALU.mult))
                ip = e_addr[:, bass.ds(n * EW, EW)]
                pos = e_pos[:, bass.ds(n * EW, EW)]
                link(dve.tensor_reduce(pos, r_pos.rearrange("p b w -> p w b"), axis=AX.X, op=ALU.add))
                link(dve.tensor_copy(ip, pos))
                addresses(ip, e_scan[:, 0:EW]).then_inc(s_rank, 1)
            ch.loop(ES, 7, rank_all)
            link(dve.tensor_copy(base, r_mask[:, :, 0]))

            for n, width in list(enumerate(SEGS))[ES:]:
                cols = slice(sum(SEGS[:n]), sum(SEGS[:n + 1]))
                scan = e_scan[:, 0:width]
                mask = e_mask[:, 0:width]

                def rank(i):
                    for k in range(5):
                        b = i * 5 + k
                        link(dve.tensor_scalar(mask, e_blk[:, cols], iota_b[:, bass.ds(b, 1)], None, op0=ALU.is_equal))
                        link(dve.tensor_tensor_scan(scan, mask, e_zero[:, 0:width], base[:, bass.ds(b, 1)], op0=ALU.add, op1=ALU.add))
                        dve.tensor_copy(base[:, bass.ds(b, 1)], scan[:, width - 1:width])
                        link(dve.copy_predicated(e_pos[:, cols], mask.bitcast(U16), scan))
                ch.loop(NB // 5, 15, rank)
                link(dve.tensor_copy(e_addr[:, cols], e_pos[:, cols]))
                addresses(e_addr[:, cols], scan).then_inc(s_rank, 1)
                dve.wait_ge(s_rank, n + 1)

            dve.wait_ge(s_endc, 1)
            link(dve.tensor_copy(small[0:BLK, 302:303], bank[3][0:BLK, 0:1]))
            dve.wait_ge(s_ci, 1)
            dve.tensor_scalar(e_cmp, e_cmp, small[0:BLK, 302:303], None, op0=ALU.is_ge).then_inc(s_blkc, 1)
            dve.wait_ge(s_blkm, 1)
            for n in range(4):
                w = TW // 4
                ins = dve.tensor_copy(blk_row[0:1, n * w:(n + 1) * w], bank[n][0:1, 0:w])
            ins.then_inc(s_blkp, 1)

            def stat_tile(buf, t):
                return dve.bn_stats(stats[:, bass.ds(t * 6, 6)], tile(buf, t))

            def variances(ready):
                sv = stats[:, :].rearrange("p (t c) -> p t c", c=6)
                link(dve.tensor_tensor(mean_all, sv[:, :, 1], sv[:, :, 4], op=ALU.add))
                link(dve.tensor_scalar(mean_all, mean_all, 0.5, None, op0=ALU.mult))
                link(dve.tensor_tensor(nmr[:, :], sv[:, :, 1], sv[:, :, 4], op=ALU.subtract))
                link(dve.tensor_tensor(nmr[:, :], nmr[:, :], nmr[:, :], op=ALU.mult))
                link(dve.tensor_tensor(var_all, sv[:, :, 2], sv[:, :, 5], op=ALU.add))
                link(dve.tensor_scalar(nmr[:, :], nmr[:, :], 0.25, None, op0=ALU.mult))
                dve.scalar_tensor_tensor(var_all, var_all, 1.0 / D, nmr[:, :], op0=ALU.mult, op1=ALU.add).then_inc(ready, 1)

            def finish_stats(std, value, signal=True):
                dve.wait_ge(std, value)
                link(dve.reciprocal(rstd[:, :], rstd[:, :]))
                ins = dve.scalar_tensor_tensor(nmr[:, :], mean_all, -1.0, rstd[:, :], op0=ALU.mult, op1=ALU.mult)
                if signal:
                    ins.then_inc(s_nmr, 1)
                else:
                    link(ins)

            for n in range(5):
                dve.wait_ge(s_x[n], 16)
            ch.loop(NT, 1, lambda t: link(stat_tile(xs, t)))
            variances(s_sq1)
            finish_stats(s_rs1, 1, False)
            link(dve.memset(scale_c[:, 0:1], X_SCALE))
            link(dve.memset(unscale_c[:, 0:1], 1.0 / X_SCALE))
            dve.sem_inc(s_sc, 1)

            def table_low(l, p, b):
                dve.wait_ge(s_hi[l], p + 1)
                dve.nop(nofuse=True)
                dve.scalar_tensor_tensor(split(b)[:, :, 1, :], two(tile(xn, p * 2, 2)), scale_c[:, l:l + 1],
                                         split(b)[:, :, 0, :], op0=ALU.mult, op1=ALU.subtract).then_inc(s_lo[l], 1)

            def norm_pair(p):
                for q in range(2):
                    t = p * 2 + q
                    ins = dve.tensor_scalar(tile(xn, t), tile(xs, t), rstd[:, bass.ds(t, 1)], nmr[:, bass.ds(t, 1)],
                                            op0=ALU.mult, op1=ALU.add)
                return ins

            def first(p, b):
                if isinstance(p, int) and p == 0:
                    norm_pair(0).then_inc(s_nrm, 1)
                if not isinstance(p, int) or p + 1 < NP:
                    norm_pair(p + 1).then_inc(s_nrm, 1)
                table_low(0, p, b)
            pairs(dve, first)

            dve.wait_ge(s_wmix, 48)
            wg = wkv_s.rearrange("p (g e) -> p g e", e=DH)
            link(dve.tensor_reduce(small[:, 0:32], wg, axis=AX.X, op=ALU.add))
            link(dve.tensor_scalar(small[:, 0:32], small[:, 0:32], -1.0 / DH, None, op0=ALU.mult))
            dve.tensor_tensor(wg, wg, small[:, 0:32].unsqueeze(2).to_broadcast([P, 32, DH]), op=ALU.add).then_inc(s_wc, 1)
            dve.memset(zeros, 0.0).then_inc(s_wc, 1)
            link(dve.memset(dots_s, 0.0))

            def kv_tile(t):
                dve.wait_ge(s_kvq, t + 1)
                dve.nop(nofuse=True)
                link(dve.tensor_reduce(small[:, 0:16], kv_sq.rearrange("p (g e) -> p g e", e=DH), axis=AX.X, op=ALU.add))
                link(dve.tensor_scalar(small[:, 0:16], small[:, 0:16], 1.0 / DH, EPS, op0=ALU.mult, op1=ALU.add))
                dve.tensor_tensor(small[:, 16:24], small[:, 0:8], small[:, 8:16], op=ALU.mult).then_inc(s_kvr, 1)
                dve.wait_ge(s_kvs, t + 1)
                dve.nop(nofuse=True)
                link(dve.reciprocal(small[:, 32:40], small[:, 24:32]))
                kg = kv[:, 0:512].rearrange("p (g e) -> p g e", e=DH)
                dve.tensor_tensor(kg, kg, small[:, 32:40].unsqueeze(2).to_broadcast([P, 8, DH]), op=ALU.mult).then_inc(s_kn, 1)
            ch.loop(NT, 3, kv_tile)
            dve.wait_ge(s_dots, NT + 1)
            for h in range(2):
                src_d = bank[7][h * DH:(h + 1) * DH, :].rearrange("p (q d) -> p q d", d=P)[:, :, h * DH:(h + 1) * DH]
                dst_d = dots_s[h * DH:(h + 1) * DH, :].rearrange("p (q d) -> p q d", d=P)[:, :, h * DH:(h + 1) * DH]
                ins = dve.tensor_copy(dst_d, src_d)
                if h == 0:
                    link(ins)
            ins.then_inc(s_dd, 1)
            with dve.Fori(0, NP // 2) as i:
                for b in range(2):
                    p = i * 2 + b
                    dve.wait_ge(s_op, p + 1)
                    dve.nop(nofuse=True)
                    dve.tensor_tensor(tile(xs, p * 2, 2), tile(xs, p * 2, 2), bank[b][:, :], op=ALU.add).then_inc(s_oa, 1)
            dve.wait_ge(s_op, NP)
            dve.tensor_tensor(tile(xs, NT - 2, 2), tile(xs, NT - 2, 2), bank[0][:, :], op=ALU.add).then_inc(s_oa, 1)
            dve.wait_ge(s_w, 16 * 11)
            for l in range(2):
                gwv = gw[l].rearrange("p (c e) -> p c e", c=DC)
                link(dve.tensor_reduce(small[:, 0:DC], gwv, axis=AX.X, op=ALU.add))
                link(dve.tensor_reduce(small[:, DC:DC + 1], brow[l], axis=AX.X, op=ALU.add))
                link(dve.tensor_scalar(small[:, 0:DC + 1], small[:, 0:DC + 1], -1.0 / D, None, op0=ALU.mult))
                link(dve.tensor_tensor(gwv, gwv, small[:, 0:DC].unsqueeze(2).to_broadcast([P, DC, D]), op=ALU.add))
                link(dve.tensor_scalar(brow[l], brow[l], small[:, DC:DC + 1], None, op0=ALU.add))
                link(dve.tensor_reduce(small[:, 47 + l:48 + l], gw[l], axis=AX.X, op=ALU.max, apply_absolute_value=True))
            link(dve.tensor_reduce(small[:, 40:41], gvec[0][0], axis=AX.X, op=ALU.max, apply_absolute_value=True))
            link(dve.tensor_reduce(small[:, 41:42], gvec[0][1], axis=AX.X, op=ALU.max, apply_absolute_value=True))
            link(dve.scalar_tensor_tensor(small[:, 40:41], small[:, 40:41], 16.0, small[:, 41:42], op0=ALU.mult, op1=ALU.add))
            link(dve.tensor_scalar(small[:, 40:41], small[:, 40:41], 2.0 ** -60, 2.0 ** 60, op0=ALU.max, op1=ALU.min))
            bits = small[:, 42:43].bitcast(I32)
            link(dve.tensor_scalar(bits, small[:, 40:41].bitcast(I32), 0x7F800000, None, op0=ALU.bitwise_and))
            link(dve.tensor_scalar(scale_c[:, 1:2].bitcast(I32), bits, -1.0, float(268 << 23), op0=ALU.mult, op1=ALU.add))
            link(dve.tensor_scalar(unscale_c[:, 1:2].bitcast(I32), bits, -float(14 << 23), None, op0=ALU.add))
            dve.sem_inc(s_sc, 1)
            for n in range(4):
                dve.wait_ge(s_wmax, 16 * (n + 1))
                dve.tensor_reduce(small[:, 304 + n:305 + n], fw_all, axis=AX.X, op=ALU.max, apply_absolute_value=True).then_inc(s_wred, 1)
            dve.wait_ge(s_wmax, 16 * 5)
            link(dve.tensor_reduce(small[:, 46:47], fw_all[:, 0:NE * F // P], axis=AX.X, op=ALU.max, apply_absolute_value=True))
            dve.wait_ge(s_wred, 4)
            dve.tensor_reduce(small[:, 44:46], small[:, 304:308].rearrange("p (n h) -> p n h", h=2), axis=AX.X,
                              op=ALU.max).then_inc(s_wred, 1)
            dve.wait_ge(s_rowmax, 1)
            mx = small[0:1, 308:313]
            for n, (row, count) in enumerate(((bank[6], 3), (bank[7], 2))):
                link(dve.tensor_reduce(mx[:, 3 * n:3 * n + count], row[0:1, 0:count * P].rearrange("o (n p) -> o n p", p=P),
                                       axis=AX.X, op=ALU.max))
            link(dve.scalar_tensor_tensor(mx[:, 2:3], mx[:, 0:1], 256.0, mx[:, 2:3], op0=ALU.mult, op1=ALU.add))
            link(dve.tensor_scalar(mx, mx, 2.0 ** -30, 2.0 ** 60, op0=ALU.max, op1=ALU.min))
            mxi = mx.bitcast(I32)
            link(dve.tensor_scalar(mxi, mxi, 0x7F800000, None, op0=ALU.bitwise_and))
            link(dve.tensor_scalar(fsc[0:1, 0:5].bitcast(I32), mxi, -1.0, float(268 << 23), op0=ALU.mult, op1=ALU.add))
            dve.tensor_scalar(fsc[0:1, 5:10].bitcast(I32), mxi, -float(14 << 23), None, op0=ALU.add).then_inc(s_scrow, 1)
            dve.wait_ge(s_scall, 1)
            link(dve.tensor_copy(fsc[:, 0:10], bank[5][:, 0:10]))
            link(dve.tensor_scalar(fsc[:, 10:11], fsc[:, 5:6], 1.0 / X_SCALE, None, op0=ALU.mult))
            link(dve.tensor_tensor(fsc[:, 11:12], fsc[:, 6:7], fsc[:, 7:8], op=ALU.mult))
            link(dve.tensor_scalar(zsc[:, :], scale_c[:, :], 0.5, None, op0=ALU.mult))
            link(dve.scalar_tensor_tensor(fsc[:, 12:14], unscale_c[:, :], 2.0, fsc[:, 8:10], op0=ALU.mult, op1=ALU.mult))
            link(dve.tensor_tensor(fsc[:, 14:16], zsc[:, :], fsc[:, 3:5], op=ALU.mult))
            part = [kv[:, n * P:(n + 1) * P].bitcast(BF16) for n in range(3)]
            gwt = kv[:, 512:1024].bitcast(F16).rearrange("p (h c) -> p h c", h=2)
            for l in range(2):
                link(dve.tensor_scalar(gwt[:, 0, :], gw[l], fsc[:, 3 + l:4 + l], None, op0=ALU.mult))
                link(dve.scalar_tensor_tensor(gwt[:, 1, :], gw[l], fsc[:, 3 + l:4 + l], gwt[:, 0, :], op0=ALU.mult, op1=ALU.subtract))
                link(dve.tensor_copy(gwp[l], gwt))
                link(dve.tensor_scalar(brow[l], brow[l], fsc[:, 14 + l:15 + l], None, op0=ALU.mult))
                for n in range(3):
                    link(dve.tensor_copy(part[n], brow[l]))
                    if n < 2:
                        link(dve.tensor_tensor(brow[l], brow[l], part[n], op=ALU.subtract))
                for n in reversed(range(3)):
                    link(dve.tensor_copy(bparts[l][0:n + 1, :].rearrange("p (t d) -> p t d", t=2),
                                         part[n][0:n + 1, :].unsqueeze(1).to_broadcast([n + 1, 2, D])))
            link(dve.memset(agg[:, EC:2 * EC], 0.0))
            link(dve.memset(agg[:, 3 * EC:], 0.0))
            dve.wait_ge(s_back, 16)
            link(dve.tensor_scalar(e_tmp, edst[:, :], 255, None, op0=ALU.bitwise_and))
            link(dve.tensor_scalar(edst[:, :], edst[:, :], 8, None, op0=ALU.arith_shift_right))
            link(dve.tensor_copy(esrc[:, :], e_tmp))
            link(dve.memset(ring[:, :, :, 2 * D:2 * D + 1], 1.0))
            dve.sem_inc(s_blkp, 1)

            for l in range(2):
                def selectors(i, b):
                    dve.wait_ge(s_chunk[l], (i * 2 + b + 1) * GB)
                    dve.nop(nofuse=True)
                    dve.tensor_tensor(sel[:, b, :, :], iota_p[:, :].unsqueeze(1).to_broadcast([P, GB, P]),
                                      esrc[:, bass.ds((i * 2 + b) * GB, GB)].unsqueeze(2).to_broadcast([P, GB, P]),
                                      op=ALU.is_equal).then_inc(s_sel[l][b], 1)
                tab_written(dve, l)
                for b in range(2):
                    selectors(0, b)
                if l == 0:
                    dve.memset(agg[:, 0:EC], 0.0)
                    link(dve.memset(agg[:, 2 * EC:3 * EC], 0.0))
                else:
                    dve.wait_ge(s_zero, 2)
                dve.sem_inc(s_added[l], 4)

                def adds(i, skip):
                    for b in range(2):
                        _, where = nc.values_load_multi_w_load_instructions(
                            blk_row[0:1, bass.ds((i * 2 + b) * GB, GB)], engines=(mybir.EngineType.DVE,), min_val=0, max_val=NT - 1)
                        for k in range(GB - skip * b):
                            n = (i * 2 + b) * GB + k
                            dve.wait_ge(s_chunk[l], n + 2 * GB + 1)
                            dve.wait_ge(s_added[l], n + 4)
                            dve.nop(nofuse=True)
                            part = agg[:, bass.ds(where[k] * AW, AW)]
                            dve.tensor_tensor(part, part, bank[k % 4][:, 0:AW], op=ALU.add).then_inc(s_added[l], 1)
                        if not skip:
                            selectors(i + 1, b)
                with dve.Fori(0, NCH // (2 * GB) - 1) as i:
                    adds(i, 0)
                adds(NCH // (2 * GB) - 1, NCH - USED)
                dve.wait_ge(s_added[l], USED + 4)
                u = small[:, 0:NT]
                link(dve.tensor_scalar(u, aggv[:, :, D], 1.0, None, op0=ALU.max))
                link(dve.reciprocal(u, u))
                link(dve.tensor_scalar(u, u, unscale_c[:, l:l + 1], None, op0=ALU.mult))

                def z_pair(p, b):
                    if not isinstance(p, int) or p >= 2:
                        dve.wait_ge(s_zt[l], p - 1)
                        dve.nop(nofuse=True)
                    for q in range(2):
                        t = p * 2 + q
                        ins = dve.scalar_tensor_tensor(stage[b][:, q * D:(q + 1) * D], agg[:, bass.ds(t * AW, D)],
                                                       small[:, bass.ds(t, 1)], tile(xn, t), op0=ALU.mult, op1=ALU.add)
                    ins.then_inc(s_z[l], 1)

                def h_pair(p, b):
                    dve.wait_ge(s_zc[l], p + 1)
                    dve.nop(nofuse=True)
                    dve.scalar_tensor_tensor(xTs[b][:, 1, :], bank[4 + b][:, :], zsc[:, l:l + 1], xTs[b][:, 0, :],
                                             op0=ALU.mult, op1=ALU.subtract).then_inc(s_zl[l], 1)
                    if not isinstance(p, int) or p + 2 < NP:
                        z_pair(p + 2, b)
                    if not isinstance(p, int) or p >= 1:
                        h_stats(p - 1)

                def h_stats(p):
                    dve.wait_ge(s_hc[l], p + 1)
                    dve.nop(nofuse=True)
                    for q in range(2):
                        stat_tile(xn, p * 2 + q).then_inc(s_st[l], 1)
                z_pair(0, 0)
                z_pair(1, 1)
                pairs(dve, h_pair)
                h_stats(NP - 1)
                dve.wait_ge(s_st[l], NT)
                variances(s_var[l])
                finish_stats(s_std[l], 1, False)
                if l == 0:
                    link(dve.memset(ring[:, :, :, 2 * D:2 * D + 1], 1.0))

                def scaled(p):
                    for q in range(2):
                        t = p * 2 + q
                        ins = dve.scalar_tensor_tensor(tile(xn, t), tile(xn, t), rstd[:, bass.ds(t, 1)], gvec[l][0],
                                                       op0=ALU.mult, op1=ALU.mult)
                    ins.then_inc(s_nr[l], 1)

                def emit(p, b):
                    if not isinstance(p, int) or p + 2 < NP:
                        scaled(p + 2)
                    if l == 0:
                        table_low(1, p, b)
                    else:
                        dve.wait_ge(s_y[1], p + 1)
                        dve.nop(nofuse=True)
                        dve.tensor_tensor(tile(xs, p * 2, 2), tile(xs, p * 2, 2), tile(xn, p * 2, 2), op=ALU.add).then_inc(s_res, 1)
                        if not isinstance(p, int) or p >= 1:
                            res_stats(p - 1)

                def res_stats(p):
                    dve.wait_ge(s_res, p + 1)
                    dve.nop(nofuse=True)
                    for q in range(2):
                        stat_tile(xs, p * 2 + q).then_inc(s_st[2], 1)
                scaled(0)
                scaled(1)
                (quads if l == 0 else pairs)(dve, emit)
                if l == 1:
                    res_stats(NP - 1)
            dve.wait_ge(s_st[2], NT)
            variances(s_var[2])
            finish_stats(s_std[2], 1)
            dve.wait_ge(s_nmr, 1)

            def xfT_low(p, b):
                if not isinstance(p, int) or p + 4 < NP:
                    norm_pair(p + 4).then_inc(s_xf, 1)
                dve.wait_ge(s_fc, p + 1)
                dve.nop(nofuse=True)
                dve.scalar_tensor_tensor(xfp[:, bass.ds(p * 2, 2), D:2 * D], two(bank[4 + b][:, :]), X_SCALE,
                                         xfp[:, bass.ds(p * 2, 2), 0:D], op0=ALU.mult, op1=ALU.subtract).then_inc(s_fl, 1)
            for p in range(4):
                norm_pair(p).then_inc(s_xf, 1)
            quads(dve, xfT_low)

            dve.wait_ge(s_mean, 1)
            dve.tensor_scalar(mean_row, bank[0][0:1, 0:D], 1.0 / N, None, op0=ALU.mult).then_inc(s_mrow, 1)
            dve.wait_ge(s_mcol, 1)
            for c in range(DC):
                ins = dve.tensor_scalar(mean_s[:, c * P:(c + 1) * P], ones[:, :], bank[1 + 2 * c][:, 0:1], None, op0=ALU.mult)
            ins.then_inc(s_mb, 1)
            w8, e8, c8, o8, p8 = (small[:, 8 * n:8 * n + 8] for n in (0, 1, 2, 3, 4))
            one = small[:, 60:61]

            def softmax(src_ap, dst_ap, n):
                link(dve.tensor_reduce(one, src_ap, axis=AX.X, op=ALU.max))
                dve.tensor_scalar(w8, src_ap, one, None, op0=ALU.subtract).then_inc(s_exin, 1)
                dve.wait_ge(s_ex, n)
                dve.nop(nofuse=True)
                link(dve.tensor_reduce(one, e8, axis=AX.X, op=ALU.add))
                link(dve.reciprocal(one, one))
                link(dve.tensor_scalar(dst_ap, e8, one, None, op0=ALU.mult))
            dve.wait_ge(s_lg, 1)
            softmax(bank[2][:, 0:NE], c8, 1)
            link(dve.tensor_scalar(o8, c8, float(N), 1e-30, op0=ALU.mult, op1=ALU.max))
            link(dve.reciprocal(o8, o8))
            link(dve.tensor_scalar(o8, o8, CAP, 1.0, op0=ALU.mult, op1=ALU.min))
            link(dve.tensor_tensor(c8, c8, o8, op=ALU.mult))
            softmax(c8, c8, 2)
            for k in range(2):
                top = small[:, 62 + k:63 + k]
                link(dve.tensor_reduce(top, c8, axis=AX.X, op=ALU.max))
                link(dve.tensor_scalar(o8, c8, top, -100.0, op0=ALU.is_equal, op1=ALU.mult))
                link(dve.tensor_tensor(o8, o8, iota_b[:, 0:NE], op=ALU.add))
                link(dve.tensor_reduce(small[:, 66 + k:67 + k], o8, axis=AX.X, op=ALU.min))
                link(dve.tensor_scalar(small[:, 66 + k:67 + k], small[:, 66 + k:67 + k], 100.0, None, op0=ALU.add))
                link(dve.tensor_copy(small[:, 64 + k:65 + k].bitcast(I32), small[:, 66 + k:67 + k]))
                if k == 0:
                    link(dve.tensor_scalar(p8, iota_b[:, 0:NE], small[:, 66:67], 4.0, op0=ALU.is_equal, op1=ALU.mult))
                    link(dve.tensor_tensor(c8, c8, p8, op=ALU.subtract))
            dve.sem_inc(s_pick, 1)
            dve.tensor_scalar(w8, ones[:, 0:NE], small[:, 63:64], small[:, 62:63], op0=ALU.mult, op1=ALU.subtract).then_inc(s_exin, 1)
            dve.wait_ge(s_ex, 3)
            tw = [small[:, 70:71], small[:, 71:72]]
            link(dve.tensor_scalar(tw[0], e8[:, 0:1], 1.0, None, op0=ALU.add))
            link(dve.reciprocal(tw[0], tw[0]))
            link(dve.tensor_tensor(tw[1], e8[:, 0:1], tw[0], op=ALU.mult))
            for k in range(2):
                cols = slice(k * 1024, (k + 1) * 1024)
                dve.wait_ge(s_w1h, k + 1)
                dve.scalar_tensor_tensor(w1p[:, 1, cols], fw1_in[:, cols], fsc[:, 0:1], w1p[:, 0, cols],
                                         op0=ALU.mult, op1=ALU.subtract).then_inc(s_w1l, 1)
            dve.wait_ge(s_fw2, 64)
            for k in range(2):
                cols = slice(k * 1024, (k + 1) * 1024)
                dve.tensor_scalar(fw2_in[:, cols], fw2_in[:, cols], tw[k], fsc[:, 1:2], op0=ALU.mult, op1=ALU.mult).then_inc(s_w2t, 1)
            for k in range(2):
                cols = slice(k * 1024, (k + 1) * 1024)
                dve.wait_ge(s_w2h, k + 1)
                dve.tensor_tensor(w2p[:, 1, cols], fw2_in[:, cols], w2p[:, 0, cols], op=ALU.subtract).then_inc(s_w2l, 1)
            link(dve.tensor_scalar(b2two[:, D:2 * D], b2two[:, D:2 * D], tw[1], None, op0=ALU.mult))
            dve.scalar_tensor_tensor(b2row, b2row, tw[0], b2two[:, D:2 * D], op0=ALU.mult, op1=ALU.add).then_inc(s_b2, 1)

            def add_outputs(g, nt):
                dve.wait_ge(s_xfb, g * 2 + min(nt, 2))
                for q in range(nt):
                    t = g * 4 + q
                    dve.wait_ge(s_outp, t + 1)
                    dve.nop(nofuse=True)
                    dve.scalar_tensor_tensor(tile(xn, t), bank[q][:, 0:D], fsc[:, 11:12], tile(xn, t),
                                             op0=ALU.mult, op1=ALU.add).then_inc(s_fo, 1)

            def out_stats(g, nt):
                dve.wait_ge(s_fo, g * 4 + nt)
                dve.nop(nofuse=True)
                for q in range(nt):
                    ins = dve.bn_stats(stats[:, q * 6:q * 6 + 6], tile(xn, g * 4 + q))
                link(ins)
                for q in range(nt):
                    ins = dve.bn_aggr(mv[:, q * 2:q * 2 + 2], stats[:, q * 6:q * 6 + 6])
                link(ins)
                dve.tensor_copy(small[:, 20:20 + nt], mv[:, 0:2 * nt].rearrange("p (q c) -> p q c", c=2)[:, :, 1]).then_inc(s_fvar, 1)

            def out_norm(g, nt):
                dve.wait_ge(s_fstd, g + 1)
                dve.wait_ge(s_resb, g * 2 + min(nt, 2))
                dve.nop(nofuse=True)
                dve.reciprocal(small[:, 28:28 + nt], small[:, 24:24 + nt])
                for q in range(nt):
                    t = g * 4 + q
                    ins = dve.scalar_tensor_tensor(tile(xn, t), tile(xn, t), mv[:, q * 2:q * 2 + 1], gab,
                                                   op0=ALU.subtract, op1=ALU.mult)
                link(ins)
                for q in range(nt):
                    t = g * 4 + q
                    ins = dve.scalar_tensor_tensor(tile(xn, t), tile(xn, t), small[:, 28 + q:29 + q], tile(xs, t),
                                                   op0=ALU.mult, op1=ALU.add)
                ins.then_inc(s_out, 1)

            def lows(g, nt, before):
                w = nt * P
                for j in range(FJ):
                    dve.wait_ge(s_hhi, g * FJ + j + 1)
                    dve.nop(nofuse=True)
                    dve.scalar_tensor_tensor(hp[:, j % 4, 1, 0:w], hid[j % 2][:, 0:w], fsc[:, 2:3], hp[:, j % 4, 0, 0:w],
                                             op0=ALU.mult, op1=ALU.subtract).then_inc(s_hlo, 1)
                    if before and j == 0:
                        add_outputs(g - 1, 4)
                    if before and j == 2:
                        out_stats(g - 1, 4)
                    if before and j == 5:
                        out_norm(g - 1, 4)
            lows(0, 4, False)
            ch.loop(FN_GROUPS - 1, 3, lambda i: lows(i + 1, 4, True))
            lows(FN_GROUPS, 1, True)
            add_outputs(FN_GROUPS, 1)
            out_stats(FN_GROUPS, 1)
            out_norm(FN_GROUPS, 1)


def kernel(**inputs):
    import numpy as np
    import concourse.bacc as bacc
    from concourse.bass_utils import run_bass_kernel_spmd

    a = {k: np.ascontiguousarray(v) for k, v in inputs.items()}
    edges = {}
    for name, fill in (("src", PAD_NODE), ("dst", 0)):
        flat = np.full(P * EC, fill, a[name].dtype)
        flat[:E] = a[name]
        edges[name] = flat.reshape(P, EC)
    rows = np.zeros((NT * P, D), a["x"].dtype)
    rows[:N] = a["x"]
    wqkv = a["L0_mix_w_qkv"]

    def row(name):
        return a[name].reshape(1, -1)
    arrays = {
        "x": rows, "src": edges["src"], "dst": edges["dst"],
        "w0": np.ascontiguousarray(a["L0_gnn_W0"].T), "b0": row("L0_gnn_b0"), "g0": row("L0_gnn_g0"), "be0": row("L0_gnn_beta0"),
        "w1": np.ascontiguousarray(a["L0_gnn_W1"].T), "b1": row("L0_gnn_b1"), "g1": row("L0_gnn_g1"), "be1": row("L0_gnn_beta1"),
        "wq": np.ascontiguousarray(wqkv[:INNER]), "wkv": np.ascontiguousarray(wqkv[INNER:].T),
        "wo": np.ascontiguousarray(a["L0_mix_w_out"].T), "bo": row("L0_mix_b_out"),
        "wr": a["L0_ffn_Wr"], "br": row("L0_ffn_br"), "fw1": a["L0_ffn_W1"],
        "fb1": np.ascontiguousarray(a["L0_ffn_b1"].reshape(NE, F // P, P).transpose(0, 2, 1)),
        "fw2": a["L0_ffn_W2"], "fb2": a["L0_ffn_b2"], "ga": row("L0_ffn_gamma"), "be": row("L0_ffn_beta"),
    }
    nc = bacc.Bacc("TRN2", target_bir_lowering=False, num_devices=1)
    args = {n: nc.dram_tensor(f"in_{n}", v.shape, mybir.dt.from_np(v.dtype), kind="ExternalInput").ap() for n, v in arrays.items()}
    out = nc.dram_tensor("out", (NT * P, D), F32, kind="ExternalOutput").ap()
    gps_layer(nc, **args, out=out)
    r = run_bass_kernel_spmd(nc, [{f"in_{n}": v for n, v in arrays.items()}], core_ids=[0])
    return r.results[0]["out"][:N]
```
